# Optimizing a Trainium2 kernel written in Bass

```python
import numpy as np
import jax
import jax.numpy as jnp

def _softmax(x, axis=-1):
    return jax.nn.softmax(x, axis=axis)

def _gelu(x):
    return jax.nn.gelu(x, approximate=True)

def _silu(x):
    return jax.nn.silu(x)

def _sigmoid(x):
    return jax.nn.sigmoid(x)

def _layernorm(x, axis=-1, eps=1e-05):
    m = jnp.mean(x, axis=axis, keepdims=True)
    v = jnp.var(x, axis=axis, keepdims=True)
    return (x - m) / jnp.sqrt(v + eps)

def _scatter_add(tgt, idx, src, axis=0):
    return tgt.at[idx].add(src)

def _segment_sum(src, seg, n):
    return jax.ops.segment_sum(src, seg, n)
kernel_name = 'mk_adaln_ffn_d2_seqx_r4_058f0b'

def setup_inputs(seed: int=0):
    np.random.seed(seed)
    _w = jnp.asarray

    def _rec_inputs():
        import jax
        import jax.numpy as jnp
        _rk = jax.random.key(seed)
        x = -0.000125 + 0.9999 * jax.random.normal(jax.random.fold_in(_rk, 1), (32, 64, 1024), jnp.float32)
        _lenS = 64 - jax.random.randint(jax.random.fold_in(_rk, 7), (32,), 0, max(1, 64 // 4) + 1, jnp.int32)
        _lenS2 = 64 - jax.random.randint(jax.random.fold_in(_rk, 8), (32,), 0, max(1, 64 // 4) + 1, jnp.int32)
        itok_B_0_7 = jax.random.randint(jax.random.fold_in(_rk, 11), (32,), 0, 8, jnp.int32)
        itok_B_78_3631 = jax.random.randint(jax.random.fold_in(_rk, 12), (32,), 78, 908, jnp.int32)
        return (x, itok_B_0_7, itok_B_78_3631)
    x, itok_B_0_7, itok_B_78_3631 = _rec_inputs()

    def _L0_cond_setup():
        import jax, jax.numpy as jnp
        import numpy as np
        TOP_K = 2
        LANG_BIAS = 5.0
        SCALING = 32.0 / 16.0
        LANGUAGE_PAD_ID = -1
        key = jax.random.key(seed)
        ks = jax.random.split(key, 6)
        B, T, D, O, E, R = (4, 512, 1024, 1024, 8, 16)
        x = jax.random.normal(ks[0], (B, T, D), dtype=jnp.float32)
        language_ids = jax.random.randint(ks[1], (B,), 0, E).astype(jnp.int64)
        W = jax.random.normal(ks[2], (O, D), dtype=jnp.float32) * (1.0 / np.sqrt(D))
        Wr = jax.random.normal(ks[3], (E, D), dtype=jnp.float32) * (1.0 / np.sqrt(D))
        A = jax.random.normal(ks[4], (E, R, D), dtype=jnp.float32) * (1.0 / np.sqrt(D))
        Bm = jax.random.normal(ks[5], (O, R), dtype=jnp.float32) * 0.0
        Bm = jnp.broadcast_to(Bm, (E, O, R)) + jax.random.normal(ks[5], (E, O, R), dtype=jnp.float32) * 0.02
        return {'x': x, 'language_ids': language_ids, 'W': W, 'Wr': Wr, 'A': A, 'B': Bm}
    _L0_cond_all = _L0_cond_setup()
    _L0_cond_in = {k: v for k, v in _L0_cond_all.items() if k in ('W', 'Wr', 'A', 'B')}
    del _L0_cond_all

    def _L0_ffn_setup():
        import jax, jax.numpy as jnp
        import numpy as np
        HID, BOT, RDIM, NSLOT, K, VB = (1024, 64, 48, 256, 8, 64)
        TAU_LOW, TAU_HIGH, EARLY_EXIT = (0.5, 2.0, 0.05)

        def _uncertainty(h, Wu1, bu1, Wu2, bu2):
            var = jnp.var(h, axis=-1)
            log_var = jnp.log1p(var)
            norm_var = log_var / (jnp.mean(log_var) + 1e-06)
            learned = (jax.nn.gelu(h @ Wu1.T + bu1) @ Wu2.T + bu2)[..., 0]
            return jnp.clip(norm_var * 0.5 + jax.nn.sigmoid(learned) * 2.5, 0.0, 5.0)
        key = jax.random.key(seed)
        ks = jax.random.split(key, 12)
        B, S = (2, 512)
        return {'hidden_states': jax.random.normal(ks[0], (B, S, HID), dtype=jnp.float32), 'Wq': jax.random.normal(ks[1], (BOT, HID), dtype=jnp.float32) / np.sqrt(HID), 'Wr': jax.random.normal(ks[2], (RDIM, BOT), dtype=jnp.float32) / np.sqrt(BOT), 'aux_keys': jax.random.normal(ks[3], (NSLOT, BOT), dtype=jnp.float32) * 0.01, 'aux_values': jax.random.normal(ks[4], (NSLOT, HID), dtype=jnp.float32) * 0.02, 'Wvd': jax.random.normal(ks[5], (VB, HID), dtype=jnp.float32) * 0.1 / np.sqrt(HID), 'Wvu': jax.random.normal(ks[6], (HID, VB), dtype=jnp.float32) * 0.1 / np.sqrt(VB), 'Wu1': jax.random.normal(ks[7], (HID // 4, HID), dtype=jnp.float32) / np.sqrt(HID), 'bu1': jnp.zeros((HID // 4,), dtype=jnp.float32), 'Wu2': jax.random.normal(ks[8], (1, HID // 4), dtype=jnp.float32) * 0.01, 'bu2': jnp.zeros((1,), dtype=jnp.float32), 'gate_w1': jnp.float32(0.5), 'gate_bias': jnp.float32(-1.0), 'log_rel': jnp.zeros((NSLOT,), dtype=jnp.float32)}
    _L0_ffn_all = _L0_ffn_setup()
    _L0_ffn_in = {k: v for k, v in _L0_ffn_all.items() if k in ('Wq', 'Wr', 'aux_keys', 'aux_values', 'Wvd', 'Wvu', 'Wu1', 'bu1', 'Wu2', 'bu2', 'gate_w1', 'gate_bias', 'log_rel')}
    del _L0_ffn_all

    def _L1_cond_setup():
        import math
        import jax, jax.numpy as jnp
        import numpy as np
        B, H, N, L = (16, 64, 64, 1024)
        DT_MIN, DT_MAX = (0.001, 0.1)

        def _get_kernel(log_dt, C, log_A_real, A_imag, length):
            dt = jnp.exp(log_dt)
            Cc = C[..., 0] + 1j * C[..., 1]
            A = -jnp.exp(log_A_real) + 1j * A_imag
            dtA = A * dt[:, None]
            Ct = Cc * (jnp.exp(dtA) - 1.0) / A
            P = dtA[:, :, None] * jnp.arange(length, dtype=jnp.float32)
            K = 2.0 * jnp.einsum('hn,hnl->hl', Ct, jnp.exp(P)).real
            return K
        key = jax.random.key(seed)
        ks = jax.random.split(key, 5)
        u = jax.random.normal(ks[0], (B, H, L), dtype=jnp.float32)
        log_dt = jax.random.uniform(ks[1], (H,), dtype=jnp.float32) * (math.log(DT_MAX) - math.log(DT_MIN)) + math.log(DT_MIN)
        C = jax.random.normal(ks[2], (H, N, 2), dtype=jnp.float32)
        log_A_real = jnp.log(0.5 * jnp.ones((H, N), dtype=jnp.float32))
        A_imag = math.pi * jnp.broadcast_to(jnp.arange(N, dtype=jnp.float32), (H, N))
        D = jax.random.normal(ks[3], (H,), dtype=jnp.float32)
        length = jax.random.randint(ks[4], (B,), 1, L + 1, dtype=jnp.int32)
        return {'u': u, 'log_dt': log_dt, 'C': C, 'log_A_real': log_A_real, 'A_imag': A_imag, 'D': D, 'length': length}
    _L1_cond_all = _L1_cond_setup()
    _L1_cond_in = {k: v for k, v in _L1_cond_all.items() if k in ('log_dt', 'C', 'log_A_real', 'A_imag', 'D')}
    del _L1_cond_all

    def _L1_ffn_setup():
        import jax, jax.numpy as jnp
        import numpy as np
        DIM = 1024
        INTER = 3584
        SPARSITY = 64
        RANK = 16
        key = jax.random.key(seed)
        ks = jax.random.split(key, 5)
        B, T = (64, 1)
        x = jax.random.normal(ks[0], (B, T, DIM), dtype=jnp.float32)
        c1_w = jax.random.normal(ks[1], (RANK, DIM), dtype=jnp.float32) * (1.0 / np.sqrt(DIM))
        c2_w = jax.random.normal(ks[2], (INTER, RANK), dtype=jnp.float32) * (1.0 / np.sqrt(RANK))
        w1 = jax.random.normal(ks[3], (INTER, DIM), dtype=jnp.float32) * (1.0 / np.sqrt(DIM))
        w2t = jax.random.normal(ks[4], (INTER, DIM), dtype=jnp.float32) * (1.0 / np.sqrt(INTER))
        return {'x': x, 'c1_w': c1_w, 'c2_w': c2_w, 'w1': w1, 'w2t': w2t}
    _L1_ffn_all = _L1_ffn_setup()
    _L1_ffn_in = {k: v for k, v in _L1_ffn_all.items() if k in ('c1_w', 'c2_w', 'w1', 'w2t')}
    del _L1_ffn_all
    return {'x': x, 'itok_B_0_7': itok_B_0_7, 'itok_B_78_3631': itok_B_78_3631, 'L0_cond_W': _L0_cond_in['W'], 'L0_cond_Wr': _L0_cond_in['Wr'], 'L0_cond_A': _L0_cond_in['A'], 'L0_cond_B': _L0_cond_in['B'], 'L0_ffn_Wq': _L0_ffn_in['Wq'], 'L0_ffn_Wr': _L0_ffn_in['Wr'], 'L0_ffn_aux_keys': _L0_ffn_in['aux_keys'], 'L0_ffn_aux_values': _L0_ffn_in['aux_values'], 'L0_ffn_Wvd': _L0_ffn_in['Wvd'], 'L0_ffn_Wvu': _L0_ffn_in['Wvu'], 'L0_ffn_Wu1': _L0_ffn_in['Wu1'], 'L0_ffn_bu1': _L0_ffn_in['bu1'], 'L0_ffn_Wu2': _L0_ffn_in['Wu2'], 'L0_ffn_bu2': _L0_ffn_in['bu2'], 'L0_ffn_gate_w1': _L0_ffn_in['gate_w1'], 'L0_ffn_gate_bias': _L0_ffn_in['gate_bias'], 'L0_ffn_log_rel': _L0_ffn_in['log_rel'], 'L1_cond_log_dt': _L1_cond_in['log_dt'], 'L1_cond_C': _L1_cond_in['C'], 'L1_cond_log_A_real': _L1_cond_in['log_A_real'], 'L1_cond_A_imag': _L1_cond_in['A_imag'], 'L1_cond_D': _L1_cond_in['D'], 'L1_ffn_c1_w': _L1_ffn_in['c1_w'], 'L1_ffn_c2_w': _L1_ffn_in['c2_w'], 'L1_ffn_w1': _L1_ffn_in['w1'], 'L1_ffn_w2t': _L1_ffn_in['w2t']}

def reference(x, itok_B_0_7, itok_B_78_3631, L0_cond_W, L0_cond_Wr, L0_cond_A, L0_cond_B, L0_ffn_Wq, L0_ffn_Wr, L0_ffn_aux_keys, L0_ffn_aux_values, L0_ffn_Wvd, L0_ffn_Wvu, L0_ffn_Wu1, L0_ffn_bu1, L0_ffn_Wu2, L0_ffn_bu2, L0_ffn_gate_w1, L0_ffn_gate_bias, L0_ffn_log_rel, L1_cond_log_dt, L1_cond_C, L1_cond_log_A_real, L1_cond_A_imag, L1_cond_D, L1_ffn_c1_w, L1_ffn_c2_w, L1_ffn_w1, L1_ffn_w2t):
    import jax
    import jax.numpy as jnp

    def _L0_cond_ref(x, language_ids, W, Wr, A, B):
        import jax, jax.numpy as jnp
        import numpy as np
        TOP_K = 2
        LANG_BIAS = 5.0
        SCALING = 32.0 / 16.0
        LANGUAGE_PAD_ID = -1
        base = jnp.einsum('btd,od->bto', x, W)
        E = Wr.shape[0]
        logits = jnp.einsum('btd,ed->bte', x.astype(jnp.float32), Wr.astype(jnp.float32))
        expert_targets = language_ids
        valid = expert_targets >= 0
        tgt = jnp.where(valid, expert_targets, 0)
        bias = jax.nn.one_hot(tgt, E, dtype=logits.dtype) * LANG_BIAS
        bias = jnp.where(valid[:, None], bias, 0.0)
        logits = logits + bias[:, None, :]
        topw, topi = jax.lax.top_k(logits, TOP_K)
        weights = jax.nn.softmax(topw, axis=-1)
        gates = jnp.sum(jax.nn.one_hot(topi, E, dtype=weights.dtype) * weights[..., None], axis=-2)
        gates = gates.astype(x.dtype)
        h = jnp.einsum('btd,erd->bter', x, A)
        lora_out = jnp.einsum('bter,bte,eor->bto', h, gates, B)
        return base + SCALING * lora_out

    def _L0_ffn_ref(hidden_states, Wq, Wr, aux_keys, aux_values, Wvd, Wvu, Wu1, bu1, Wu2, bu2, gate_w1, gate_bias, log_rel):
        import jax, jax.numpy as jnp
        import numpy as np
        HID, BOT, RDIM, NSLOT, K, VB = (1024, 64, 48, 256, 8, 64)
        TAU_LOW, TAU_HIGH, EARLY_EXIT = (0.5, 2.0, 0.05)

        def _uncertainty(h, Wu1, bu1, Wu2, bu2):
            var = jnp.var(h, axis=-1)
            log_var = jnp.log1p(var)
            norm_var = log_var / (jnp.mean(log_var) + 1e-06)
            learned = (jax.nn.gelu(h @ Wu1.T + bu1) @ Wu2.T + bu2)[..., 0]
            return jnp.clip(norm_var * 0.5 + jax.nn.sigmoid(learned) * 2.5, 0.0, 5.0)
        query = hidden_states @ Wq.T
        rq = query @ Wr.T
        rk = aux_keys @ Wr.T
        router_scores = jnp.einsum('bsr,nr->bsn', rq, rk) / np.sqrt(RDIM) + log_rel
        top_scores, top_idx = jax.lax.top_k(router_scores, K)
        sel_keys = aux_keys[top_idx]
        attn = jnp.einsum('bsd,bskd->bsk', query, sel_keys) / np.sqrt(BOT) + log_rel[top_idx]
        w = jax.nn.softmax(attn, axis=-1)
        sel_vals = aux_values[top_idx]
        aux_out = jnp.einsum('bsk,bskh->bsh', w, sel_vals)
        aux_out = aux_out @ Wvd.T @ Wvu.T
        u = _uncertainty(hidden_states, Wu1, bu1, Wu2, bu2)
        u_norm = jnp.clip((u - TAU_LOW) / (TAU_HIGH - TAU_LOW), 0.0, 1.0)
        gate = jax.nn.sigmoid(gate_w1 * u_norm + gate_bias)
        gate = jnp.where(gate < EARLY_EXIT, 0.0, gate)
        return hidden_states + gate[..., None] * aux_out

    def _L1_cond_ref(u, log_dt, C, log_A_real, A_imag, D, length):
        import math
        import jax, jax.numpy as jnp
        import numpy as np
        B, H, N, L = (16, 64, 64, 1024)
        DT_MIN, DT_MAX = (0.001, 0.1)

        def _get_kernel(log_dt, C, log_A_real, A_imag, length):
            dt = jnp.exp(log_dt)
            Cc = C[..., 0] + 1j * C[..., 1]
            A = -jnp.exp(log_A_real) + 1j * A_imag
            dtA = A * dt[:, None]
            Ct = Cc * (jnp.exp(dtA) - 1.0) / A
            P = dtA[:, :, None] * jnp.arange(length, dtype=jnp.float32)
            K = 2.0 * jnp.einsum('hn,hnl->hl', Ct, jnp.exp(P)).real
            return K
        Bq, Hq, Lq = u.shape
        K = _get_kernel(log_dt, C, log_A_real, A_imag, Lq)
        n = 2 * Lq
        kf = jnp.fft.rfft(K, n=n)
        uf = jnp.fft.rfft(u, n=n)
        y = jnp.fft.irfft(uf * kf[None], n=n)[..., :Lq]
        y = y + u * D[:, None]
        mask = (jnp.arange(Lq)[None, :] < length[:, None]).astype(u.dtype)
        return y * mask[:, None, :]

    def _L1_ffn_ref(x, c1_w, c2_w, w1, w2t):
        import jax, jax.numpy as jnp
        import numpy as np
        DIM = 1024
        INTER = 3584
        SPARSITY = 64
        RANK = 16
        B, T, M = x.shape
        xf = x.reshape(B * T, M)
        inter = xf @ c1_w.T @ c2_w.T
        n_blocks = INTER // SPARSITY
        blk = inter.reshape(B * T, n_blocks, SPARSITY)
        idx = jnp.argmax(blk, axis=-1) + jnp.arange(0, INTER, SPARSITY)
        w1_g = w1[idx]
        w2_g = w2t[idx]
        h = jax.nn.relu(jnp.einsum('bkm,bm->bk', w1_g, xf))
        out = jnp.einsum('bk,bkm->bm', h, w2_g)
        return out.reshape(B, T, M)
    x = x + _L0_ffn_ref(_L0_cond_ref(x, itok_B_0_7, L0_cond_W, L0_cond_Wr, L0_cond_A, L0_cond_B), L0_ffn_Wq, L0_ffn_Wr, L0_ffn_aux_keys, L0_ffn_aux_values, L0_ffn_Wvd, L0_ffn_Wvu, L0_ffn_Wu1, L0_ffn_bu1, L0_ffn_Wu2, L0_ffn_bu2, L0_ffn_gate_w1, L0_ffn_gate_bias, L0_ffn_log_rel)
    x = x + _L1_ffn_ref(_L1_cond_ref(x, L1_cond_log_dt, L1_cond_C, L1_cond_log_A_real, L1_cond_A_imag, L1_cond_D, itok_B_78_3631), L1_ffn_c1_w, L1_ffn_c2_w, L1_ffn_w1, L1_ffn_w2t)
    return x

_drawn_inputs = setup_inputs


def setup_inputs(seed=0):
    import zlib

    import numpy as np

    out = dict(_drawn_inputs(seed))
    spreads = {'L0_ffn_bu1': (0.0, 2.0),
     'L0_ffn_log_rel': (0.0, 2.0),
     'L1_cond_log_A_real': (-0.6931471824645996, 0.2)}
    factors = {'L0_cond_Wr': 3.689,
     'L0_ffn_Wq': 25.155,
     'L0_ffn_Wr': 27.846,
     'L0_ffn_aux_keys': 25.744,
     'L0_ffn_aux_values': 24.628,
     'L0_ffn_Wvd': 24.662,
     'L0_ffn_Wvu': 25.156,
     'L0_ffn_Wu1': 64.0,
     'L0_ffn_Wu2': 64.0}
    for name, (base, spread) in spreads.items():
        noise = np.random.default_rng([zlib.crc32(name.encode()), seed]).standard_normal(out[name].shape)
        drawn = base * np.exp(spread * noise) if base else spread * noise
        out[name] = jnp.asarray(drawn.astype(out[name].dtype))
    for name, factor in factors.items():
        out[name] = (out[name] * factor).astype(out[name].dtype)
    return out
```

```python
from contextlib import ExitStack

import numpy as np

import concourse.bass as bass
from concourse import mybir

F32 = mybir.dt.float32
F16 = mybir.dt.float16
I32 = mybir.dt.int32
ALU = mybir.AluOpType
ACT = mybir.ActivationFunctionType
AX_X = mybir.AxisListType.X

P = 128
B, H, L = 32, 64, 1024
TOK = B * H
KT = L // P
GT = 512
NG = TOK // GT
TPG = GT // P
HPG = GT // B
NE, RK = 8, 16
BOT, RD, NS = 64, 48, 256
UH = 256
SN = 64
TA, TB = 32, 32
RANK, INTER, BLK = 16, 3584, 64
IT = INTER // P
CI = 4
NC = IT // CI
RING = 6
BODY = 3
KROWS = L + P
RB = 32
C1R = 80

S_W = 64.0
S_R = 16.0
TWO_PI = 6.283185
MAGIC = 12582912.0
BIG = 1.0e30

C_TB, C_TA, C_POS, C_EXP, C_PHA, C_PHB, C_SGN, C_ONE, C_E64, C_ID = 0, 32, 64, 72, 80, 81, 82, 83, 84, 85
C_N = C_ID + P


def shape_constants():
    c = np.zeros((P, C_N), np.float32)
    c[:, C_TB:C_TB + TB] = np.arange(TB)[::-1]
    c[:, C_TA:C_TA + TA] = TB * np.arange(TA)[::-1]
    c[:, C_POS:C_POS + KT] = np.arange(KT)[None] * P + np.arange(P)[::-1, None]
    c[:, C_EXP:C_EXP + NE] = np.arange(NE)
    c[:SN, C_PHA] = 0.25
    c[SN:, C_PHB] = 0.25
    c[:SN, C_SGN] = 1.0
    c[SN:, C_SGN] = -1.0
    c[:, C_ONE] = 1.0
    c[64, C_E64] = 1.0
    c[:, C_ID:] = np.eye(P)
    return c


class Arena:

    def __init__(self, region, words):
        self.region, self.words, self.at = region, words, 0

    def take(self, shape, dt=F32, parts=P):
        n = int(np.prod(shape))
        words = n if dt != F16 else (n + 1) // 2
        words = (words + 7) // 8 * 8
        ap = self.region[0:parts, self.at:self.at + words]
        if dt != F32:
            ap = ap.bitcast(dt)
        ap = ap[:, 0:n]
        self.at += words
        assert self.at <= self.words, (self.at, self.words)
        if len(shape) == 2:
            ap = ap.rearrange("p (a b) -> p a b", a=shape[0])
        elif len(shape) == 3:
            ap = ap.rearrange("p (a b c) -> p a b c", a=shape[0], b=shape[1])
        return ap


def build(nc, xT, WT, WrT, AT, BT, WqT, Wr, Wr2T, keysT, valuesT, WvdT, WvuT, Wu1T, bu1, Wu2, bu2, gate_w1,
          gate_bias, log_rel, log_dt, Cri, lar, aim, Dh, c1P, c2T, w1L, w2, ids, lens, consts, out):
    with ExitStack() as ctx:
        def sem(name):
            return ctx.enter_context(nc.semaphore(name))

        OUT = ctx.enter_context(nc.sbuf_tensor("OUT", [P, KT, TOK], F32))
        XF = ctx.enter_context(nc.sbuf_tensor("XF", [P, KT * TOK], F32))
        WORDS = 20440
        AR = ctx.enter_context(nc.sbuf_tensor("AR", [P, WORDS], F32))
        PS = ctx.enter_context(nc.psum_tensor("PS", [P, 8, 512], F32))
        PSH = PS[:, :, :].bitcast(F16)
        kp = [nc.dram_tensor(n, (H, KROWS), F16).ap() for n in ("taps_hi", "taps_lo")]

        xr = Arena(XF, KT * TOK)
        Wsp = [xr.take([KT, L], F16) for _ in range(2)]
        xsp = [xr.take([KT, GT], F16) for _ in range(2)]
        hsp = [xr.take([KT, GT], F16) for _ in range(2)]
        assert xr.at == KT * TOK
        xr = Arena(XF, KT * TOK)
        fsp = [xr.take([KT, TOK], F16) for _ in range(2)]

        a = Arena(AR, WORDS)
        cst = a.take([C_N])
        e_all = a.take([TOK // P, NS])
        stage = [e_all[:, 4 * i:4 * i + 4, :].rearrange("p a b -> p (a b)") for i in range(2)]
        u1_at = a.at
        U1 = [a.take([KT, UH], F16) for _ in range(2)]
        Asp = [a.take([KT, P], F16) for _ in range(2)]
        Bsp = [a.take([L], F16) for _ in range(2)]
        Qsp = [a.take([KT, BOT + 1], F16) for _ in range(2)]
        Rsp = [a.take([KT, NE], F16) for _ in range(2)]
        h32 = a.take([2, GT])
        sq = a.take([GT])
        acc = a.take([GT])
        ones = sq[:, 0:P]
        gl = a.take([2, GT])
        Gx, gTs = gl[:, 0, :], gl[:, 1, :]
        hg32 = a.take([GT])
        kf = hg32[0:TA, :].rearrange("p (h b) -> p h b", h=HPG)
        hgsp = [a.take([GT], F16) for _ in range(2)]
        ksp = [a.take([HPG, TB], F16, TA) for _ in range(2)]
        qT = a.take([GT])
        MK = a.take([2 * NS])
        AV = a.take([2, BOT])
        SA = a.take([2 * NS])
        tm = a.take([NS])
        ph = [a.take([HPG, TB]) for _ in range(3)]
        mg = [a.take([HPG, TB]) for _ in range(2)]
        lrel = a.take([NS])
        small = a.take([20, SN])
        gts = a.take([7, TPG * NE])
        gs = a.take([6, TPG])
        st = a.take([3, TOK // P])
        seall = a.take([TOK // P])
        nm = a.take([2])
        v8 = a.take([8])
        b5 = a.take([NE])
        gate = a.take([12, TOK // P])
        scal = a.take([8])
        bu1s = a.take([2])
        wu2s = a.take([2])
        ids_i = a.take([1], I32)
        ids_f = a.take([1])
        zpad = a.take([P], F16)
        Dall = a.take([H], F32, TA)
        c = Arena(AR, WORDS)
        c.at = u1_at
        wvu = c.take([L])
        zT = c.take([GT])
        c = Arena(AR, WORDS)
        c.at = u1_at + 2048
        eT = c.take([2, GT])
        eg = c.take([2, NS])

        ident = cst[:, C_ID:C_ID + P]
        lar_s, aim_s, cr_s, ci_s, dt_s, R_s, th_s, s1_s, s2_s = (small[:, i, :] for i in range(9))
        t_ = [small[:, 9 + i, :] for i in range(11)]

        f = Arena(AR, WORDS)
        w1r = [f.take([RING, KT, P], F16) for _ in range(2)]
        w2_at = f.at
        w2r = [f.take([RING, L], F16) for _ in range(2)]
        m_at = f.at
        msp = [f.take([CI, GT], F16) for _ in range(2)]
        a1s = f.take([TOK], F16, C1R)
        c2s = f.take([INTER], F16, C1R)
        mT_at = f.at
        mT = f.take([CI, GT], F16)
        mk = f.take([2, GT], F16)
        fst = [f.take([512]) for _ in range(2)]
        m32 = f.take([GT])
        bm = f.take([BLK // 8])
        idF = f.take([P], F16)
        f2 = Arena(AR, WORDS)
        f2.at = w2_at
        toep = [[f2.take([L], F16) for _ in range(2)] for _ in range(4)]
        c1s = [f2.take([KT, C1R], F16) for _ in range(2)]
        id32 = f2.take([P])
        len_i = f2.take([B], I32)
        len_f = f2.take([B])
        posF = f2.take([KT])
        f2.at = m_at
        y32 = f2.take([2, KT * 2 * B])
        f2.at = mT_at
        ymask = f2.take([KT, 2 * B])

        s_x = sem("x_loaded")
        s_stage = [sem("stage0_loaded"), sem("stage1_loaded")]
        s_shi = sem("stage_hi_made")
        s_slo = sem("stage_lo_made")
        s_small = sem("small_loaded")
        s_xh = sem("x_hi_made")
        s_xl = sem("x_lo_made")
        s_pre = sem("prep_product")
        s_prev = sem("prep_evacuated")
        s_lg = sem("logits_ready")
        s_ha = sem("lora_down_ready")
        s_base = sem("h0_ready")
        s_d = sem("expert_gap_ready")
        s_ex = sem("expert_exp_ready")
        s_gx = sem("gates_spread")
        s_gT = sem("gates_turned")
        s_gTs = sem("gates_turned_in_sbuf")
        s_hg = sem("gated_down_ready")
        s_hgh = sem("gated_hi_made")
        s_hgl = sem("gated_lo_made")
        s_hev = sem("h0_in_sbuf")
        s_hh = sem("h0_hi_made")
        s_hl = sem("h0_lo_made")
        s_oadd = sem("h0_added_to_x")
        s_sq = sem("h0_squares_summed")
        s_q = sem("query_ready")
        s_qT = sem("query_in_sbuf")
        s_u = sem("uncertainty_hidden_ready")
        s_gl = sem("gelu_done")
        s_sc = sem("scores_ready")
        s_scr = sem("scores_read")
        s_t = sem("attention_masked")
        s_e = sem("attention_exp_done")
        s_st = sem("token_sums_ready")
        s_str = sem("token_sums_read")
        s_rexp = sem("state_exp_small")
        s_dsm = sem("state_reciprocal")
        s_ph = sem("state_phases_ready")
        s_phd = sem("state_waves_done")
        s_L = sem("state_factors_ready")
        s_k = sem("taps_ready")
        s_kc = sem("taps_split")
        s_kst = sem("taps_stored")
        s_pz = sem("tap_zeros_made")
        s_dve = sem("vector_step")
        s_pool = sem("pool_step")
        s_one = sem("query_ones_set")
        s_wvu = sem("Wvu_loaded")
        s_var = sem("variance_ready")
        s_lv = sem("log_variance_ready")
        s_lvs = sem("log_variance_sums_ready")
        s_un = sem("uncertainty_ready")
        s_sg = sem("gate_sigmoid_ready")
        s_gate = sem("gate_ready")
        s_ulp = sem("x1_lo_made_by_gpsimd")
        s_idf = sem("identity_cast")
        s_lenf = sem("lengths_cast")
        s_bm = sem("block_max_ready")
        s_out = sem("out_stored")
        s_gsum = sem("log_var_summed")
        s_eT = sem("attention_turned")
        s_eTs = sem("attention_turned_in_sbuf")
        s_eg = sem("attention_gated")
        s_z = sem("memory_read")
        s_zTs = sem("memory_in_sbuf")
        s_aux = sem("memory_out_ready")
        s_x1 = sem("x1_ready")
        s_uh = sem("x1_hi_made")
        s_ul = sem("x1_lo_made")
        s_lenl = sem("lengths_loaded")
        s_ym = sem("length_mask_made")
        s_tp = [sem(f"toeplitz{i}_loaded") for i in range(4)]
        s_cv = sem("head_convolved")
        s_y = sem("y_masked")
        s_yh = sem("y_hi_made")
        s_yl = sem("y_lo_made")
        s_fst = [sem("ffn_stage0_loaded"), sem("ffn_stage1_loaded")]
        s_fhi = sem("ffn_weight_hi_made")
        s_flo = sem("ffn_weight_lo_made")
        s_a1 = sem("rank_product_ready")
        s_a1h = sem("rank_hi_made")
        s_a1l = sem("rank_lo_made")
        s_in = sem("inter_ready")
        s_mk = sem("argmax_mask_made")
        s_mkT = sem("mask_turned")
        s_mT = sem("mask_in_sbuf")
        s_g1 = sem("ffn_hidden_ready")
        s_m = sem("hidden_masked")
        s_mh = sem("hidden_hi_made")
        s_ml = sem("hidden_lo_made")
        s_o = sem("ffn_out_ready")
        s_oa = sem("ffn_out_added")

        pieces = [
            (Rsp[0], Rsp[1], WrT.rearrange("(k p) e -> p k e", p=P), [KT, NE], S_R),
            (Asp[0], Asp[1], AT.rearrange("(k p) e -> p k e", p=P), [KT, P], S_W),
        ]
        wt = WT.rearrange("(k p) o -> k p o", p=P)
        pieces += [(Wsp[0][:, k, :], Wsp[1][:, k, :], wt[k], [L], S_W) for k in range(KT)]
        pieces += [
            (Bsp[0], Bsp[1], BT, [L], S_W),
            (Qsp[0][:, :, 0:BOT], Qsp[1][:, :, 0:BOT], WqT.rearrange("(k p) e -> p k e", p=P), [KT, BOT], 1.0),
        ]
        u1v = Wu1T.rearrange("(k p) e -> p k e", p=P)
        pieces += [(U1[0][:, 4 * i:4 * i + 4, :], U1[1][:, 4 * i:4 * i + 4, :], u1v[:, 4 * i:4 * i + 4, :], [4, UH], 1.0)
                   for i in range(2)]
        NPC = len(pieces)
        N_A, N_W, N_ALL = 2, 2 + KT, NPC

        def staged(n, shape):
            s = stage[n % 2][:, 0:int(np.prod(shape))]
            return s.rearrange("p (a b) -> p a b", a=shape[0]) if len(shape) == 2 else s

        def tok(g):
            return bass.ds(g * GT, GT)

        small_loads = [
            (cst, consts), (bu1s, bu1), (wu2s, Wu2),
            (scal[:, 0:1], bu2.partition_broadcast(P)), (scal[:, 1:2], gate_w1.partition_broadcast(P)),
            (scal[:, 2:3], gate_bias.partition_broadcast(P)),
            (lrel, log_rel.partition_broadcast(P)),
        ]
        small_loads += [(ids_i[B * i:B * i + B, :], ids) for i in range(P // B)]
        for half in range(2):
            r = slice(SN * half, SN * half + SN)
            small_loads += [(lar_s[r, :], lar), (aim_s[r, :], aim), (cr_s[r, :], Cri[0]), (ci_s[r, :], Cri[1])]
        small_loads += [(t_[0], log_dt.partition_broadcast(P)), (Dall[TA - 1:TA, :], Dh)]
        fold_wr = ph[0][0:RD, 0:2, :].rearrange("p a b -> p (a b)")
        fold_wr2 = ph[0][0:BOT, 2:4, :].rearrange("p a b -> p (a b)")[:, 0:RD]
        fold_keys = ph[0][0:BOT, 4:12, :].rearrange("p a b -> p (a b)")
        fold_rk = ph[1][0:RD, 0:8, :].rearrange("p a b -> p (a b)")
        vT = e_all[:, 8:16, :]
        vdT = gl.rearrange("p a b -> p (a b)")[:, 0:KT * BOT].rearrange("p (k e) -> p k e", k=KT)
        small_loads += [
            (fold_wr, Wr), (fold_wr2, Wr2T), (fold_keys, keysT),
            (vT, valuesT.rearrange("(k p) n -> p k n", p=P)), (vdT, WvdT.rearrange("(k p) e -> p k e", p=P)),
        ]
        NSM = len(small_loads)
        w1v = w1L.rearrange("i p c -> (i p) c")

        def ffn_source(ring, it, half):
            return (w1v if ring == 1 else w2)[bass.ds(it * P, P), half * 512:half * 512 + 512]

        def ffn_slot(part, ring, tile, half):
            r = tile % RING
            if ring == 1:
                return w1r[part][:, r, 4 * half:4 * half + 4, :]
            return w2r[part][:, r, 512 * half:512 * half + 512]

        def as4(x):
            return x.rearrange("p (k i) -> p k i", k=4)

        N_C1, N_W1, N_C2, N_W2 = 2, 2 + 2 * CI, 2 + 2 * CI + 8, 2 + 2 * CI + 8 + 4
        CPC = INTER // 8
        CHUNK = [(2, 0, 2), (2, 0, 3), (1, 1, 0), (1, 1, 1), (2, 1, 0), (2, 1, 1), (1, 1, 2), (1, 1, 3)]
        PPC = 2 * len(CHUNK)
        AT_STEP = [(4, 5), (6, 7), (8, 9, 10, 11), (12, 13, 14, 15)]
        POOL_DEN, POOL_HALF = 7, 10
        KST_FIRST, KST_GROUP = 32, 32 * HPG

        def tap_rows(i, g, hh):
            src = kp[i][bass.ds(g * HPG + hh, 1), 0:L]
            return bass.AP(tensor=src.tensor, offset=src.offset, ap=[[TB, TA], [1, TB]])

        block = ctx.enter_context(nc.Block())

        @block.sync
        def _(sp):
            xv = xT.rearrange("(k p) t -> p k t", p=P)
            ov = out.rearrange("(k p) t -> p k t", p=P)
            sp.dma_start(OUT[:, :, 0:GT], xv[:, :, 0:GT]).then_inc(s_x, 16)
            for n, (hi, lo, src, shape, _) in enumerate(pieces):
                if n >= 2:
                    sp.wait_ge(s_shi, n - 1)
                    sp.wait_ge(s_slo, n - 1)
                sp.dma_start(staged(n, shape), src).then_inc(s_stage[n % 2], 16)
            sp.wait_ge(s_pz, 2)
            for i in range(2):
                sp.dma_start(kp[i][:, L:KROWS], zpad[0:H, :]).then_inc(s_kst, 16)
            with sp.Fori(0, NG - 1) as g:
                sp.wait_ge(s_x, g * 16 + 16)
                sp.dma_start(OUT[:, :, tok(g + 1)], xv[:, :, tok(g + 1)]).then_inc(s_x, 16)
                sp.wait_ge(s_kc, 2 * g + 2)
                for i in range(2):
                    for hh in range(HPG):
                        sp.dma_start(tap_rows(i, g, hh), ksp[i][:, hh, :]).then_inc(s_kst, 16)
            sp.wait_ge(s_kc, 2 * NG)
            for i in range(2):
                for hh in range(HPG):
                    sp.dma_start(tap_rows(i, NG - 1, hh), ksp[i][:, hh, :]).then_inc(s_kst, 16)
            sp.wait_ge(s_u, 2 * NG)
            sp.dma_start(wvu[0:BOT, :], WvuT).then_inc(s_wvu, 16)
            sp.wait_ge(s_aux, KT * NG)
            sp.dma_start(len_i, lens.partition_broadcast(P)).then_inc(s_lenl, 16)
            sp.dma_start(posF, consts[:, C_POS:C_POS + KT], allow_slow_non_contiguous=True).then_inc(s_lenl, 16)
            sp.dma_start(id32, consts[:, C_ID:C_ID + P]).then_inc(s_lenl, 16)
            sp.wait_ge(s_kst, 32 + 32 * HPG * NG)

            def toeplitz(h, i):
                for j in range(2):
                    src = kp[j][bass.ds(h, 1), 0:L]
                    src = bass.AP(tensor=src.tensor, offset=src.offset, ap=[[1, P], [1, L]])
                    sp.dma_start(toep[i][j], src).then_inc(s_tp[i], 16)

            def piece(n, par, dst, src, first=False):
                if not first:
                    sp.wait_ge(s_fhi, n - 1)
                    sp.wait_ge(s_flo, n - 1)
                sp.dma_start(dst, src).then_inc(s_fst[par], 16)

            for i in range(4):
                toeplitz(i, i)
            c1v = c1P.rearrange("(k p) c -> p k c", p=P)
            for n in range(N_C1):
                piece(n, n, fst[n][:, 0:4 * C1R].rearrange("p (k c) -> p k c", k=4), c1v[:, 4 * n:4 * n + 4, :], first=True)

            def heads(q, pieces_of):
                for i in range(8):
                    if i in (0, 4):
                        pieces_of(q, i // 4)
                    sp.wait_ge(s_cv, 8 * q + i + 1)
                    toeplitz(8 * q + 4 + i, i % 4)

            def w1_piece(q, par):
                piece(N_C1 + 2 * q + par, par, fst[par], ffn_source(1, q, par))

            def c2_piece(q, par):
                piece(N_W1 + 2 * (q - 4) + par, par, fst[par][0:C1R, 0:CPC],
                      c2T[:, bass.ds((2 * (q - 4) + par) * CPC, CPC)])

            with sp.Fori(0, 4) as q:
                heads(q, w1_piece)
            with sp.Fori(4, 7) as q:
                heads(q, c2_piece)
            c2_piece(7, 0)
            for i in range(4):
                sp.wait_ge(s_cv, 56 + i + 1)
                toeplitz(60 + i, i)
            c2_piece(7, 1)
            for j in range(4):
                piece(N_C2 + j, j % 2, fst[j % 2], ffn_source(2, j // 2, j % 2))
            with sp.Fori(0, NC - 1) as s:
                for j in range(PPC):
                    ring, ahead, tile = CHUNK[j // 2]
                    piece(N_W2 + PPC * s + j, j % 2, fst[j % 2], ffn_source(ring, CI * (s + ahead) + tile, j % 2))
            for j in range(4):
                ring, _, tile = CHUNK[j // 2]
                piece(N_W2 + PPC * (NC - 1) + j, j % 2, fst[j % 2], ffn_source(ring, CI * (NC - 1) + tile, j % 2))
            for g in range(NG):
                for o in range(KT):
                    sp.wait_ge(s_oa, KT * (NG * (NC - 1) + g) + o + 1)
                    sp.dma_start(ov[:, o, g * GT:(g + 1) * GT], OUT[:, o, g * GT:(g + 1) * GT]).then_inc(s_out, 16)
            sp.wait_ge(s_out, 16 * NG * KT)

        @block.tensor
        def _(pe):
            def mm3(dst, lhs, rhs, k, n, more=False):
                (lh, ll), (rh, rl) = lhs, rhs
                pe.matmul(dst, lh, rh, start=(k == 0), stop=False)
                pe.matmul(dst, lh, rl, start=False, stop=False)
                return pe.matmul(dst, ll, rh, start=False, stop=(k == n - 1 and not more))

            pe.wait_ge(s_small, 16 * NSM)
            pe.matmul(PS[0:RD, 0, 0:NS], fold_wr2, fold_keys, start=True, stop=True).then_inc(s_pre, 1)
            for n in range(2):
                for k in range(KT):
                    mm = pe.matmul(PS[:, 1, BOT * n:BOT * n + BOT], vT[:, k, n * P:n * P + P], vdT[:, k, :],
                                   start=(k == 0), stop=(k == KT - 1))
            mm.then_inc(s_pre, 1)
            pe.wait_ge(s_prev, 1)
            pe.matmul(PS[0:BOT, 2, 0:NS], fold_wr, fold_rk, start=True, stop=True).then_inc(s_pre, 1)
            pe.wait_ge(s_prev, 4)

            def group(g):
                pe.wait_ge(s_xh, g + 1)
                pe.wait_ge(s_xl, g + 1)
                pe.wait_ge(s_shi, N_A)
                pe.wait_ge(s_slo, N_A)
                pe.wait_ge(s_str, g)
                for t in range(TPG):
                    for k in range(KT):
                        mm = mm3(PS[:, 0, NE * t:NE * t + NE], [x[:, k, t * P:t * P + P] for x in xsp],
                                 [w[:, k, :] for w in Rsp], k, KT)
                mm.then_inc(s_lg, 1)
                pe.wait_ge(s_scr, TPG * g)
                for k in range(KT):
                    mm = mm3(PS[:, 1, :], [w[:, k, :] for w in Asp], [x[:, k, :] for x in xsp], k, KT)
                mm.then_inc(s_ha, 1)

                def base(o):
                    for k in range(KT):
                        mm3(PS[:, 2 + o % 2, :], [w[:, k, o * P:o * P + P] for w in Wsp],
                            [x[:, k, :] for x in xsp], k, KT, more=True)

                def lora(o):
                    (bh, bl), (gh, gl_) = [w[:, o * P:o * P + P] for w in Bsp], hgsp
                    pe.matmul(PS[:, 2 + o % 2, :], bh, gh, start=False, stop=False)
                    pe.matmul(PS[:, 2 + o % 2, :], bh, gl_, start=False, stop=False)
                    pe.matmul(PS[:, 2 + o % 2, :], bl, gh, start=False, stop=True).then_inc(s_base, 1)

                pe.wait_ge(s_shi, N_W)
                pe.wait_ge(s_slo, N_W)
                pe.wait_ge(s_hev, KT * g)
                base(0)
                pe.wait_ge(s_gx, g + 1)
                for t in range(TPG):
                    mm = pe.transpose(PS[:, 4, t * P:t * P + P], Gx[:, t * P:t * P + P], ident)
                mm.then_inc(s_gT, 1)
                base(1)
                pe.wait_ge(s_hgh, g + 1)
                pe.wait_ge(s_hgl, g + 1)
                pe.wait_ge(s_shi, NPC)
                pe.wait_ge(s_slo, NPC)
                lora(0)
                lora(1)
                for o in range(2, KT):
                    pe.wait_ge(s_hev, KT * g + o - 1)
                    base(o)
                    lora(o)
                pe.wait_ge(s_one, 1)
                pe.wait_ge(s_hh, KT * g + KT)
                pe.wait_ge(s_hl, KT * g + KT)
                pe.wait_ge(s_kc, 2 * g)
                for k in range(KT):
                    mm = mm3(PS[0:BOT + 1, 5, :], [w[:, k, :] for w in Qsp], [x[:, k, :] for x in hsp], k, KT)
                mm.then_inc(s_q, 1)
                pe.wait_ge(s_gl, 2 * g)
                for n in range(2):
                    for k in range(KT):
                        mm = mm3(PS[:, 6 + n, :], [w[:, k, n * P:n * P + P] for w in U1], [x[:, k, :] for x in hsp], k, KT)
                    mm.then_inc(s_u, 1)
                pe.wait_ge(s_qT, g + 1)
                for t in range(TPG):
                    if t >= 2:
                        pe.wait_ge(s_scr, TPG * g + t - 1)
                    pe.matmul(PS[:, 1 + 3 * (t % 2), :], qT[0:BOT, t * P:t * P + P], MK[0:BOT, :],
                              start=True, stop=True).then_inc(s_sc, 1)
                pe.wait_ge(s_L, g + 1)
                for h in range(HPG):
                    mm = pe.matmul(PS[0:TA, 5, h * TB:h * TB + TB], ph[1][:, h, :], ph[0][:, h, :], start=True, stop=True)
                mm.then_inc(s_k, 1)
                pe.wait_ge(s_sq, 2 * KT * g + 2 * KT)
                pe.wait_ge(s_gl, 2 * g + 2)
                for t in range(TPG):
                    c = slice(t * P, t * P + P)
                    pe.matmul(PS[:, 0, 64 + t:65 + t], qT[0:BOT + 1, c], cst[0:BOT + 1, C_E64:C_E64 + 1], start=True, stop=True)
                    pe.matmul(PS[:, 0, 68 + t:69 + t], acc[:, c], cst[:, C_ONE:C_ONE + 1], start=True, stop=True)
                    pe.matmul(PS[:, 0, 72 + t:73 + t], gl[:, 0, c], wu2s[:, 0:1], start=True, stop=False)
                    mm = pe.matmul(PS[:, 0, 72 + t:73 + t], gl[:, 1, c], wu2s[:, 1:2], start=False, stop=True)
                mm.then_inc(s_st, 1)

            with pe.Fori(0, NG - 1) as g:
                group(g)
            group(NG - 1)

            pe.wait_ge(s_lvs, 1)
            pe.matmul(PS[:, 0, 0:1], ones, gate[:, 3, 0:1], start=True, stop=True).then_inc(s_gsum, 1)
            pe.wait_ge(s_wvu, 16)
            pe.wait_ge(s_e, NG * TPG)
            pe.wait_ge(s_gate, 1)

            def mix(g):
                for t in range(TPG):
                    pe.wait_ge(s_eg, TPG * g + t + 1)
                    pe.wait_ge(s_eTs, TPG * g + (t - 1 if t >= 2 else 0))
                    for n in range(2):
                        mm = pe.transpose(PS[:, t % 2, n * P:n * P + P], eg[:, t % 2, n * P:n * P + P], ident)
                    mm.then_inc(s_eT, 1)
                pe.wait_ge(s_eTs, TPG * g + TPG)
                pe.wait_ge(s_zTs, g)
                for n in range(2):
                    mm = pe.matmul(PS[0:BOT, 4, :], AV[:, n, :], eT[:, n, :], start=(n == 0), stop=(n == 1))
                mm.then_inc(s_z, 1)
                pe.wait_ge(s_zTs, g + 1)
                for o in range(KT):
                    pe.wait_ge(s_x1, KT * g + (o - 1 if o >= 2 else 0))
                    pe.matmul(PS[:, 6 + o % 2, :], wvu[0:BOT, o * P:o * P + P], zT[0:BOT, :],
                              start=True, stop=True).then_inc(s_aux, 1)

            with pe.Fori(0, NG) as g:
                mix(g)

            pe.wait_ge(s_uh, KT * NG)
            pe.wait_ge(s_ul, KT * NG // 2)
            pe.wait_ge(s_ulp, KT * NG // 2)

            with pe.Fori(0, H // 8) as q:
                for i in range(8):
                    pair = i // 2
                    if i % 2 == 0:
                        pe.wait_ge(s_y, 4 * q)
                    pe.wait_ge(s_tp[i % 4], 32 * (2 * q + i // 4 + 1))
                    bank = PS[:, pair, :].rearrange("p (i c b) -> p i c b", i=KT, c=2)
                    for d in range(KT):
                        dst = bank[:, d:KT, i % 2, :]
                        th, tl = [t[:, (KT - 1 - d) * P:(KT - d) * P] for t in toep[i % 4]]
                        uh, ul = [u[:, 0:KT - d, bass.ds(q * 8 * B + i * B, B)] for u in fsp]
                        pe.matmul(dst, th, uh, start=(d == 0), stop=False)
                        pe.matmul(dst, th, ul, start=False, stop=False)
                        mm = pe.matmul(dst, tl, uh, start=False, stop=(d == KT - 1))
                    mm.then_inc(s_cv, 1)

            pe.wait_ge(s_fhi, N_C1)
            pe.wait_ge(s_flo, N_C1)
            pe.wait_ge(s_yh, H // 2)
            pe.wait_ge(s_yl, H // 2)
            with pe.Fori(0, NG // 2) as g2:
                for j in range(2):
                    pe.wait_ge(s_a1l, 2 * g2)
                    for k in range(KT):
                        mm = mm3(PS[0:C1R, 4 + j, :], [w[:, k, :] for w in c1s],
                                 [y[:, k, bass.ds(g2 * 2 * GT + j * GT, GT)] for y in fsp], k, KT)
                    mm.then_inc(s_a1, 1)

            def inter(n, s, g, t):
                pe.wait_ge(s_mk, 4 * n + (t - 1 if t >= 2 else 0))
                pe.matmul(PS[:, t % 2, :], a1s[:, g * GT + t * P:g * GT + t * P + P], c2s[:, bass.ds(s * CI * P, CI * P)],
                          start=True, stop=True).then_inc(s_in, 1)

            def turn_mask(n, t):
                if t == 0:
                    pe.wait_ge(s_mT, 2 * n)
                pe.wait_ge(s_mk, 4 * n + t + 1)
                for i in range(CI):
                    mm = pe.transpose(PSH[:, 2 + i // 2, (i % 2) * GT + t * P:(i % 2) * GT + t * P + P],
                                      mk[:, t % 2, i * P:i * P + P], idF)
                mm.then_inc(s_mkT, 1)

            pe.wait_ge(s_a1h, NG)
            pe.wait_ge(s_a1l, NG)
            pe.wait_ge(s_fhi, N_C2)
            pe.wait_ge(s_flo, N_C2)
            for t in range(TPG):
                inter(0, 0, 0, t)
                if t >= 1:
                    turn_mask(0, t - 1)
            turn_mask(0, TPG - 1)

            def chunk(s, phase, last=False):
                for g in range(NG):
                    n = NG * s + g
                    nxt = None if (last and g == NG - 1) else (n + 1, s + (g + 1) // NG, (g + 1) % NG)
                    for i in range(CI):
                        pe.wait_ge(s_fhi, 16 * s + (14 if i < 2 else 22))
                        pe.wait_ge(s_flo, 16 * s + (14 if i < 2 else 22))
                        pe.wait_ge(s_m, CI * n + (i - 1 if i >= 2 else 0))
                        r = (CI * phase + i) % RING
                        for k in range(KT):
                            mm = mm3(PS[:, 4 + i % 2, :], [w[:, r, k, :] for w in w1r],
                                     [y[:, k, g * GT:g * GT + GT] for y in fsp], k, KT)
                        mm.then_inc(s_g1, 1)
                    if nxt:
                        inter(*nxt, 0)
                        inter(*nxt, 1)
                    for o in range(KT):
                        pe.wait_ge(s_oa, KT * n + (o - 1 if o >= 2 else 0))
                        for k in range(CI):
                            if o == 0:
                                pe.wait_ge(s_fhi, 16 * s + (22 if k < 2 else 26))
                                pe.wait_ge(s_flo, 16 * s + (22 if k < 2 else 26))
                                pe.wait_ge(s_mh, CI * n + k + 1)
                                pe.wait_ge(s_ml, CI * n + k + 1)
                            r = (CI * phase + k) % RING
                            mm = mm3(PS[:, 6 + o % 2, :], [w[:, r, o * P:o * P + P] for w in w2r],
                                     [m[:, k, :] for m in msp], k, CI)
                        mm.then_inc(s_o, 1)
                        if nxt and o < TPG:
                            turn_mask(nxt[0], o)
                            if o + 2 < TPG:
                                inter(*nxt, o + 2)

            with pe.Fori(0, NC - BODY, BODY) as s:
                for j in range(BODY):
                    chunk(s + j, j)
            chunk(NC - 1, (NC - 1) % BODY, last=True)

        @block.scalar
        def _(act):
            act.wait_ge(s_pz, 2)
            for dst, src in small_loads:
                act.dma_start(dst, src, allow_slow_non_contiguous=True).then_inc(s_small, 16)

            def hi_piece(n):
                hi, _, _, shape, scale = pieces[n]
                act.wait_ge(s_stage[n % 2], 16 * (n // 2 + 1))
                act.activation(hi, staged(n, shape), ACT.Copy, scale=scale).then_inc(s_shi, 1)

            act.wait_ge(s_x, 16)
            act.activation(xsp[0], OUT[:, :, 0:GT], ACT.Copy).then_inc(s_xh, 1)
            hi_piece(0)
            hi_piece(1)
            act.wait_ge(s_small, 16 * NSM)
            act.activation(dt_s, t_[0], ACT.Exp).then_inc(s_rexp, 1)
            act.activation(t_[1], lar_s, ACT.Exp).then_inc(s_rexp, 1)
            act.wait_ge(s_pre, 1)
            act.activation(fold_rk, PS[0:RD, 0, 0:NS], ACT.Copy).then_inc(s_prev, 1)
            act.activation(MK[0:BOT, NS:2 * NS], fold_keys, ACT.Copy, scale=BOT ** -0.5).then_inc(s_prev, 1)
            act.wait_ge(s_pre, 2)
            act.activation(AV.rearrange("p a b -> p (a b)"), PS[:, 1, 0:2 * BOT], ACT.Copy).then_inc(s_prev, 1)
            act.wait_ge(s_pre, 3)
            act.activation(MK[0:BOT, 0:NS], PS[0:BOT, 2, 0:NS], ACT.Copy, scale=RD ** -0.5).then_inc(s_prev, 1)
            act.wait_ge(s_pool, POOL_HALF)
            act.activation(t_[3], t_[3], ACT.Sin, scale=TWO_PI).then_inc(s_rexp, 1)
            act.activation(t_[4], t_[4], ACT.Sin, scale=TWO_PI / 2).then_inc(s_rexp, 1)
            for n in range(2, NPC):
                hi_piece(n)

            def group(g, last=False):
                act.wait_ge(s_d, g + 1)
                act.activation(gs[:, 3, :], gs[:, 2, :], ACT.Exp).then_inc(s_ex, 1)
                act.wait_ge(s_gT, g + 1)
                act.activation(gTs, PS[:, 4, :], ACT.Copy).then_inc(s_gTs, 1)
                act.wait_ge(s_hg, g + 1)
                act.activation(hgsp[0], hg32, ACT.Copy).then_inc(s_hgh, 1)
                for o in range(KT):
                    act.wait_ge(s_base, KT * g + o + 1)
                    act.wait_ge(s_oadd, KT * g + (o - 1 if o >= 2 else 0))
                    act.wait_ge(s_sq, 2 * (KT * g + (o - 1 if o >= 2 else 0)))
                    act.activation(h32[:, o % 2, :], PS[:, 2 + o % 2, :], ACT.Copy, scale=1.0 / S_W).then_inc(s_hev, 1)
                    act.wait_ge(s_hev, KT * g + o + 1)
                    act.activation(hsp[0][:, o, :], h32[:, o % 2, :], ACT.Copy).then_inc(s_hh, 1)
                    if o == 4:
                        act.wait_ge(s_ph, g + 1)
                        for i in range(3):
                            act.activation(ph[i], ph[i], ACT.Sin, scale=TWO_PI).then_inc(s_phd, 1)
                        for i in range(2):
                            act.activation(mg[i], mg[i], ACT.Exp).then_inc(s_phd, 1)
                if not last:
                    act.wait_ge(s_x, 16 * g + 32)
                    act.activation(xsp[0], OUT[:, :, tok(g + 1)], ACT.Copy).then_inc(s_xh, 1)
                act.wait_ge(s_q, g + 1)
                act.activation(qT[0:BOT + 1, :], PS[0:BOT + 1, 5, :], ACT.Copy).then_inc(s_qT, 1)
                for n in range(2):
                    act.wait_ge(s_u, 2 * g + n + 1)
                    act.activation(gl[:, n, :], PS[:, 6 + n, :], ACT.Gelu_apprx_tanh, bias=bu1s[:, n:n + 1]).then_inc(s_gl, 1)
                for t in range(TPG):
                    act.wait_ge(s_t, TPG * g + t + 1)
                    at = bass.ds(TPG * g + t, 1)
                    act.activation(e_all[:, at, :].rearrange("p a b -> p (a b)"), tm, ACT.Exp, bias=nm[:, t % 2:t % 2 + 1],
                                   accum_out=seall[:, at]).then_inc(s_e, 1)

            with act.Fori(0, NG - 1) as g:
                group(g)
            group(NG - 1, last=True)

            act.wait_ge(s_var, 1)
            act.activation(gate[:, 2, :], gate[:, 1, :], ACT.Ln, bias=1.0).then_inc(s_lv, 1)
            act.activation(gate[:, 4, :], st[:, 2, :], ACT.Sigmoid, bias=scal[:, 0:1]).then_inc(s_lv, 1)
            act.wait_ge(s_un, 1)
            act.activation(gate[:, 7, :], gate[:, 6, :], ACT.Sigmoid, bias=scal[:, 2:3], scale=scal[:, 1:2]).then_inc(s_sg, 1)

            with act.Fori(0, NG) as g:
                for t in range(TPG):
                    act.wait_ge(s_eT, TPG * g + t + 1)
                    act.wait_ge(s_z, g)
                    act.activation(eT[:, :, t * P:t * P + P], PS[:, t % 2, 0:2 * P].rearrange("p (n c) -> p n c", n=2),
                                   ACT.Copy).then_inc(s_eTs, 1)
                act.wait_ge(s_z, g + 1)
                act.activation(zT[0:BOT, :], PS[0:BOT, 4, :], ACT.Copy).then_inc(s_zTs, 1)
                for o in range(KT):
                    act.wait_ge(s_x1, KT * g + o + 1)
                    act.activation(fsp[0][:, o, tok(g)], OUT[:, o, tok(g)], ACT.Copy).then_inc(s_uh, 1)

            act.wait_ge(s_lenl, 48)
            act.activation(idF, id32, ACT.Copy).then_inc(s_idf, 1)
            act.activation(len_f, len_i, ACT.Copy).then_inc(s_lenf, 1)

            def piece(n, par, dst, src, scale):
                act.wait_ge(s_fst[par], 8 * (n - par) + 16)
                act.activation(dst, src, ACT.Copy, scale=scale).then_inc(s_fhi, 1)

            for n in range(N_C1):
                piece(n, n, c1s[0][:, 4 * n:4 * n + 4, :], fst[n][:, 0:4 * C1R].rearrange("p (k c) -> p k c", k=4), S_W)

            def w1_piece(q, par):
                piece(N_C1 + 2 * q + par, par, w1r[0][:, bass.ds(q, 1), 4 * par:4 * par + 4, :].rearrange("p a k i -> p (a k) i"),
                      as4(fst[par]), S_W)

            def c2_piece(q, par):
                piece(N_W1 + 2 * (q - 4) + par, par, c2s[:, bass.ds((2 * (q - 4) + par) * CPC, CPC)],
                      fst[par][0:C1R, 0:CPC], S_R)

            def convolved(q, pieces_of):
                for pair in range(4):
                    act.wait_ge(s_y, 4 * q + pair + 1)
                    act.activation(fsp[0][:, :, bass.ds(q * 8 * B + pair * 2 * B, 2 * B)],
                                   y32[:, pair % 2, :].rearrange("p (k c) -> p k c", k=KT), ACT.Copy).then_inc(s_yh, 1)
                    if pair % 2:
                        pieces_of(q, pair // 2)

            with act.Fori(0, 4) as q:
                convolved(q, w1_piece)
            with act.Fori(4, 8) as q:
                convolved(q, c2_piece)

            def ffn_piece(n, par, phase, ring, tile):
                dst = ffn_slot(0, ring, CI * phase + tile, par)
                piece(n, par, dst, as4(fst[par]) if ring == 1 else fst[par], S_W)

            for g in range(NG):
                act.wait_ge(s_a1, g + 1)
                act.activation(a1s[:, g * GT:g * GT + GT], PS[0:C1R, 4 + g % 2, :], ACT.Copy, scale=1.0 / S_W).then_inc(s_a1h, 1)
            for j in range(4):
                ffn_piece(N_C2 + j, j % 2, 0, 2, j // 2)

            def mask_out(n):
                act.wait_ge(s_mkT, TPG * n + TPG)
                act.wait_ge(s_m, CI * n)
                for i in range(2):
                    act.activation(mT[:, 2 * i:2 * i + 2, :].rearrange("p a b -> p (a b)"), PSH[:, 2 + i, :],
                                   ACT.Copy, scale=1.0 / S_W).then_inc(s_mT, 1)

            mask_out(0)

            def chunk(s, phase, last=False):
                base = N_W2 + PPC * s
                for g in range(NG):
                    n = NG * s + g
                    act.wait_ge(s_o, KT * n)
                    for i in range(CI):
                        act.wait_ge(s_m, CI * n + i + 1)
                        act.activation(msp[0][:, i, :], m32, ACT.Copy).then_inc(s_mh, 1)
                        if g == 0:
                            ring, ahead, tile = CHUNK[i // 2]
                            ffn_piece(base + i, i % 2, phase + ahead, ring, tile)
                    if not (last and g == NG - 1):
                        mask_out(n + 1)
                    if not last:
                        for j in AT_STEP[g]:
                            ring, ahead, tile = CHUNK[j // 2]
                            if j == 12:
                                act.wait_ge(s_g1, CI * (n + 1))
                            ffn_piece(base + j, j % 2, phase + ahead, ring, tile)

            with act.Fori(0, NC - BODY, BODY) as s:
                for j in range(BODY):
                    chunk(s + j, j)
            chunk(NC - 1, (NC - 1) % BODY, last=True)

        @block.vector
        def _(dve):
            done = [0]

            def step(ins):
                ins.then_inc(s_dve, 1)
                done[0] += 1
                dve.wait_ge(s_dve, done[0])

            dve.memset(zpad, 0.0).then_inc(s_pz, 1)
            dve.memset(Dall, 0.0).then_inc(s_pz, 1)
            dve.wait_ge(s_xh, 1)
            dve.tensor_tensor(xsp[1], OUT[:, :, 0:GT], xsp[0], ALU.subtract).then_inc(s_xl, 1)

            def lo_piece(n):
                hi, lo, _, shape, scale = pieces[n]
                dve.wait_ge(s_shi, n + 1)
                dve.scalar_tensor_tensor(out=lo, in0=staged(n, shape), scalar=scale, in1=hi, op0=ALU.mult,
                                         op1=ALU.subtract).then_inc(s_slo, 1)

            for n in range(2):
                lo_piece(n)
            dve.memset(Qsp[0][:, :, BOT:BOT + 1], 1.0).then_inc(s_dve, 1)
            dve.memset(Qsp[1][:, :, BOT:BOT + 1], 0.0).then_inc(s_one, 1)
            done[0] = 1
            dve.wait_ge(s_small, 16 * NSM)
            step(dve.tensor_copy(ids_f, ids_i))
            step(dve.tensor_scalar(b5, cst[:, C_EXP:C_EXP + NE], ids_f[:, 0:1], 5.0, ALU.is_equal, ALU.mult))
            dve.wait_ge(s_pool, POOL_DEN)
            dve.reciprocal(t_[2], t_[2]).then_inc(s_dsm, 1)
            for n in range(2, NPC):
                lo_piece(n)

            def t8(i):
                return gts[:, i, :].rearrange("p (t e) -> p t e", t=TPG)

            def wide(ap, n):
                return ap.unsqueeze(2).broadcast_to([P, TPG, n])

            def row(ap):
                return ap.unsqueeze(1).broadcast_to([P, TPG, NE])

            iota = cst[:, C_EXP:C_EXP + NE]

            def group(g, last=False):
                dve.wait_ge(s_lg, g + 1)
                Lg = t8(0)
                step(dve.scalar_tensor_tensor(out=Lg, in0=PS[:, 0, 0:TPG * NE].rearrange("p (t e) -> p t e", t=TPG),
                                              scalar=1.0 / S_R, in1=row(b5), op0=ALU.mult, op1=ALU.add))
                for i in range(2):
                    eq, cand, one = t8(1), t8(2), t8(3 + i)
                    top, first = gs[:, i, :], gs[:, 5, :]
                    step(dve.tensor_reduce(top, Lg, AX_X, ALU.max))
                    step(dve.tensor_tensor(eq, Lg, wide(top, NE), ALU.is_equal))
                    step(dve.scalar_tensor_tensor(out=cand, in0=eq, scalar=-100.0, in1=row(iota), op0=ALU.mult, op1=ALU.add))
                    step(dve.tensor_reduce(first, cand, AX_X, ALU.min))
                    step(dve.tensor_tensor(one, cand, wide(first, NE), ALU.is_equal))
                    if i == 0:
                        step(dve.scalar_tensor_tensor(out=t8(5), in0=one, scalar=-BIG, in1=Lg, op0=ALU.mult, op1=ALU.add))
                        Lg = t8(5)
                dve.tensor_tensor(gs[:, 2, :], gs[:, 1, :], gs[:, 0, :], ALU.subtract).then_inc(s_d, 1)
                dve.wait_ge(s_ex, g + 1)
                step(dve.tensor_scalar(gs[:, 4, :], gs[:, 3, :], 1.0, None, ALU.add))
                step(dve.reciprocal(gs[:, 0, :], gs[:, 4, :]))
                step(dve.tensor_tensor(gs[:, 1, :], gs[:, 0, :], gs[:, 3, :], ALU.mult))
                step(dve.tensor_tensor(t8(1), t8(3), wide(gs[:, 0, :], NE), ALU.mult))
                step(dve.tensor_tensor(t8(2), t8(4), wide(gs[:, 1, :], NE), ALU.mult))
                step(dve.tensor_tensor(gts[:, 6, :], gts[:, 1, :], gts[:, 2, :], ALU.add))
                dve.tensor_copy(Gx.rearrange("p (e r) -> p e r", r=RK),
                                gts[:, 6, :].unsqueeze(2).broadcast_to([P, TPG * NE, RK])).then_inc(s_gx, 1)
                dve.wait_ge(s_gTs, g + 1)
                dve.wait_ge(s_ha, g + 1)
                dve.scalar_tensor_tensor(out=hg32, in0=PS[:, 1, :], scalar=2.0 / S_W, in1=gTs, op0=ALU.mult,
                                         op1=ALU.mult).then_inc(s_hg, 1)
                dve.wait_ge(s_hgh, g + 1)
                dve.wait_ge(s_hg, g + 1)
                dve.tensor_tensor(hgsp[1], hg32, hgsp[0], ALU.subtract).then_inc(s_hgl, 1)
                for o in range(KT):
                    dve.wait_ge(s_hh, KT * g + o + 1)
                    dve.tensor_tensor(hsp[1][:, o, :], h32[:, o % 2, :], hsp[0][:, o, :], ALU.subtract).then_inc(s_hl, 1)
                    dve.tensor_tensor(OUT[:, o, tok(g)], OUT[:, o, tok(g)], h32[:, o % 2, :], ALU.add).then_inc(s_oadd, 1)
                if not last:
                    dve.wait_ge(s_xh, g + 2)
                    dve.tensor_tensor(xsp[1], OUT[:, :, tok(g + 1)], xsp[0], ALU.subtract).then_inc(s_xl, 1)
                for t in range(TPG):
                    dve.wait_ge(s_sc, TPG * g + t + 1)
                    dve.tensor_tensor(SA.rearrange("p (a n) -> p a n", a=2), PS[:, 1 + 3 * (t % 2), :].rearrange("p (a n) -> p a n", a=2),
                                      lrel.unsqueeze(1).broadcast_to([P, 2, NS]), ALU.add).then_inc(s_scr, 1)
                    dve.wait_ge(s_scr, TPG * g + t + 1)
                    step(dve.max(v8, SA[:, 0:NS]))
                    dve.wait_ge(s_e, TPG * g + t)
                    step(dve.match_replace(tm, v8, SA[:, 0:NS], -3.0e38))
                    step(dve.tensor_tensor(tm, tm, SA[:, 0:NS], ALU.is_equal))
                    step(dve.scalar_tensor_tensor(out=tm, in0=tm, scalar=-BIG, in1=SA[:, NS:2 * NS], op0=ALU.mult, op1=ALU.add))
                    dve.tensor_reduce(nm[:, t % 2:t % 2 + 1], tm, AX_X, ALU.max, negate=True).then_inc(s_t, 1)
                dve.wait_ge(s_k, g + 1)
                dve.wait_ge(s_kst, KST_FIRST + g * KST_GROUP)
                step(dve.tensor_scalar(kf, PS[0:TA, 5, :].rearrange("p (h b) -> p h b", h=HPG), 2.0 * S_W, None, ALU.mult))
                step(dve.scalar_tensor_tensor(out=kf[:, :, TB - 1], in0=Dall[:, bass.ds(g * HPG, HPG)], scalar=S_W,
                                              in1=kf[:, :, TB - 1], op0=ALU.mult, op1=ALU.add))
                dve.tensor_copy(ksp[0], kf).then_inc(s_kc, 1)
                dve.wait_ge(s_kc, 2 * g + 1)
                dve.tensor_tensor(ksp[1], kf, ksp[0], ALU.subtract).then_inc(s_kc, 1)
                dve.wait_ge(s_st, g + 1)
                dve.tensor_copy(st[:, :, bass.ds(TPG * g, TPG)], PS[:, 0, 64:64 + 3 * TPG].rearrange("p (a t) -> p a t", a=3))\
                   .then_inc(s_str, 1)

            for g in range(NG):
                group(g, last=(g == NG - 1))

            dve.wait_ge(s_str, NG)
            dve.wait_ge(s_sq, 2 * KT * NG)
            step(dve.memset(ones, 1.0))
            step(dve.tensor_scalar(gate[:, 0, :], st[:, 0, :], 1.0 / L, None, ALU.mult))
            step(dve.tensor_tensor(gate[:, 1, :], gate[:, 0, :], gate[:, 0, :], ALU.mult))
            dve.scalar_tensor_tensor(out=gate[:, 1, :], in0=st[:, 1, :], scalar=1.0 / L, in1=gate[:, 1, :], op0=ALU.mult,
                                     op1=ALU.subtract).then_inc(s_var, 1)
            dve.wait_ge(s_lv, 2)
            dve.tensor_reduce(gate[:, 3, 0:1], gate[:, 2, :], AX_X, ALU.add).then_inc(s_lvs, 1)
            dve.wait_ge(s_gsum, 1)
            step(dve.tensor_scalar(gate[:, 3, 1:2], PS[:, 0, 0:1], 1.0 / TOK, 1e-6, ALU.mult, ALU.add))
            step(dve.reciprocal(gate[:, 3, 2:3], gate[:, 3, 1:2]))
            step(dve.tensor_scalar(gate[:, 5, :], gate[:, 2, :], gate[:, 3, 2:3], 0.5, ALU.mult, ALU.mult))
            step(dve.scalar_tensor_tensor(out=gate[:, 5, :], in0=gate[:, 4, :], scalar=2.5, in1=gate[:, 5, :], op0=ALU.mult, op1=ALU.add))
            step(dve.tensor_scalar(gate[:, 5, :], gate[:, 5, :], 0.0, 5.0, ALU.max, ALU.min))
            step(dve.tensor_scalar(gate[:, 6, :], gate[:, 5, :], -0.5, 1.0 / 1.5, ALU.add, ALU.mult))
            dve.tensor_scalar(gate[:, 6, :], gate[:, 6, :], 0.0, 1.0, ALU.max, ALU.min).then_inc(s_un, 1)
            dve.wait_ge(s_sg, 1)
            step(dve.tensor_scalar(gate[:, 8, :], gate[:, 7, :], 0.05, None, ALU.is_ge))
            step(dve.tensor_tensor(gate[:, 8, :], gate[:, 8, :], gate[:, 7, :], ALU.mult))
            dve.wait_ge(s_e, NG * TPG)
            step(dve.reciprocal(gate[:, 9, :], seall))
            dve.tensor_tensor(gate[:, 10, :], gate[:, 8, :], gate[:, 9, :], ALU.mult).then_inc(s_gate, 1)
            dve.wait_ge(s_gate, 1)

            with dve.Fori(0, NG) as g:
                for t in range(TPG):
                    dve.wait_ge(s_eT, TPG * g + (t - 1 if t >= 2 else 0))
                    at = bass.ds(TPG * g + t, 1)
                    dve.tensor_scalar(eg[:, t % 2, :], e_all[:, at, :].rearrange("p a b -> p (a b)"), gate[:, 10, at], None,
                                      ALU.mult).then_inc(s_eg, 1)
                for o in range(KT):
                    dve.wait_ge(s_aux, KT * g + o + 1)
                    dve.tensor_tensor(OUT[:, o, tok(g)], OUT[:, o, tok(g)], PS[:, 6 + o % 2, :], ALU.add).then_inc(s_x1, 1)
                    if o % 2 == 0:
                        dve.wait_ge(s_uh, KT * g + o + 1)
                        dve.tensor_tensor(fsp[1][:, o, tok(g)], OUT[:, o, tok(g)], fsp[0][:, o, tok(g)], ALU.subtract)\
                           .then_inc(s_ul, 1)

            dve.wait_ge(s_lenf, 1)
            dve.wait_ge(s_aux, KT * NG)
            for k in range(KT):
                for c in range(2):
                    ins = dve.tensor_scalar(ymask[:, k, c * B:c * B + B], len_f, posF[:, k:k + 1], 1.0 / S_W, ALU.is_gt, ALU.mult)
            ins.then_inc(s_ym, 1)
            dve.wait_ge(s_ym, 1)

            def piece(n, lo, src, hi, scale):
                dve.wait_ge(s_fhi, n + 1)
                dve.scalar_tensor_tensor(out=lo, in0=src, scalar=scale, in1=hi, op0=ALU.mult, op1=ALU.subtract).then_inc(s_flo, 1)

            for n in range(N_C1):
                c = [x[:, 4 * n:4 * n + 4, :] for x in c1s]
                piece(n, c[1], fst[n][:, 0:4 * C1R].rearrange("p (k c) -> p k c", k=4), c[0], S_W)

            def w1_piece(q, par):
                c = [x[:, bass.ds(q, 1), 4 * par:4 * par + 4, :].rearrange("p a k i -> p (a k) i") for x in w1r]
                piece(N_C1 + 2 * q + par, c[1], as4(fst[par]), c[0], S_W)

            def c2_piece(q, par):
                c = c2s[RB:RB + RANK, bass.ds((2 * (q - 4) + par) * CPC, CPC)]
                piece(N_W1 + 2 * (q - 4) + par, c, fst[par][RB:RB + RANK, 0:CPC], c, S_R)

            def convolved(q, pieces_of):
                def mask(pair):
                    dve.wait_ge(s_cv, 8 * q + 2 * pair + 2)
                    dve.wait_ge(s_yh, 4 * q + (pair - 1 if pair >= 2 else 0))
                    dve.wait_ge(s_yl, 4 * q + (pair - 1 if pair >= 2 else 0))
                    dve.tensor_tensor(y32[:, pair % 2, :], PS[:, pair, :], ymask.rearrange("p k c -> p (k c)"), ALU.mult)\
                       .then_inc(s_y, 1)

                def low(pair):
                    dve.wait_ge(s_yh, 4 * q + pair + 1)
                    c = [x[:, :, bass.ds(q * 8 * B + pair * 2 * B, 2 * B)] for x in fsp]
                    dve.tensor_tensor(c[1], y32[:, pair % 2, :].rearrange("p (k c) -> p k c", k=KT), c[0], ALU.subtract)\
                       .then_inc(s_yl, 1)
                    if pair % 2:
                        pieces_of(q, pair // 2)

                mask(0)
                mask(1)
                low(0)
                mask(2)
                low(1)
                mask(3)
                low(2)
                low(3)

            with dve.Fori(0, 4) as q:
                convolved(q, w1_piece)
            with dve.Fori(4, 8) as q:
                convolved(q, c2_piece)

            def ffn_piece(n, par, phase, ring, tile):
                hi, lo = [ffn_slot(x, ring, CI * phase + tile, par) for x in range(2)]
                piece(n, lo, as4(fst[par]) if ring == 1 else fst[par], hi, S_W)

            for g in range(NG):
                dve.wait_ge(s_a1h, g + 1)
                c = a1s[2 * RB:2 * RB + RANK, g * GT:g * GT + GT]
                dve.scalar_tensor_tensor(out=c, in0=PS[2 * RB:2 * RB + RANK, 4 + g % 2, :], scalar=1.0 / S_W, in1=c,
                                         op0=ALU.mult, op1=ALU.subtract).then_inc(s_a1l, 1)
            for j in range(4):
                ffn_piece(N_C2 + j, j % 2, 0, 2, j // 2)

            def mask(n, t):
                sc = PS[:, t % 2, :].rearrange("p (k i) -> p k i", i=BLK)
                dve.wait_ge(s_in, TPG * n + t + 1)
                dve.wait_ge(s_mk, TPG * n + t)
                dve.tensor_reduce(bm, sc, AX_X, ALU.max).then_inc(s_bm, 1)
                dve.wait_ge(s_bm, TPG * n + t + 1)
                dve.wait_ge(s_mkT, TPG * n + (t - 1 if t >= 2 else 0))
                dve.tensor_tensor(mk[:, t % 2, :].rearrange("p (k i) -> p k i", i=BLK), sc,
                                  bm.unsqueeze(2).broadcast_to([P, CI * P // BLK, BLK]), ALU.is_equal).then_inc(s_mk, 1)

            for t in range(TPG):
                mask(0, t)

            def chunk(s, phase, last=False):
                base = N_W2 + PPC * s
                for g in range(NG):
                    n = NG * s + g
                    todo = [] if last else list(AT_STEP[g])

                    def next_piece():
                        if todo:
                            j = todo.pop(0)
                            ring, ahead, tile = CHUNK[j // 2]
                            ffn_piece(base + j, j % 2, phase + ahead, ring, tile)

                    dve.wait_ge(s_mT, 2 * n + 2)
                    for i in range(CI):
                        dve.wait_ge(s_g1, CI * n + i + 1)
                        dve.wait_ge(s_mh, CI * n + i)
                        dve.wait_ge(s_ml, CI * n + i)
                        dve.scalar_tensor_tensor(out=m32, in0=PS[:, 4 + i % 2, :], scalar=0.0, in1=mT[:, i, :], op0=ALU.max,
                                                 op1=ALU.mult).then_inc(s_m, 1)
                        if g == 0:
                            ring, ahead, tile = CHUNK[i // 2]
                            ffn_piece(base + i, i % 2, phase + ahead, ring, tile)
                    more = not (last and g == NG - 1)
                    if more:
                        mask(n + 1, 0)
                        mask(n + 1, 1)
                    for o in range(KT):
                        dve.wait_ge(s_o, KT * n + o + 1)
                        c = OUT[:, o, g * GT:g * GT + GT]
                        dve.scalar_tensor_tensor(out=c, in0=PS[:, 6 + o % 2, :], scalar=1.0 / S_W, in1=c, op0=ALU.mult,
                                                 op1=ALU.add).then_inc(s_oa, 1)
                        if more and o < 2:
                            mask(n + 1, o + 2)
                        if o >= 3:
                            next_piece()
                    assert not todo

            with dve.Fori(0, NC - BODY, BODY) as s:
                for j in range(BODY):
                    chunk(s + j, j)
            chunk(NC - 1, (NC - 1) % BODY, last=True)

        @block.gpsimd
        def _(pool):
            done = [0]

            def step(ins):
                ins.then_inc(s_pool, 1)
                done[0] += 1
                pool.wait_ge(s_pool, done[0])

            def tt(out_, a_, b_, op):
                step(pool.tensor_tensor(out_, a_, b_, op))

            def ts(out_, a_, x, y, o0, o1):
                step(pool.tensor_scalar(out_, a_, x, y, o0, o1))

            def fraction(out_, a_, tmp):
                ts(tmp, a_, MAGIC, -MAGIC, ALU.add, ALU.add)
                tt(out_, a_, tmp, ALU.subtract)

            pool.wait_ge(s_small, 16 * NSM)
            pool.wait_ge(s_rexp, 2)
            are, den, sn, sh, em = t_[1], t_[2], t_[3], t_[4], t_[5]
            tt(R_s, are, dt_s, ALU.mult)
            ts(R_s, R_s, -1.0, 0.0, ALU.mult, ALU.add)
            tt(th_s, aim_s, dt_s, ALU.mult)
            ts(th_s, th_s, 1.0 / (2.0 * np.pi), 0.0, ALU.mult, ALU.add)
            tt(t_[6], are, are, ALU.mult)
            tt(t_[7], aim_s, aim_s, ALU.mult)
            tt(den, t_[6], t_[7], ALU.add)
            assert done[0] == POOL_DEN
            fraction(sn, th_s, t_[6])
            ts(sh, sn, 1.0, 0.0, ALU.mult, ALU.add)
            assert done[0] == POOL_HALF
            ts(em, R_s, 1.0 / 9, 1.0, ALU.mult, ALU.add)
            for i in range(8, 1, -1):
                tt(em, em, R_s, ALU.mult)
                ts(em, em, 1.0 / i, 1.0, ALU.mult, ALU.add)
            tt(em, em, R_s, ALU.mult)
            pool.wait_ge(s_rexp, 4)
            c1m, er, ei, u, v = t_[6], t_[7], t_[8], t_[9], t_[10]
            tt(c1m, sh, sh, ALU.mult)
            ts(c1m, c1m, -2.0, 0.0, ALU.mult, ALU.add)
            tt(er, em, c1m, ALU.mult)
            tt(er, er, em, ALU.add)
            tt(er, er, c1m, ALU.add)
            tt(ei, em, sn, ALU.mult)
            tt(ei, ei, sn, ALU.add)
            tt(u, cr_s, er, ALU.mult)
            tt(v, ci_s, ei, ALU.mult)
            tt(u, u, v, ALU.subtract)
            tt(v, cr_s, ei, ALU.mult)
            tt(s1_s, ci_s, er, ALU.mult)
            tt(v, v, s1_s, ALU.add)
            pool.wait_ge(s_dsm, 1)
            tt(s1_s, v, aim_s, ALU.mult)
            tt(s2_s, u, are, ALU.mult)
            tt(s1_s, s1_s, s2_s, ALU.subtract)
            tt(s1_s, s1_s, den, ALU.mult)
            tt(s2_s, u, aim_s, ALU.mult)
            tt(v, v, are, ALU.mult)
            tt(s2_s, s2_s, v, ALU.add)
            tt(s2_s, s2_s, den, ALU.mult)
            ts(s1_s, s1_s, cst[:, C_SGN:C_SGN + 1], 0.0, ALU.mult, ALU.add)

            def group(g):
                hs = bass.ds(g * HPG, HPG)

                def head(x):
                    return x[:, hs].unsqueeze(2).broadcast_to([P, HPG, TB])

                def ramp(at):
                    return cst[:, at:at + TB].unsqueeze(1).broadcast_to([P, HPG, TB])

                E2, EA, EB = ph
                tt(E2, head(th_s), ramp(C_TB), ALU.mult)
                ts(E2, E2, cst[:, C_PHA:C_PHA + 1], 0.0, ALU.add, ALU.add)
                fraction(E2, E2, mg[0])
                tt(EA, head(th_s), ramp(C_TA), ALU.mult)
                ts(EB, EA, cst[:, C_PHB:C_PHB + 1], 0.0, ALU.add, ALU.add)
                ts(EA, EA, cst[:, C_PHA:C_PHA + 1], 0.0, ALU.add, ALU.add)
                fraction(EB, EB, mg[0])
                fraction(EA, EA, mg[0])
                tt(mg[1], head(R_s), ramp(C_TA), ALU.mult)
                pool.tensor_tensor(mg[0], head(R_s), ramp(C_TB), ALU.mult).then_inc(s_ph, 1)
                for o in range(KT):
                    pool.wait_ge(s_hev, KT * g + o + 1)
                    pool.wait_ge(s_sq, 2 * (KT * g + o))
                    if o == 0:
                        pool.wait_ge(s_st, g)
                        pool.tensor_tensor(acc, h32[:, 0, :], h32[:, 0, :], ALU.mult).then_inc(s_sq, 2)
                        continue
                    pool.tensor_tensor(sq, h32[:, o % 2, :], h32[:, o % 2, :], ALU.mult).then_inc(s_sq, 1)
                    pool.wait_ge(s_sq, 2 * (KT * g + o) + 1)
                    pool.tensor_tensor(acc, acc, sq, ALU.add).then_inc(s_sq, 1)
                pool.wait_ge(s_phd, 5 * g + 5)
                tt(E2, E2, mg[0], ALU.mult)
                tt(EA, EA, mg[1], ALU.mult)
                tt(EB, EB, mg[1], ALU.mult)
                tt(EA, EA, head(s1_s), ALU.mult)
                tt(EB, EB, head(s2_s), ALU.mult)
                pool.tensor_tensor(EA, EA, EB, ALU.add).then_inc(s_L, 1)
                pool.wait_ge(s_k, g + 1)

            for g in range(NG):
                group(g)

            for g in range(NG):
                for o in range(1, KT, 2):
                    pool.wait_ge(s_uh, KT * g + o + 1)
                    pool.tensor_tensor(fsp[1][:, o, tok(g)], OUT[:, o, tok(g)], fsp[0][:, o, tok(g)], ALU.subtract)\
                        .then_inc(s_ulp, 1)

            with pool.Fori(0, NC * NG) as n:
                for i in range(CI):
                    pool.wait_ge(s_mh, CI * n + i + 1)
                    pool.tensor_tensor(msp[1][:, i, :], m32, msp[0][:, i, :], ALU.subtract).then_inc(s_ml, 1)


def kernel(**inputs):
    import concourse.bacc as _bacc
    from concourse.bass_utils import run_bass_kernel_spmd as _run

    v = {k: np.asarray(a) for k, a in inputs.items()}

    def turned(w):
        return w.reshape(-1, KT, P)[:, :, ::-1].reshape(-1, L)

    bands = np.zeros((L, C1R), np.float32)
    bands2 = np.zeros((C1R, INTER), np.float32)
    for i in range(3):
        bands[:, RB * i:RB * i + RANK] = turned(v["L1_ffn_c1_w"]).T
        bands2[RB * i:RB * i + RANK] = v["L1_ffn_c2_w"].T
    Cm = v["L1_cond_C"]
    arrays = {
        "xT": v["x"].transpose(2, 1, 0).reshape(L, TOK),
        "WT": v["L0_cond_W"].T,
        "WrT": v["L0_cond_Wr"].T,
        "AT": v["L0_cond_A"].reshape(NE * RK, L).T,
        "BT": v["L0_cond_B"].transpose(0, 2, 1).reshape(NE * RK, L),
        "WqT": v["L0_ffn_Wq"].T,
        "Wr": v["L0_ffn_Wr"],
        "Wr2T": v["L0_ffn_Wr"].T,
        "keysT": v["L0_ffn_aux_keys"].T,
        "valuesT": v["L0_ffn_aux_values"].T,
        "WvdT": v["L0_ffn_Wvd"].T,
        "WvuT": v["L0_ffn_Wvu"].T,
        "Wu1T": v["L0_ffn_Wu1"].T,
        "bu1": v["L0_ffn_bu1"].reshape(2, P).T,
        "Wu2": v["L0_ffn_Wu2"].reshape(2, P).T,
        "bu2": v["L0_ffn_bu2"].reshape(1),
        "gate_w1": v["L0_ffn_gate_w1"].reshape(1),
        "gate_bias": v["L0_ffn_gate_bias"].reshape(1),
        "log_rel": v["L0_ffn_log_rel"],
        "log_dt": v["L1_cond_log_dt"],
        "Cri": Cm.transpose(2, 1, 0),
        "lar": v["L1_cond_log_A_real"].T,
        "aim": v["L1_cond_A_imag"].T,
        "Dh": v["L1_cond_D"].reshape(1, H),
        "c1P": bands,
        "c2T": bands2,
        "w1L": turned(v["L1_ffn_w1"]).reshape(IT, P, KT, P).transpose(0, 3, 2, 1).reshape(IT, P, L),
        "w2": v["L1_ffn_w2t"],
        "ids": v["itok_B_0_7"].reshape(B, 1),
        "lens": v["itok_B_78_3631"],
        "consts": shape_constants(),
    }
    nc = _bacc.Bacc("TRN2", target_bir_lowering=False, num_devices=1)
    given, args = {}, []
    for name, a in arrays.items():
        a = np.ascontiguousarray(a)
        given[f"in_{name}"] = a
        args.append(nc.dram_tensor(f"in_{name}", a.shape, mybir.dt.from_np(a.dtype), kind="ExternalInput").ap())
    args.append(nc.dram_tensor("out_0", (L, TOK), F32, kind="ExternalOutput").ap())
    build(nc, *args)
    r = _run(nc, [given], core_ids=[0])
    return np.ascontiguousarray(r.results[0]["out_0"].reshape(L, H, B).transpose(2, 1, 0))
```

```python
from contextlib import ExitStack

import numpy as np

import concourse.bass as bass
from concourse import mybir

F32 = mybir.dt.float32
F16 = mybir.dt.float16
I32 = mybir.dt.int32
ALU = mybir.AluOpType
ACT = mybir.ActivationFunctionType
AX_X = mybir.AxisListType.X

P = 128
B, H, L = 32, 64, 1024
TOK = B * H
KT = L // P
GT = 512
NG = TOK // GT
TPG = GT // P
BPT = P // H
HPG = H // NG
NE, RK = 8, 16
BOT, RD, NS = 64, 48, 256
UH = 256
SN = 64
TA, TB = 32, 32
RANK, INTER, BLK = 16, 3584, 64
IT = INTER // P
CI = 4
NC = IT // CI
RING = 6
BODY = 3
PAIR = 2 * P
STEP = 2
NT = TOK // P
SPC = NT // STEP
ST = STEP * P
OP = KT // 2
KROWS = L + P
RB = 32
C1R = 80

S_W = 64.0
S_R = 16.0
TWO_PI = 6.283185
LN2_HI, LN2_LO = 0.693359375, -2.12194440e-4
MAGIC = 12582912.0
BIG = 1.0e30

C_TB, C_TA, C_POS, C_EXP, C_PHA, C_PHB, C_SGN, C_ONE, C_E64, C_ID = 0, 32, 64, 72, 80, 81, 82, 83, 84, 85
C_N = C_ID + P


def shape_constants():
    c = np.zeros((P, C_N), np.float32)
    c[:, C_TB:C_TB + TB] = np.arange(TB)[::-1]
    c[:, C_TA:C_TA + TA] = TB * np.arange(TA)[::-1]
    c[:, C_POS:C_POS + KT] = np.arange(KT)[None] * P + np.arange(P)[::-1, None]
    c[:, C_EXP:C_EXP + NE] = np.arange(NE)
    c[:SN, C_PHA] = 0.25
    c[SN:, C_PHB] = 0.25
    c[:SN, C_SGN] = 1.0
    c[SN:, C_SGN] = -1.0
    c[:, C_ONE] = 1.0
    c[64, C_E64] = 1.0
    c[:, C_ID:] = np.eye(P)
    return c


class Arena:

    def __init__(self, region, words):
        self.region, self.words, self.at = region, words, 0

    def take(self, shape, dt=F32, parts=P):
        n = int(np.prod(shape))
        words = n if dt != F16 else (n + 1) // 2
        words = (words + 7) // 8 * 8
        ap = self.region[0:parts, self.at:self.at + words]
        if dt != F32:
            ap = ap.bitcast(dt)
        ap = ap[:, 0:n]
        self.at += words
        assert self.at <= self.words, (self.at, self.words)
        if len(shape) == 2:
            ap = ap.rearrange("p (a b) -> p a b", a=shape[0])
        elif len(shape) == 3:
            ap = ap.rearrange("p (a b c) -> p a b c", a=shape[0], b=shape[1])
        return ap


def build(nc, xT, WT, WrT, AT, BT, WqT, Wr, Wr2T, keysT, valuesT, WvdT, WvuT, Wu1T, bu1, Wu2, bu2, gate_w1,
          gate_bias, log_rel, log_dt, Cri, lar, aim, Dh, c1P, c2T, w1L, w2, ids, lens, consts, out):
    with ExitStack() as ctx:
        def sem(name):
            return ctx.enter_context(nc.semaphore(name))

        OUT = ctx.enter_context(nc.sbuf_tensor("OUT", [P, KT, TOK], F32))
        XF = ctx.enter_context(nc.sbuf_tensor("XF", [P, KT * TOK], F32))
        WORDS = 20440
        AR = ctx.enter_context(nc.sbuf_tensor("AR", [P, WORDS], F32))
        PS = ctx.enter_context(nc.psum_tensor("PS", [P, 8, 512], F32))
        PSH = PS[:, :, :].bitcast(F16)
        kp = [nc.dram_tensor(n, (H, KROWS), F16).ap() for n in ("taps_hi", "taps_lo")]

        xr = Arena(XF, KT * TOK)
        Wsp = [xr.take([KT, L], F16) for _ in range(2)]
        xsp = [xr.take([KT, GT], F16) for _ in range(2)]
        hsp = [xr.take([KT, GT], F16) for _ in range(2)]
        assert xr.at == KT * TOK
        xr = Arena(XF, KT * TOK)
        fsp = [xr.take([KT, TOK], F16) for _ in range(2)]

        a = Arena(AR, WORDS)
        cst = a.take([C_N])
        e_all = a.take([TOK // P, NS])
        stage = [e_all[:, 4 * i:4 * i + 4, :].rearrange("p a b -> p (a b)") for i in range(2)]
        u1_at = a.at
        U1 = [a.take([KT, UH], F16) for _ in range(2)]
        Asp = [a.take([KT, P], F16) for _ in range(2)]
        Bsp = [a.take([L], F16) for _ in range(2)]
        Qsp = [a.take([KT, BOT + 1], F16) for _ in range(2)]
        Rsp = [a.take([KT, NE], F16) for _ in range(2)]
        h32 = a.take([2, GT])
        sq = a.take([GT])
        acc = a.take([GT])
        ones = sq[:, 0:P]
        gl = a.take([2, GT])
        Gx, gTs = gl[:, 0, :], gl[:, 1, :]
        hg32 = a.take([GT])
        kf = hg32[0:TA, :].rearrange("p (h b) -> p h b", h=HPG)
        hgsp = [a.take([GT], F16) for _ in range(2)]
        ksp = [a.take([HPG, TB], F16, TA) for _ in range(2)]
        qT = a.take([GT])
        MK = a.take([2 * NS])
        AV = a.take([2, BOT])
        SA = a.take([2 * NS])
        tm = a.take([NS])
        ph = [a.take([HPG, TB]) for _ in range(3)]
        mg = [a.take([HPG, TB]) for _ in range(2)]
        lrel = a.take([NS])
        small = a.take([20, SN])
        gts = a.take([7, TPG * NE])
        gs = a.take([6, TPG])
        st = a.take([3, TOK // P])
        seall = a.take([TOK // P])
        nm = a.take([2])
        v8 = a.take([8])
        b5 = a.take([TOK // P, NE])
        gate = a.take([12, TOK // P])
        scal = a.take([8])
        bu1s = a.take([2])
        wu2s = a.take([2])
        ids_i = tm[:, 0:TOK // P].bitcast(I32)
        ids_f = tm[:, TOK // P:2 * TOK // P]
        zpad = a.take([P], F16)
        Dall = a.take([H], F32, TA)
        c = Arena(AR, WORDS)
        c.at = u1_at
        wvu = c.take([L])
        zT = c.take([GT])
        c = Arena(AR, WORDS)
        c.at = u1_at + 2048
        eT = c.take([2, GT])
        eg = c.take([2, NS])

        ident = cst[:, C_ID:C_ID + P]
        logs, exps = small[:, 0:2, :], small[:, 2:4, :]
        dt_s, are_s = exps[:, 0, :], exps[:, 1, :]
        aim_s, cr_s, ci_s, R_s, th_s, s1_s, s2_s = (small[:, i, :] for i in range(4, 11))
        t_ = [small[:, 11 + i, :] for i in range(9)]

        f = Arena(AR, WORDS)
        w1r = [f.take([RING // 2, KT, PAIR], F16) for _ in range(2)]
        w2_at = f.at
        w2r = [f.take([RING, L], F16) for _ in range(2)]
        m_at = f.at
        msp = [f.take([2, CI, ST], F16) for _ in range(2)]
        a1s = f.take([TOK], F16, C1R)
        c2s = f.take([INTER], F16, C1R)
        mk_at = f.at
        mtok = [f.take([2, CI * P], F16) for _ in range(2)]
        mk = f.take([2, CI * P], F16)
        fst = [f.take([512]) for _ in range(2)]
        m32 = f.take([CI * P])
        bm = f.take([BLK // 8])
        idF = f.take([P], F16)
        nk_i = f.take([NT], I32)
        f2 = Arena(AR, WORDS)
        f2.at = w2_at
        toep = [[f2.take([L], F16) for _ in range(2)] for _ in range(4)]
        c1s = [f2.take([KT, C1R], F16) for _ in range(2)]
        id32 = f2.take([P])
        len_i = f2.take([B], I32)
        len_f = f2.take([B])
        posF = f2.take([KT])
        nkf = f2.take([2, NT])
        f2.at = m_at
        y32 = f2.take([2, KT * 2 * B])
        f2.at = mk_at
        ymask = f2.take([KT, 2 * B])

        s_x = sem("x_loaded")
        s_stage = [sem("stage0_loaded"), sem("stage1_loaded")]
        s_shi = sem("stage_hi_made")
        s_slo = sem("stage_lo_made")
        s_small = sem("small_loaded")
        s_xh = sem("x_hi_made")
        s_xl = sem("x_lo_made")
        s_pre = sem("prep_product")
        s_prev = sem("prep_evacuated")
        s_lg = sem("logits_ready")
        s_ha = sem("lora_down_ready")
        s_base = sem("h0_ready")
        s_d = sem("expert_gap_ready")
        s_ex = sem("expert_exp_ready")
        s_gx = sem("gates_spread")
        s_gT = sem("gates_turned")
        s_gTs = sem("gates_turned_in_sbuf")
        s_hg = sem("gated_down_ready")
        s_hgh = sem("gated_hi_made")
        s_hgl = sem("gated_lo_made")
        s_hev = sem("h0_in_sbuf")
        s_hh = sem("h0_hi_made")
        s_hl = sem("h0_lo_made")
        s_oadd = sem("h0_added_to_x")
        s_sq = sem("h0_squares_summed")
        s_q = sem("query_ready")
        s_qT = sem("query_in_sbuf")
        s_u = sem("uncertainty_hidden_ready")
        s_gl = sem("gelu_done")
        s_sc = sem("scores_ready")
        s_scr = sem("scores_read")
        s_t = sem("attention_masked")
        s_e = sem("attention_exp_done")
        s_st = sem("token_sums_ready")
        s_str = sem("token_sums_read")
        s_rexp = sem("state_exp_small")
        s_dsm = sem("state_reciprocal")
        s_ph = sem("state_phases_ready")
        s_phd = sem("state_waves_done")
        s_L = sem("state_factors_ready")
        s_k = sem("taps_ready")
        s_kc = sem("taps_split")
        s_kst = sem("taps_stored")
        s_pz = sem("tap_zeros_made")
        s_dve = sem("vector_step")
        s_pool = sem("pool_step")
        s_one = sem("query_ones_set")
        s_wvu = sem("Wvu_loaded")
        s_var = sem("variance_ready")
        s_lv = sem("log_variance_ready")
        s_lvs = sem("log_variance_sums_ready")
        s_un = sem("uncertainty_ready")
        s_sg = sem("gate_sigmoid_ready")
        s_gate = sem("gate_ready")
        s_ulp = sem("x1_lo_made_by_gpsimd")
        s_idf = sem("identity_cast")
        s_lenf = sem("lengths_cast")
        s_bm = sem("block_max_ready")
        s_out = sem("out_stored")
        s_gsum = sem("log_var_summed")
        s_eT = sem("attention_turned")
        s_eTs = sem("attention_turned_in_sbuf")
        s_eg = sem("attention_gated")
        s_z = sem("memory_read")
        s_zTs = sem("memory_in_sbuf")
        s_aux = sem("memory_out_ready")
        s_x1 = sem("x1_ready")
        s_uh = sem("x1_hi_made")
        s_ul = sem("x1_lo_made")
        s_lenl = sem("lengths_loaded")
        s_ym = sem("length_mask_made")
        s_tp = [sem(f"toeplitz{i}_loaded") for i in range(4)]
        s_cv = sem("head_convolved")
        s_y = sem("y_masked")
        s_yh = sem("y_hi_made")
        s_yl = sem("y_lo_made")
        s_fst = [sem("ffn_stage0_loaded"), sem("ffn_stage1_loaded")]
        s_fhi = sem("ffn_weight_hi_made")
        s_flo = sem("ffn_weight_lo_made")
        s_a1 = sem("rank_product_ready")
        s_a1h = sem("rank_hi_made")
        s_a1l = sem("rank_lo_made")
        s_in = sem("inter_ready")
        s_mk = sem("argmax_mask_made")
        s_mT = sem("hidden_turned")
        s_mTs = sem("hidden_in_sbuf")
        s_nk = sem("tile_counts_made")
        s_g1 = sem("ffn_hidden_ready")
        s_m = sem("hidden_masked")
        s_mh = sem("hidden_hi_made")
        s_ml = sem("hidden_lo_made")
        s_o = sem("ffn_out_ready")
        s_oa = sem("ffn_out_added")

        START = 2
        from_start = [s_str, s_scr, s_hev, s_kc, s_gl, s_oadd, s_sq, s_zTs, s_x1, s_z, s_eTs, s_eT, s_y, s_yh, s_yl, s_a1l,
                    s_oa, s_o, s_e]

        pieces = [
            (Rsp[0], Rsp[1], WrT.rearrange("(k p) e -> p k e", p=P), [KT, NE], S_R),
            (Asp[0], Asp[1], AT.rearrange("(k p) e -> p k e", p=P), [KT, P], S_W),
        ]
        wt = WT.rearrange("(k p) o -> k p o", p=P)
        pieces += [(Wsp[0][:, k, :], Wsp[1][:, k, :], wt[k], [L], S_W) for k in range(KT)]
        pieces += [
            (Bsp[0], Bsp[1], BT, [L], S_W),
            (Qsp[0][:, :, 0:BOT], Qsp[1][:, :, 0:BOT], WqT.rearrange("(k p) e -> p k e", p=P), [KT, BOT], 1.0),
        ]
        u1v = Wu1T.rearrange("(k p) e -> p k e", p=P)
        pieces += [(U1[0][:, 4 * i:4 * i + 4, :], U1[1][:, 4 * i:4 * i + 4, :], u1v[:, 4 * i:4 * i + 4, :], [4, UH], 1.0)
                   for i in range(2)]
        NPC = len(pieces)
        N_A, N_W, N_ALL = 2, 2 + KT, NPC

        def staged(n, shape):
            s = stage[n % 2][:, 0:int(np.prod(shape))]
            return s.rearrange("p (a b) -> p a b", a=shape[0]) if len(shape) == 2 else s

        def head_of(x, h, n):
            v = x.rearrange("p k (b h) -> p k h b", h=H)
            return v[:, :, bass.ds(h, n), :] if n > 1 else v[:, :, bass.ds(h, 1), :].rearrange("p k c b -> p k (c b)")

        def tok(g):
            return bass.ds(g * GT, GT)

        small_loads = [
            (cst, consts), (bu1s, bu1), (wu2s, Wu2),
            (scal[:, 0:1], bu2.partition_broadcast(P)), (scal[:, 1:2], gate_w1.partition_broadcast(P)),
            (scal[:, 2:3], gate_bias.partition_broadcast(P)),
            (lrel, log_rel.partition_broadcast(P)),
        ]
        idv = ids.rearrange("(t c) -> c t", c=BPT)
        small_loads += [(ids_i[H * i:H * i + H, :], idv[i].partition_broadcast(H)) for i in range(BPT)]
        for half in range(2):
            r = slice(SN * half, SN * half + SN)
            small_loads += [(logs[r, 1, :], lar), (aim_s[r, :], aim), (cr_s[r, :], Cri[0]), (ci_s[r, :], Cri[1])]
        small_loads += [(logs[:, 0, :], log_dt.partition_broadcast(P)), (Dall[TA - 1:TA, :], Dh)]
        fold_wr = ph[0][0:RD, 0:2, :].rearrange("p a b -> p (a b)")
        fold_wr2 = ph[0][0:BOT, 2:4, :].rearrange("p a b -> p (a b)")[:, 0:RD]
        fold_keys = ph[0][0:BOT, 4:12, :].rearrange("p a b -> p (a b)")
        fold_rk = ph[1][0:RD, 0:8, :].rearrange("p a b -> p (a b)")
        vT = e_all[:, 8:16, :]
        vdT = gl.rearrange("p a b -> p (a b)")[:, 0:KT * BOT].rearrange("p (k e) -> p k e", k=KT)
        small_loads += [
            (fold_wr, Wr), (fold_wr2, Wr2T), (fold_keys, keysT),
            (vT, valuesT.rearrange("(k p) n -> p k n", p=P)), (vdT, WvdT.rearrange("(k p) e -> p k e", p=P)),
        ]
        NSM = len(small_loads)
        w1v = w1L.rearrange("t p c -> (t p) c")

        def w1_source(pair, q):
            return w1v[bass.ds(pair * P, P), q * 512:q * 512 + 512]

        def w2_source(it, half):
            return w2[bass.ds(it * P, P), half * 512:half * 512 + 512]

        def as4(x):
            return x.rearrange("p (k i) -> p k i", k=4)

        N_C1, N_W1, N_C2, N_W2 = 2, 2 + 2 * CI, 2 + 2 * CI + 8, 2 + 2 * CI + 8 + 6
        CPC = INTER // 8
        W1_SLOTS = [(0, 1), (0, 2), (1, 2)]
        W1_EARLY = [1, 0, 0]

        def chunk_pieces(s, phase, last=False):
            def w1_pair(which):
                slot = W1_SLOTS[(phase + 1) % BODY][which]
                return [(1, w1_source((s + 1) * (CI // 2) + which, q), slot * KT * PAIR + q * 512) for q in range(4)]

            def w2_half(c, tile, half):
                slot = (CI * (phase + c) + tile) % RING
                return (2, w2_source((s + c) * CI + tile, half), slot * L + half * 512)

            own = [w2_half(0, 2, 1), w2_half(0, 3, 1)]
            if last:
                return own
            early = W1_EARLY[phase]
            return (own + w1_pair(early)
                    + [w2_half(1, t, h) for t in range(2) for h in range(2)]
                    + w1_pair(1 - early) + [w2_half(1, 2, 0), w2_half(1, 3, 0)])

        def first(n):
            return isinstance(n, int) and n == 0

        w2_first = [(0, 0), (0, 1), (1, 0), (1, 1), (2, 0), (3, 0)]
        PPC = 16

        AT_STEP = [((0, 1), (), (), ()), ((), (), (2,), (3,)), ((), (), (4,), (5,)), ((), (), (6,), (7,)),
                   ((), (), (8,), (9,)), ((), (), (), ()), ((), (10,), (11,), (12, 13)), ((), (), (), (14, 15))]

        def w1_flat(part):
            return w1r[part].rearrange("p a b c -> p (a b c)")

        def ring_slot(part, ring, at):
            flat = w1_flat(part) if ring == 1 else w2r[part].rearrange("p a b -> p (a b)")
            return flat[:, at:at + 512]

        POOL_DEN, POOL_HALF = 31, 34
        KST_FIRST, KST_GROUP = 32, 32 * HPG

        def tap_rows(i, g, hh):
            src = kp[i][bass.ds(g * HPG + hh, 1), 0:L]
            return bass.AP(tensor=src.tensor, offset=src.offset, ap=[[TB, TA], [1, TB]])

        block = ctx.enter_context(nc.Block())

        @block.sync
        def _(sp):
            xv = xT.rearrange("(k p) t -> p k t", p=P)
            ov = out.rearrange("(k p) t -> p k t", p=P)
            sp.dma_start(OUT[:, :, 0:GT], xv[:, :, 0:GT]).then_inc(s_x, 16)
            for n, (hi, lo, src, shape, _) in enumerate(pieces):
                if n >= 2:
                    sp.wait_ge(s_shi, n - 1)
                    sp.wait_ge(s_slo, n - 1)
                sp.dma_start(staged(n, shape), src).then_inc(s_stage[n % 2], 16)
            sp.wait_ge(s_pz, 2)
            for i in range(2):
                sp.dma_start(kp[i][:, L:KROWS], zpad[0:H, :]).then_inc(s_kst, 16)
            with sp.Fori(0, NG - 1) as g:
                sp.wait_ge(s_x, g * 16 + 16)
                sp.dma_start(OUT[:, :, tok(g + 1)], xv[:, :, tok(g + 1)]).then_inc(s_x, 16)
                sp.wait_ge(s_kc, START + 2 * g + 2)
                for i in range(2):
                    for hh in range(HPG):
                        sp.dma_start(tap_rows(i, g, hh), ksp[i][:, hh, :]).then_inc(s_kst, 16)
            sp.wait_ge(s_kc, START + 2 * NG)
            for i in range(2):
                for hh in range(HPG):
                    sp.dma_start(tap_rows(i, NG - 1, hh), ksp[i][:, hh, :]).then_inc(s_kst, 16)
            sp.wait_ge(s_u, 2 * NG)
            sp.dma_start(wvu[0:BOT, :], WvuT).then_inc(s_wvu, 16)
            sp.wait_ge(s_aux, KT * NG)
            sp.dma_start(len_i, lens.partition_broadcast(P)).then_inc(s_lenl, 16)
            sp.dma_start(posF, consts[:, C_POS:C_POS + KT], allow_slow_non_contiguous=True).then_inc(s_lenl, 16)
            sp.dma_start(id32, consts[:, C_ID:C_ID + P]).then_inc(s_lenl, 16)
            sp.wait_ge(s_kst, 32 + 32 * HPG * NG)

            def toeplitz(h, i):
                for j in range(2):
                    src = kp[j][bass.ds(h, 1), 0:L]
                    src = bass.AP(tensor=src.tensor, offset=src.offset, ap=[[1, P], [1, L]])
                    sp.dma_start(toep[i][j], src).then_inc(s_tp[i], 16)

            def piece(n, par, dst, src, first=False):
                if not first:
                    sp.wait_ge(s_fhi, n - 1)
                    sp.wait_ge(s_flo, n - 1)
                sp.dma_start(dst, src).then_inc(s_fst[par], 16)

            for i in range(4):
                toeplitz(i, i)
            c1v = c1P.rearrange("(k p) c -> p k c", p=P)
            for n in range(N_C1):
                piece(n, n, fst[n][:, 0:4 * C1R].rearrange("p (k c) -> p k c", k=4), c1v[:, 4 * n:4 * n + 4, :], first=True)

            def heads(q, pieces_of):
                for i in range(8):
                    if i in (0, 4):
                        pieces_of(q, i // 4)
                    sp.wait_ge(s_cv, 8 * q + i + 1)
                    toeplitz(8 * q + 4 + i, i % 4)

            def w1_piece(q, par):
                src = w1L[0:1, 0:P, 0:512]
                at = (q // 2) * (P * KT * PAIR) + (2 * (q % 2) + par) * 512
                src = bass.AP(tensor=src.tensor, offset=src.offset + at, ap=[[KT * PAIR, P], [1, 512]])
                piece(N_C1 + 2 * q + par, par, fst[par], src)

            def c2_piece(q, par):
                piece(N_W1 + 2 * (q - 4) + par, par, fst[par][0:C1R, 0:CPC],
                      c2T[:, bass.ds((2 * (q - 4) + par) * CPC, CPC)])

            with sp.Fori(0, 4) as q:
                heads(q, w1_piece)
            with sp.Fori(4, 7) as q:
                heads(q, c2_piece)
            c2_piece(7, 0)
            for i in range(4):
                sp.wait_ge(s_cv, 56 + i + 1)
                toeplitz(60 + i, i)
            c2_piece(7, 1)
            for j, (tile, half) in enumerate(w2_first):
                piece(N_C2 + j, j % 2, fst[j % 2], w2_source(tile, half))

            def chunk(s, phase, last=False):
                for j, (_, src, _) in enumerate(chunk_pieces(s, phase, last)):
                    piece(N_W2 + PPC * s + j, j % 2, fst[j % 2], src)

            with sp.Fori(0, NC - BODY, BODY) as s:
                for j in range(BODY):
                    chunk(s + j, j)
            chunk(NC - 1, (NC - 1) % BODY, last=True)
            stores = 0
            for j in range(SPC):
                w = 4 if j < SPC - 1 else 2
                for o in range(0, KT, w):
                    sp.wait_ge(s_oa, START + OP * (SPC * (NC - 1) + j) + (o + w) // 2)
                    sp.dma_start(ov[:, o:o + w, j * ST:j * ST + ST], OUT[:, o:o + w, j * ST:j * ST + ST]).then_inc(s_out, 16)
                    stores += 1
            sp.wait_ge(s_out, 16 * stores)

        @block.tensor
        def _(pe):
            def mm3(dst, lhs, rhs, k, n, more=False):
                (lh, ll), (rh, rl) = lhs, rhs
                pe.matmul(dst, lh, rh, start=(k == 0), stop=False)
                pe.matmul(dst, lh, rl, start=False, stop=False)
                return pe.matmul(dst, ll, rh, start=False, stop=(k == n - 1 and not more))

            pe.wait_ge(s_small, 16 * NSM)
            pe.matmul(PS[0:RD, 0, 0:NS], fold_wr2, fold_keys, start=True, stop=True).then_inc(s_pre, 1)
            for n in range(2):
                for k in range(KT):
                    mm = pe.matmul(PS[:, 1, BOT * n:BOT * n + BOT], vT[:, k, n * P:n * P + P], vdT[:, k, :],
                                   start=(k == 0), stop=(k == KT - 1))
            mm.then_inc(s_pre, 1)
            pe.wait_ge(s_prev, 1)
            pe.matmul(PS[0:BOT, 2, 0:NS], fold_wr, fold_rk, start=True, stop=True).then_inc(s_pre, 1)
            pe.wait_ge(s_prev, 4)

            def group(g):
                pe.wait_ge(s_xh, g + 1)
                pe.wait_ge(s_xl, g + 1)
                pe.wait_ge(s_shi, N_A)
                pe.wait_ge(s_slo, N_A)
                pe.wait_ge(s_str, START + g)
                for t in range(TPG):
                    for k in range(KT):
                        mm = mm3(PS[:, 0, NE * t:NE * t + NE], [x[:, k, t * P:t * P + P] for x in xsp],
                                 [w[:, k, :] for w in Rsp], k, KT)
                mm.then_inc(s_lg, 1)
                pe.wait_ge(s_scr, START + TPG * g)
                for k in range(KT):
                    mm = mm3(PS[:, 1, :], [w[:, k, :] for w in Asp], [x[:, k, :] for x in xsp], k, KT)
                mm.then_inc(s_ha, 1)

                def base(o):
                    for k in range(KT):
                        mm3(PS[:, 2 + o % 2, :], [w[:, k, o * P:o * P + P] for w in Wsp],
                            [x[:, k, :] for x in xsp], k, KT, more=True)

                def lora(o):
                    (bh, bl), (gh, gl_) = [w[:, o * P:o * P + P] for w in Bsp], hgsp
                    pe.matmul(PS[:, 2 + o % 2, :], bh, gh, start=False, stop=False)
                    pe.matmul(PS[:, 2 + o % 2, :], bh, gl_, start=False, stop=False)
                    pe.matmul(PS[:, 2 + o % 2, :], bl, gh, start=False, stop=True).then_inc(s_base, 1)

                pe.wait_ge(s_shi, N_W)
                pe.wait_ge(s_slo, N_W)
                pe.wait_ge(s_hev, START + KT * g)
                base(0)
                pe.wait_ge(s_gx, g + 1)
                for t in range(TPG):
                    mm = pe.transpose(PS[:, 4, t * P:t * P + P], Gx[:, t * P:t * P + P], ident)
                mm.then_inc(s_gT, 1)
                base(1)
                pe.wait_ge(s_hgh, g + 1)
                pe.wait_ge(s_hgl, g + 1)
                pe.wait_ge(s_shi, NPC)
                pe.wait_ge(s_slo, NPC)
                lora(0)
                lora(1)
                for o in range(2, KT):
                    pe.wait_ge(s_hev, START + KT * g + o - 1)
                    base(o)
                    lora(o)
                pe.wait_ge(s_one, 1)
                pe.wait_ge(s_hh, KT * g + KT)
                pe.wait_ge(s_hl, KT * g + KT)
                pe.wait_ge(s_kc, START + 2 * g)
                for k in range(KT):
                    mm = mm3(PS[0:BOT + 1, 5, :], [w[:, k, :] for w in Qsp], [x[:, k, :] for x in hsp], k, KT)
                mm.then_inc(s_q, 1)
                pe.wait_ge(s_gl, START + 2 * g)
                for n in range(2):
                    for k in range(KT):
                        mm = mm3(PS[:, 6 + n, :], [w[:, k, n * P:n * P + P] for w in U1], [x[:, k, :] for x in hsp], k, KT)
                    mm.then_inc(s_u, 1)
                pe.wait_ge(s_qT, g + 1)
                for t in range(TPG):
                    if t >= 2:
                        pe.wait_ge(s_scr, START + TPG * g + t - 1)
                    pe.matmul(PS[:, 1 + 3 * (t % 2), :], qT[0:BOT, t * P:t * P + P], MK[0:BOT, :],
                              start=True, stop=True).then_inc(s_sc, 1)
                pe.wait_ge(s_L, g + 1)
                for h in range(HPG):
                    mm = pe.matmul(PS[0:TA, 5, h * TB:h * TB + TB], ph[1][:, h, :], ph[0][:, h, :], start=True, stop=True)
                mm.then_inc(s_k, 1)
                pe.wait_ge(s_sq, START + 2 * KT * g + 2 * KT)
                pe.wait_ge(s_gl, START + 2 * g + 2)
                for t in range(TPG):
                    c = slice(t * P, t * P + P)
                    pe.matmul(PS[:, 0, 64 + t:65 + t], qT[0:BOT + 1, c], cst[0:BOT + 1, C_E64:C_E64 + 1], start=True, stop=True)
                    pe.matmul(PS[:, 0, 68 + t:69 + t], acc[:, c], cst[:, C_ONE:C_ONE + 1], start=True, stop=True)
                    pe.matmul(PS[:, 0, 72 + t:73 + t], gl[:, 0, c], wu2s[:, 0:1], start=True, stop=False)
                    mm = pe.matmul(PS[:, 0, 72 + t:73 + t], gl[:, 1, c], wu2s[:, 1:2], start=False, stop=True)
                mm.then_inc(s_st, 1)

            with pe.Fori(0, NG - 1) as g:
                group(g)
            group(NG - 1)

            pe.wait_ge(s_lvs, 1)
            pe.matmul(PS[:, 0, 0:1], ones, gate[:, 3, 0:1], start=True, stop=True).then_inc(s_gsum, 1)
            pe.wait_ge(s_wvu, 16)
            pe.wait_ge(s_e, START + NG * TPG)
            pe.wait_ge(s_gate, 1)

            def mix(g):
                for t in range(TPG):
                    pe.wait_ge(s_eg, TPG * g + t + 1)
                    pe.wait_ge(s_eTs, START + TPG * g + t - 1)
                    for n in range(2):
                        mm = pe.transpose(PS[:, t % 2, n * P:n * P + P], eg[:, t % 2, n * P:n * P + P], ident)
                    mm.then_inc(s_eT, 1)
                pe.wait_ge(s_eTs, START + TPG * g + TPG)
                pe.wait_ge(s_zTs, START + g)
                for n in range(2):
                    mm = pe.matmul(PS[0:BOT, 4, :], AV[:, n, :], eT[:, n, :], start=(n == 0), stop=(n == 1))
                mm.then_inc(s_z, 1)
                pe.wait_ge(s_zTs, START + g + 1)
                for o in range(KT):
                    pe.wait_ge(s_x1, START + KT * g + o - 1)
                    pe.matmul(PS[:, 6 + o % 2, :], wvu[0:BOT, o * P:o * P + P], zT[0:BOT, :],
                              start=True, stop=True).then_inc(s_aux, 1)

            with pe.Fori(0, NG) as g:
                mix(g)

            pe.wait_ge(s_uh, KT * NG)
            pe.wait_ge(s_ul, KT * NG // 2)
            pe.wait_ge(s_ulp, KT * NG // 2)

            with pe.Fori(0, H // 8) as q:
                for i in range(8):
                    pair = i // 2
                    if i % 2 == 0:
                        pe.wait_ge(s_y, START + 4 * q)
                    pe.wait_ge(s_tp[i % 4], 32 * (2 * q + i // 4 + 1))
                    bank = PS[:, pair, :].rearrange("p (i c b) -> p i c b", i=KT, c=2)
                    for d in range(KT):
                        dst = bank[:, d:KT, i % 2, :]
                        th, tl = [t[:, (KT - 1 - d) * P:(KT - d) * P] for t in toep[i % 4]]
                        uh, ul = [head_of(u[:, 0:KT - d, :], q * 8 + i, 1) for u in fsp]
                        pe.matmul(dst, th, uh, start=(d == 0), stop=False)
                        pe.matmul(dst, th, ul, start=False, stop=False)
                        mm = pe.matmul(dst, tl, uh, start=False, stop=(d == KT - 1))
                    mm.then_inc(s_cv, 1)

            pe.wait_ge(s_fhi, N_C1)
            pe.wait_ge(s_flo, N_C1)
            pe.wait_ge(s_yh, START + H // 2)
            pe.wait_ge(s_yl, START + H // 2)
            with pe.Fori(0, NG // 2) as g2:
                for j in range(2):
                    pe.wait_ge(s_a1l, START + 2 * g2)
                    for k in range(KT):
                        mm = mm3(PS[0:C1R, 4 + j, :], [w[:, k, :] for w in c1s],
                                 [y[:, k, bass.ds(g2 * 2 * GT + j * GT, GT)] for y in fsp], k, KT)
                    mm.then_inc(s_a1, 1)

            pe.wait_ge(s_nk, 1)
            tiles = [pe.value_load(nk_i[0:1, t:t + 1], min_val=2, max_val=KT) for t in range(NT)]

            def inter(n, s, j, t):
                if not first(n):
                    pe.wait_ge(s_mk, STEP * n + t - 1)
                T = STEP * j + t
                pe.matmul(PS[:, t, :], a1s[:, T * P:T * P + P], c2s[:, bass.ds(s * CI * P, CI * P)],
                          start=True, stop=True).then_inc(s_in, 1)

            def hidden(n, phase, j, t):
                if not first(n):
                    pe.wait_ge(s_m, STEP * n + t - 1)
                T, (a_, b_) = STEP * j + t, W1_SLOTS[phase]
                dst = PS[:, 2 + t, :]

                def operands(k):
                    if isinstance(k, int):
                        y = [x[:, k, T * P:T * P + P] for x in fsp]
                        return y, [w[:, a_:b_ + 1:b_ - a_, k, :] for w in w1r]
                    y = [x[:, bass.ds(k, 1), T * P:T * P + P].rearrange("p a b -> p (a b)") for x in fsp]
                    return y, [w[:, a_:b_ + 1:b_ - a_, bass.ds(k, 1), :].rearrange("p s a b -> p s (a b)") for w in w1r]

                (yh, yl), (wh, wl) = operands(0)
                pe.matmul(dst, yh, wh, start=True, stop=False)
                pe.matmul(dst, yh, wl, start=False, stop=False)
                with pe.Fori(1, tiles[T]) as k:
                    (kh, kl), (vh, vl) = operands(k)
                    pe.matmul(dst, kh, vh, start=False, stop=False)
                    pe.matmul(dst, kh, vl, start=False, stop=False)
                    pe.matmul(dst, kl, vh, start=False, stop=False)
                pe.matmul(dst, yl, wh, start=False, stop=True).then_inc(s_g1, 1)

            def turn(n, t):
                pe.wait_ge(s_mh, STEP * n + t + 1)
                pe.wait_ge(s_ml, STEP * n + t + 1)
                if not first(n):
                    pe.wait_ge(s_mTs, STEP * n + t - 1)
                for part in range(2):
                    for i in range(CI):
                        at = (part * CI + i) * P
                        mm = pe.transpose(PSH[:, 4 + t, at:at + P], mtok[t][:, part, i * P:i * P + P], idF)
                mm.then_inc(s_mT, 1)

            pe.wait_ge(s_a1h, NG)
            pe.wait_ge(s_a1l, START + NG)
            pe.wait_ge(s_fhi, N_C2)
            pe.wait_ge(s_flo, N_C2)
            for t in range(STEP):
                inter(0, 0, 0, t)
            for t in range(STEP):
                hidden(0, 0, 0, t)
            for t in range(STEP):
                turn(0, t)

            def chunk(s, phase, last=False):
                for j in range(SPC):
                    n = SPC * s + j
                    wrap = (j + 1) // SPC
                    nj, nphase = (j + 1) % SPC, (phase + wrap) % BODY
                    more = not (last and wrap)
                    if more:
                        for t in range(STEP):
                            inter(n + 1, s + wrap, nj, t)
                    pe.wait_ge(s_mTs, STEP * n + STEP)
                    for o in range(KT):
                        if j == 0 and o in (0, KT // 2):
                            pe.wait_ge(s_fhi, N_W2 + PPC * s + (2 if o else 0))
                            pe.wait_ge(s_flo, N_W2 + PPC * s + (2 if o else 0))
                        if o % 2 == 0:
                            pe.wait_ge(s_oa, START + OP * n + o // 2 - 1)
                        dst = PS[:, 6 + o // 2 % 2, (o % 2) * ST:(o % 2) * ST + ST]
                        for k in range(CI):
                            r = (CI * phase + k) % RING
                            mm = mm3(dst, [w[:, r, o * P:o * P + P] for w in w2r], [msp[j % 2][:, part, k, :] for part in range(2)],
                                     k, CI)
                        if o % 2:
                            mm.then_inc(s_o, 1)
                        if more and o < STEP:
                            if wrap and o == 0:
                                pe.wait_ge(s_fhi, N_W2 + PPC * s + 14)
                                pe.wait_ge(s_flo, N_W2 + PPC * s + 14)
                            hidden(n + 1, nphase, nj, o)
                        if more and o in (4, 5):
                            turn(n + 1, o - 4)

            with pe.Fori(0, NC - BODY, BODY) as s:
                for j in range(BODY):
                    chunk(s + j, j)
            chunk(NC - 1, (NC - 1) % BODY, last=True)

        @block.scalar
        def _(act):
            act.wait_ge(s_pz, 2)
            for dst, src in small_loads:
                act.dma_start(dst, src, allow_slow_non_contiguous=True).then_inc(s_small, 16)

            def hi_piece(n):
                hi, _, _, shape, scale = pieces[n]
                act.wait_ge(s_stage[n % 2], 16 * (n // 2 + 1))
                act.activation(hi, staged(n, shape), ACT.Copy, scale=scale).then_inc(s_shi, 1)

            act.wait_ge(s_x, 16)
            act.activation(xsp[0], OUT[:, :, 0:GT], ACT.Copy).then_inc(s_xh, 1)
            hi_piece(0)
            hi_piece(1)
            act.wait_ge(s_small, 16 * NSM)
            act.wait_ge(s_pre, 1)
            act.activation(fold_rk, PS[0:RD, 0, 0:NS], ACT.Copy).then_inc(s_prev, 1)
            act.activation(MK[0:BOT, NS:2 * NS], fold_keys, ACT.Copy, scale=BOT ** -0.5).then_inc(s_prev, 1)
            act.wait_ge(s_pre, 2)
            act.activation(AV.rearrange("p a b -> p (a b)"), PS[:, 1, 0:2 * BOT], ACT.Copy).then_inc(s_prev, 1)
            act.wait_ge(s_pre, 3)
            act.activation(MK[0:BOT, 0:NS], PS[0:BOT, 2, 0:NS], ACT.Copy, scale=RD ** -0.5).then_inc(s_prev, 1)
            act.wait_ge(s_pool, POOL_HALF)
            act.activation(t_[1], t_[1], ACT.Sin, scale=TWO_PI).then_inc(s_rexp, 1)
            act.activation(t_[2], t_[2], ACT.Sin, scale=TWO_PI / 2).then_inc(s_rexp, 1)
            for n in range(2, NPC):
                hi_piece(n)

            def group(g, last=False):
                act.wait_ge(s_d, g + 1)
                act.activation(gs[:, 3, :], gs[:, 2, :], ACT.Exp).then_inc(s_ex, 1)
                act.wait_ge(s_gT, g + 1)
                act.activation(gTs, PS[:, 4, :], ACT.Copy).then_inc(s_gTs, 1)
                act.wait_ge(s_hg, g + 1)
                act.activation(hgsp[0], hg32, ACT.Copy).then_inc(s_hgh, 1)
                for o in range(KT):
                    act.wait_ge(s_base, KT * g + o + 1)
                    act.wait_ge(s_oadd, START + KT * g + o - 1)
                    act.wait_ge(s_sq, START + 2 * (KT * g + o - 1))
                    act.activation(h32[:, o % 2, :], PS[:, 2 + o % 2, :], ACT.Copy, scale=1.0 / S_W).then_inc(s_hev, 1)
                    act.wait_ge(s_hev, START + KT * g + o + 1)
                    act.activation(hsp[0][:, o, :], h32[:, o % 2, :], ACT.Copy).then_inc(s_hh, 1)
                    if o == 4:
                        act.wait_ge(s_ph, g + 1)
                        for i in range(3):
                            act.activation(ph[i], ph[i], ACT.Sin, scale=TWO_PI).then_inc(s_phd, 1)
                        for i in range(2):
                            act.activation(mg[i], mg[i], ACT.Exp).then_inc(s_phd, 1)
                if not last:
                    act.wait_ge(s_x, 16 * g + 32)
                    act.activation(xsp[0], OUT[:, :, tok(g + 1)], ACT.Copy).then_inc(s_xh, 1)
                act.wait_ge(s_q, g + 1)
                act.activation(qT[0:BOT + 1, :], PS[0:BOT + 1, 5, :], ACT.Copy).then_inc(s_qT, 1)
                for n in range(2):
                    act.wait_ge(s_u, 2 * g + n + 1)
                    act.activation(gl[:, n, :], PS[:, 6 + n, :], ACT.Gelu_apprx_tanh, bias=bu1s[:, n:n + 1]).then_inc(s_gl, 1)
                for t in range(TPG):
                    act.wait_ge(s_t, TPG * g + t + 1)
                    at = bass.ds(TPG * g + t, 1)
                    act.activation(e_all[:, at, :].rearrange("p a b -> p (a b)"), tm, ACT.Exp, bias=nm[:, t % 2:t % 2 + 1],
                                   accum_out=seall[:, at]).then_inc(s_e, 1)

            with act.Fori(0, NG - 1) as g:
                group(g)
            group(NG - 1, last=True)

            act.wait_ge(s_var, 1)
            act.activation(gate[:, 2, :], gate[:, 1, :], ACT.Ln, bias=1.0).then_inc(s_lv, 1)
            act.activation(gate[:, 4, :], st[:, 2, :], ACT.Sigmoid, bias=scal[:, 0:1]).then_inc(s_lv, 1)
            act.wait_ge(s_un, 1)
            act.activation(gate[:, 7, :], gate[:, 6, :], ACT.Sigmoid, bias=scal[:, 2:3], scale=scal[:, 1:2]).then_inc(s_sg, 1)

            with act.Fori(0, NG) as g:
                for t in range(TPG):
                    act.wait_ge(s_eT, START + TPG * g + t + 1)
                    act.wait_ge(s_z, START + g)
                    act.activation(eT[:, :, t * P:t * P + P], PS[:, t % 2, 0:2 * P].rearrange("p (n c) -> p n c", n=2),
                                   ACT.Copy).then_inc(s_eTs, 1)
                act.wait_ge(s_z, START + g + 1)
                act.activation(zT[0:BOT, :], PS[0:BOT, 4, :], ACT.Copy).then_inc(s_zTs, 1)
                for o in range(KT):
                    act.wait_ge(s_x1, START + KT * g + o + 1)
                    act.activation(fsp[0][:, o, tok(g)], OUT[:, o, tok(g)], ACT.Copy).then_inc(s_uh, 1)

            act.wait_ge(s_lenl, 48)
            act.activation(idF, id32, ACT.Copy).then_inc(s_idf, 1)
            act.activation(len_f, len_i, ACT.Copy).then_inc(s_lenf, 1)

            def piece(n, par, dst, src, scale):
                act.wait_ge(s_fst[par], 8 * (n - par) + 16)
                act.activation(dst, src, ACT.Copy, scale=scale).then_inc(s_fhi, 1)

            for n in range(N_C1):
                piece(n, n, c1s[0][:, 4 * n:4 * n + 4, :], fst[n][:, 0:4 * C1R].rearrange("p (k c) -> p k c", k=4), S_W)

            def w1_piece(q, par):
                piece(N_C1 + 2 * q + par, par, w1_flat(0)[:, bass.ds((2 * q + par) * 512, 512)], fst[par], S_W)

            def c2_piece(q, par):
                piece(N_W1 + 2 * (q - 4) + par, par, c2s[:, bass.ds((2 * (q - 4) + par) * CPC, CPC)],
                      fst[par][0:C1R, 0:CPC], S_R)

            def convolved(q, pieces_of):
                for pair in range(4):
                    act.wait_ge(s_y, START + 4 * q + pair + 1)
                    act.activation(head_of(fsp[0], q * 8 + pair * 2, 2), y32[:, pair % 2, :].rearrange("p (k c b) -> p k c b", k=KT, c=2),
                                   ACT.Copy).then_inc(s_yh, 1)
                    if pair % 2:
                        pieces_of(q, pair // 2)

            with act.Fori(0, 4) as q:
                convolved(q, w1_piece)
            with act.Fori(4, 8) as q:
                convolved(q, c2_piece)

            def first_w2(j):
                tile, half = w2_first[j]
                piece(N_C2 + j, j % 2, ring_slot(0, 2, tile * L + half * 512), fst[j % 2], S_W)

            for g in range(NG):
                act.wait_ge(s_a1, g + 1)
                act.activation(a1s[:, g * GT:g * GT + GT], PS[0:C1R, 4 + g % 2, :], ACT.Copy, scale=1.0 / S_W).then_inc(s_a1h, 1)

            def high(n, t):
                act.wait_ge(s_m, STEP * n + t + 1)
                if not first(n):
                    act.wait_ge(s_mT, STEP * n + t - 1)
                act.activation(mtok[t][:, 0, :], m32, ACT.Copy, scale=1.0 / S_W).then_inc(s_mh, 1)

            def turned(n, t, buf):
                act.wait_ge(s_mT, STEP * n + t + 1)
                if not first(n):
                    act.wait_ge(s_o, START + OP * (n - 1))
                act.activation(msp[buf][:, :, :, t * P:t * P + P],
                               PSH[:, 4 + t, :].rearrange("p (a i c) -> p a i c", a=2, i=CI), ACT.Copy).then_inc(s_mTs, 1)

            first_w2(0)
            first_w2(1)
            high(0, 0)
            first_w2(2)
            high(0, 1)
            first_w2(3)
            turned(0, 0, 0)
            first_w2(4)
            turned(0, 1, 0)
            first_w2(5)

            def chunk(s, phase, last=False):
                what = chunk_pieces(s, phase, last)

                def pieces_of(js):
                    for j in js:
                        if j >= len(what):
                            continue
                        if j == 0:
                            act.wait_ge(s_o, START + OP * SPC * s)
                        elif j == 2:
                            act.wait_ge(s_g1, NT * s + 1)
                        elif j == 10:
                            act.wait_ge(s_g1, NT * s + NT)
                        elif j == 14:
                            act.wait_ge(s_o, START + OP * (SPC * s + SPC - 1) + OP // 2)
                        ring, _, at = what[j]
                        piece(N_W2 + PPC * s + j, j % 2, ring_slot(0, ring, at), fst[j % 2], S_W)

                for j in range(SPC):
                    n = SPC * s + j
                    start, behind_high, behind_first, behind_second = AT_STEP[j]
                    pieces_of(start)
                    if last and j == SPC - 1:
                        continue
                    high(n + 1, 0)
                    high(n + 1, 1)
                    pieces_of(behind_high)
                    turned(n + 1, 0, (j + 1) % 2)
                    pieces_of(behind_first)
                    turned(n + 1, 1, (j + 1) % 2)
                    pieces_of(behind_second)

            with act.Fori(0, NC - BODY, BODY) as s:
                for j in range(BODY):
                    chunk(s + j, j)
            chunk(NC - 1, (NC - 1) % BODY, last=True)

        @block.vector
        def _(dve):
            done = [0]

            def step(ins):
                ins.then_inc(s_dve, 1)
                done[0] += 1
                dve.wait_ge(s_dve, done[0])

            dve.memset(zpad, 0.0).then_inc(s_pz, 1)
            dve.memset(Dall, 0.0).then_inc(s_pz, 1)
            dve.wait_ge(s_xh, 1)
            dve.tensor_tensor(xsp[1], OUT[:, :, 0:GT], xsp[0], ALU.subtract).then_inc(s_xl, 1)

            def lo_piece(n):
                hi, lo, _, shape, scale = pieces[n]
                dve.wait_ge(s_shi, n + 1)
                dve.scalar_tensor_tensor(out=lo, in0=staged(n, shape), scalar=scale, in1=hi, op0=ALU.mult,
                                         op1=ALU.subtract).then_inc(s_slo, 1)

            for n in range(2):
                lo_piece(n)
            dve.memset(Qsp[0][:, :, BOT:BOT + 1], 1.0).then_inc(s_dve, 1)
            dve.memset(Qsp[1][:, :, BOT:BOT + 1], 0.0).then_inc(s_one, 1)
            done[0] = 1
            dve.wait_ge(s_small, 16 * NSM)
            step(dve.tensor_copy(ids_f, ids_i))
            step(dve.tensor_tensor(b5, cst[:, C_EXP:C_EXP + NE].unsqueeze(1).broadcast_to([P, TOK // P, NE]),
                                   ids_f.unsqueeze(2).broadcast_to([P, TOK // P, NE]), ALU.is_equal))
            step(dve.tensor_scalar(b5, b5, 5.0, None, ALU.mult))
            dve.wait_ge(s_pool, POOL_DEN)
            dve.reciprocal(t_[0], t_[0]).then_inc(s_dsm, 1)
            for n in range(2, NPC):
                lo_piece(n)

            def t8(i):
                return gts[:, i, :].rearrange("p (t e) -> p t e", t=TPG)

            def wide(ap, n):
                return ap.unsqueeze(2).broadcast_to([P, TPG, n])

            def row(ap):
                return ap.unsqueeze(1).broadcast_to([P, TPG, NE])

            iota = cst[:, C_EXP:C_EXP + NE]

            def group(g, last=False):
                dve.wait_ge(s_lg, g + 1)
                Lg = t8(0)
                step(dve.scalar_tensor_tensor(out=Lg, in0=PS[:, 0, 0:TPG * NE].rearrange("p (t e) -> p t e", t=TPG),
                                              scalar=1.0 / S_R, in1=b5[:, TPG * g:TPG * g + TPG, :], op0=ALU.mult, op1=ALU.add))
                for i in range(2):
                    eq, cand, one = t8(1), t8(2), t8(3 + i)
                    top, first = gs[:, i, :], gs[:, 5, :]
                    step(dve.tensor_reduce(top, Lg, AX_X, ALU.max))
                    step(dve.tensor_tensor(eq, Lg, wide(top, NE), ALU.is_equal))
                    step(dve.scalar_tensor_tensor(out=cand, in0=eq, scalar=-100.0, in1=row(iota), op0=ALU.mult, op1=ALU.add))
                    step(dve.tensor_reduce(first, cand, AX_X, ALU.min))
                    step(dve.tensor_tensor(one, cand, wide(first, NE), ALU.is_equal))
                    if i == 0:
                        step(dve.scalar_tensor_tensor(out=t8(5), in0=one, scalar=-BIG, in1=Lg, op0=ALU.mult, op1=ALU.add))
                        Lg = t8(5)
                dve.tensor_tensor(gs[:, 2, :], gs[:, 1, :], gs[:, 0, :], ALU.subtract).then_inc(s_d, 1)
                dve.wait_ge(s_ex, g + 1)
                step(dve.tensor_scalar(gs[:, 4, :], gs[:, 3, :], 1.0, None, ALU.add))
                step(dve.reciprocal(gs[:, 0, :], gs[:, 4, :]))
                step(dve.tensor_tensor(gs[:, 1, :], gs[:, 0, :], gs[:, 3, :], ALU.mult))
                step(dve.tensor_tensor(t8(1), t8(3), wide(gs[:, 0, :], NE), ALU.mult))
                step(dve.tensor_tensor(t8(2), t8(4), wide(gs[:, 1, :], NE), ALU.mult))
                step(dve.tensor_tensor(gts[:, 6, :], gts[:, 1, :], gts[:, 2, :], ALU.add))
                dve.tensor_copy(Gx.rearrange("p (e r) -> p e r", r=RK),
                                gts[:, 6, :].unsqueeze(2).broadcast_to([P, TPG * NE, RK])).then_inc(s_gx, 1)
                dve.wait_ge(s_gTs, g + 1)
                dve.wait_ge(s_ha, g + 1)
                dve.scalar_tensor_tensor(out=hg32, in0=PS[:, 1, :], scalar=2.0 / S_W, in1=gTs, op0=ALU.mult,
                                         op1=ALU.mult).then_inc(s_hg, 1)
                dve.wait_ge(s_hgh, g + 1)
                dve.wait_ge(s_hg, g + 1)
                dve.tensor_tensor(hgsp[1], hg32, hgsp[0], ALU.subtract).then_inc(s_hgl, 1)
                for o in range(KT):
                    dve.wait_ge(s_hh, KT * g + o + 1)
                    dve.tensor_tensor(hsp[1][:, o, :], h32[:, o % 2, :], hsp[0][:, o, :], ALU.subtract).then_inc(s_hl, 1)
                    dve.tensor_tensor(OUT[:, o, tok(g)], OUT[:, o, tok(g)], h32[:, o % 2, :], ALU.add).then_inc(s_oadd, 1)
                if not last:
                    dve.wait_ge(s_xh, g + 2)
                    dve.tensor_tensor(xsp[1], OUT[:, :, tok(g + 1)], xsp[0], ALU.subtract).then_inc(s_xl, 1)
                for t in range(TPG):
                    dve.wait_ge(s_sc, TPG * g + t + 1)
                    dve.tensor_tensor(SA.rearrange("p (a n) -> p a n", a=2), PS[:, 1 + 3 * (t % 2), :].rearrange("p (a n) -> p a n", a=2),
                                      lrel.unsqueeze(1).broadcast_to([P, 2, NS]), ALU.add).then_inc(s_scr, 1)
                    dve.wait_ge(s_scr, START + TPG * g + t + 1)
                    step(dve.max(v8, SA[:, 0:NS]))
                    dve.wait_ge(s_e, START + TPG * g + t)
                    step(dve.match_replace(tm, v8, SA[:, 0:NS], -3.0e38))
                    step(dve.tensor_tensor(tm, tm, SA[:, 0:NS], ALU.is_equal))
                    step(dve.scalar_tensor_tensor(out=tm, in0=tm, scalar=-BIG, in1=SA[:, NS:2 * NS], op0=ALU.mult, op1=ALU.add))
                    dve.tensor_reduce(nm[:, t % 2:t % 2 + 1], tm, AX_X, ALU.max, negate=True).then_inc(s_t, 1)
                dve.wait_ge(s_k, g + 1)
                dve.wait_ge(s_kst, KST_FIRST + g * KST_GROUP)
                step(dve.tensor_scalar(kf, PS[0:TA, 5, :].rearrange("p (h b) -> p h b", h=HPG), 2.0 * S_W, None, ALU.mult))
                step(dve.scalar_tensor_tensor(out=kf[:, :, TB - 1], in0=Dall[:, bass.ds(g * HPG, HPG)], scalar=S_W,
                                              in1=kf[:, :, TB - 1], op0=ALU.mult, op1=ALU.add))
                dve.tensor_copy(ksp[0], kf).then_inc(s_kc, 1)
                dve.wait_ge(s_kc, START + 2 * g + 1)
                dve.tensor_tensor(ksp[1], kf, ksp[0], ALU.subtract).then_inc(s_kc, 1)
                dve.wait_ge(s_st, g + 1)
                dve.tensor_copy(st[:, :, bass.ds(TPG * g, TPG)], PS[:, 0, 64:64 + 3 * TPG].rearrange("p (a t) -> p a t", a=3))\
                   .then_inc(s_str, 1)

            for g in range(NG):
                group(g, last=(g == NG - 1))

            dve.wait_ge(s_str, START + NG)
            dve.wait_ge(s_sq, START + 2 * KT * NG)
            step(dve.memset(ones, 1.0))
            step(dve.tensor_scalar(gate[:, 0, :], st[:, 0, :], 1.0 / L, None, ALU.mult))
            step(dve.tensor_tensor(gate[:, 1, :], gate[:, 0, :], gate[:, 0, :], ALU.mult))
            dve.scalar_tensor_tensor(out=gate[:, 1, :], in0=st[:, 1, :], scalar=1.0 / L, in1=gate[:, 1, :], op0=ALU.mult,
                                     op1=ALU.subtract).then_inc(s_var, 1)
            dve.wait_ge(s_lv, 2)
            dve.tensor_reduce(gate[:, 3, 0:1], gate[:, 2, :], AX_X, ALU.add).then_inc(s_lvs, 1)
            dve.wait_ge(s_gsum, 1)
            step(dve.tensor_scalar(gate[:, 3, 1:2], PS[:, 0, 0:1], 1.0 / TOK, 1e-6, ALU.mult, ALU.add))
            step(dve.reciprocal(gate[:, 3, 2:3], gate[:, 3, 1:2]))
            step(dve.tensor_scalar(gate[:, 5, :], gate[:, 2, :], gate[:, 3, 2:3], 0.5, ALU.mult, ALU.mult))
            step(dve.scalar_tensor_tensor(out=gate[:, 5, :], in0=gate[:, 4, :], scalar=2.5, in1=gate[:, 5, :], op0=ALU.mult, op1=ALU.add))
            step(dve.tensor_scalar(gate[:, 5, :], gate[:, 5, :], 0.0, 5.0, ALU.max, ALU.min))
            step(dve.tensor_scalar(gate[:, 6, :], gate[:, 5, :], -0.5, 1.0 / 1.5, ALU.add, ALU.mult))
            dve.tensor_scalar(gate[:, 6, :], gate[:, 6, :], 0.0, 1.0, ALU.max, ALU.min).then_inc(s_un, 1)
            dve.wait_ge(s_sg, 1)
            step(dve.tensor_scalar(gate[:, 8, :], gate[:, 7, :], 0.05, None, ALU.is_ge))
            step(dve.tensor_tensor(gate[:, 8, :], gate[:, 8, :], gate[:, 7, :], ALU.mult))
            dve.wait_ge(s_e, START + NG * TPG)
            step(dve.reciprocal(gate[:, 9, :], seall))
            dve.tensor_tensor(gate[:, 10, :], gate[:, 8, :], gate[:, 9, :], ALU.mult).then_inc(s_gate, 1)
            dve.wait_ge(s_gate, 1)

            with dve.Fori(0, NG) as g:
                for t in range(TPG):
                    dve.wait_ge(s_eT, START + TPG * g + t - 1)
                    at = bass.ds(TPG * g + t, 1)
                    dve.tensor_scalar(eg[:, t % 2, :], e_all[:, at, :].rearrange("p a b -> p (a b)"), gate[:, 10, at], None,
                                      ALU.mult).then_inc(s_eg, 1)
                for o in range(KT):
                    dve.wait_ge(s_aux, KT * g + o + 1)
                    dve.tensor_tensor(OUT[:, o, tok(g)], OUT[:, o, tok(g)], PS[:, 6 + o % 2, :], ALU.add).then_inc(s_x1, 1)
                    if o % 2 == 0:
                        dve.wait_ge(s_uh, KT * g + o + 1)
                        dve.tensor_tensor(fsp[1][:, o, tok(g)], OUT[:, o, tok(g)], fsp[0][:, o, tok(g)], ALU.subtract)\
                           .then_inc(s_ul, 1)

            dve.wait_ge(s_lenf, 1)
            dve.wait_ge(s_aux, KT * NG)
            for k in range(KT):
                for c in range(2):
                    ins = dve.tensor_scalar(ymask[:, k, c * B:c * B + B], len_f, posF[:, k:k + 1], 1.0 / S_W, ALU.is_gt, ALU.mult)
            ins.then_inc(s_ym, 1)
            step(dve.tensor_reduce(nkf[:, 0, :], len_f.rearrange("p (t c) -> p t c", c=BPT), AX_X, ALU.max))
            step(dve.tensor_scalar(nkf[:, 1, :], nkf[:, 0, :], 1.0 / P, (P - 1.0) / P - 0.5 + 0.5 / P, ALU.mult, ALU.add))
            step(dve.tensor_scalar(nkf[:, 1, :], nkf[:, 1, :], 2.0, float(KT), ALU.max, ALU.min))
            step(dve.tensor_scalar(nkf[:, 0, :], nkf[:, 1, :], MAGIC, -MAGIC, ALU.add, ALU.add))
            dve.tensor_copy(nk_i, nkf[:, 0, :]).then_inc(s_nk, 1)
            dve.wait_ge(s_ym, 1)

            def piece(n, lo, src, hi, scale):
                dve.wait_ge(s_fhi, n + 1)
                dve.scalar_tensor_tensor(out=lo, in0=src, scalar=scale, in1=hi, op0=ALU.mult, op1=ALU.subtract).then_inc(s_flo, 1)

            for n in range(N_C1):
                c = [x[:, 4 * n:4 * n + 4, :] for x in c1s]
                piece(n, c[1], fst[n][:, 0:4 * C1R].rearrange("p (k c) -> p k c", k=4), c[0], S_W)

            def w1_piece(q, par):
                c = [w1_flat(part)[:, bass.ds((2 * q + par) * 512, 512)] for part in range(2)]
                piece(N_C1 + 2 * q + par, c[1], fst[par], c[0], S_W)

            def c2_piece(q, par):
                c = c2s[RB:RB + RANK, bass.ds((2 * (q - 4) + par) * CPC, CPC)]
                piece(N_W1 + 2 * (q - 4) + par, c, fst[par][RB:RB + RANK, 0:CPC], c, S_R)

            def convolved(q, pieces_of):
                def mask(pair):
                    dve.wait_ge(s_cv, 8 * q + 2 * pair + 2)
                    dve.wait_ge(s_yh, START + 4 * q + pair - 1)
                    dve.wait_ge(s_yl, START + 4 * q + pair - 1)
                    dve.tensor_tensor(y32[:, pair % 2, :], PS[:, pair, :], ymask.rearrange("p k c -> p (k c)"), ALU.mult)\
                       .then_inc(s_y, 1)

                def low(pair):
                    dve.wait_ge(s_yh, START + 4 * q + pair + 1)
                    c = [head_of(x, q * 8 + pair * 2, 2) for x in fsp]
                    dve.tensor_tensor(c[1], y32[:, pair % 2, :].rearrange("p (k c b) -> p k c b", k=KT, c=2), c[0], ALU.subtract)\
                       .then_inc(s_yl, 1)
                    if pair % 2:
                        pieces_of(q, pair // 2)

                mask(0)
                mask(1)
                low(0)
                mask(2)
                low(1)
                mask(3)
                low(2)
                low(3)

            with dve.Fori(0, 4) as q:
                convolved(q, w1_piece)
            with dve.Fori(4, 8) as q:
                convolved(q, c2_piece)

            def first_w2(j):
                tile, half = w2_first[j]
                hi, lo = [ring_slot(part, 2, tile * L + half * 512) for part in range(2)]
                piece(N_C2 + j, lo, fst[j % 2], hi, S_W)

            for g in range(NG):
                dve.wait_ge(s_a1h, g + 1)
                c = a1s[2 * RB:2 * RB + RANK, g * GT:g * GT + GT]
                dve.scalar_tensor_tensor(out=c, in0=PS[2 * RB:2 * RB + RANK, 4 + g % 2, :], scalar=1.0 / S_W, in1=c,
                                         op0=ALU.mult, op1=ALU.subtract).then_inc(s_a1l, 1)

            def mask(n, t):
                sc = PS[:, t, :].rearrange("p (k i) -> p k i", i=BLK)
                dve.wait_ge(s_in, STEP * n + t + 1)
                if not first(n) or t:
                    dve.wait_ge(s_mk, STEP * n + t)
                dve.tensor_reduce(bm, sc, AX_X, ALU.max).then_inc(s_bm, 1)
                dve.wait_ge(s_bm, STEP * n + t + 1)
                if not first(n):
                    dve.wait_ge(s_m, STEP * n + t - 1)
                dve.tensor_tensor(mk[:, t, :].rearrange("p (k i) -> p k i", i=BLK), sc,
                                  bm.unsqueeze(2).broadcast_to([P, CI * P // BLK, BLK]), ALU.is_equal).then_inc(s_mk, 1)

            def masked(n, t):
                dve.wait_ge(s_mk, STEP * n + t + 1)
                dve.wait_ge(s_g1, STEP * n + t + 1)
                if not first(n) or t:
                    dve.wait_ge(s_ml, STEP * n + t)
                dve.scalar_tensor_tensor(out=m32, in0=PS[:, 2 + t, :], scalar=0.0, in1=mk[:, t, :], op0=ALU.max,
                                         op1=ALU.mult).then_inc(s_m, 1)

            def low(n, t):
                dve.wait_ge(s_mh, STEP * n + t + 1)
                dve.scalar_tensor_tensor(out=mtok[t][:, 1, :], in0=m32, scalar=1.0 / S_W, in1=mtok[t][:, 0, :], op0=ALU.mult,
                                         op1=ALU.subtract).then_inc(s_ml, 1)

            mask(0, 0)
            mask(0, 1)
            first_w2(0)
            first_w2(1)
            masked(0, 0)
            low(0, 0)
            first_w2(2)
            masked(0, 1)
            low(0, 1)
            for j in range(3, 6):
                first_w2(j)

            def chunk(s, phase, last=False):
                what = chunk_pieces(s, phase, last)

                def pieces_of(js):
                    for j in js:
                        if j < len(what):
                            ring, _, at = what[j]
                            hi, lo = [ring_slot(part, ring, at) for part in range(2)]
                            piece(N_W2 + PPC * s + j, lo, fst[j % 2], hi, S_W)

                for j in range(SPC):
                    n = SPC * s + j
                    start, behind_high, behind_first, behind_second = AT_STEP[j]
                    more = not (last and j == SPC - 1)

                    def add(a):
                        dve.wait_ge(s_o, START + OP * n + a + 1)
                        c = OUT[:, 2 * a:2 * a + 2, j * ST:j * ST + ST]
                        dve.scalar_tensor_tensor(out=c, in0=PS[:, 6 + a % 2, :].rearrange("p (o t) -> p o t", o=2),
                                                 scalar=1.0 / S_W, in1=c, op0=ALU.mult, op1=ALU.add).then_inc(s_oa, 1)

                    if more:
                        mask(n + 1, 0)
                    pieces_of(start)
                    if more:
                        mask(n + 1, 1)
                        masked(n + 1, 0)
                    add(0)
                    if more:
                        low(n + 1, 0)
                        masked(n + 1, 1)
                        low(n + 1, 1)
                    add(1)
                    pieces_of(behind_high)
                    pieces_of(behind_first)
                    add(2)
                    pieces_of(behind_second)
                    add(3)

            with dve.Fori(0, NC - BODY, BODY) as s:
                for j in range(BODY):
                    chunk(s + j, j)
            chunk(NC - 1, (NC - 1) % BODY, last=True)

        @block.gpsimd
        def _(pool):
            done = [0]

            def step(ins):
                ins.then_inc(s_pool, 1)
                done[0] += 1
                pool.wait_ge(s_pool, done[0])

            def tt(out_, a_, b_, op):
                step(pool.tensor_tensor(out_, a_, b_, op))

            def ts(out_, a_, x, y, o0, o1):
                step(pool.tensor_scalar(out_, a_, x, y, o0, o1))

            def fraction(out_, a_, tmp):
                ts(tmp, a_, MAGIC, -MAGIC, ALU.add, ALU.add)
                tt(out_, a_, tmp, ALU.subtract)

            for one in from_start:
                pool.sem_inc(one, START)

            pool.wait_ge(s_small, 16 * NSM)
            k2, r2, p2, e2 = (small[:, 11 + 2 * i:13 + 2 * i, :] for i in range(4))
            ts(logs, logs, -87.0, 88.0, ALU.max, ALU.min)
            ts(k2, logs, float(np.log2(np.e)), MAGIC, ALU.mult, ALU.add)
            ts(k2, k2, -MAGIC, 0.0, ALU.add, ALU.add)
            ts(r2, k2, -LN2_HI, 0.0, ALU.mult, ALU.add)
            tt(r2, logs, r2, ALU.add)
            ts(p2, k2, -LN2_LO, 0.0, ALU.mult, ALU.add)
            tt(r2, r2, p2, ALU.add)
            ts(p2, r2, 1.0 / 8, 1.0, ALU.mult, ALU.add)
            for i in range(7, 0, -1):
                tt(p2, p2, r2, ALU.mult)
                ts(p2, p2, 1.0 / i, 1.0, ALU.mult, ALU.add)
            ts(e2.bitcast(I32), k2, 127.0, float(2 ** 23), ALU.add, ALU.mult)
            tt(exps, p2, e2, ALU.mult)
            are, den, sn, sh, em = are_s, t_[0], t_[1], t_[2], t_[3]
            tt(R_s, are, dt_s, ALU.mult)
            ts(R_s, R_s, -1.0, 0.0, ALU.mult, ALU.add)
            tt(th_s, aim_s, dt_s, ALU.mult)
            ts(th_s, th_s, 1.0 / (2.0 * np.pi), 0.0, ALU.mult, ALU.add)
            tt(t_[4], are, are, ALU.mult)
            tt(t_[5], aim_s, aim_s, ALU.mult)
            tt(den, t_[4], t_[5], ALU.add)
            assert done[0] == POOL_DEN
            fraction(sn, th_s, t_[4])
            ts(sh, sn, 1.0, 0.0, ALU.mult, ALU.add)
            assert done[0] == POOL_HALF
            ts(em, R_s, 1.0 / 9, 1.0, ALU.mult, ALU.add)
            for i in range(8, 1, -1):
                tt(em, em, R_s, ALU.mult)
                ts(em, em, 1.0 / i, 1.0, ALU.mult, ALU.add)
            tt(em, em, R_s, ALU.mult)
            pool.wait_ge(s_rexp, 2)
            c1m, er, ei, u, v = t_[4], t_[5], t_[6], t_[7], t_[8]
            tt(c1m, sh, sh, ALU.mult)
            ts(c1m, c1m, -2.0, 0.0, ALU.mult, ALU.add)
            tt(er, em, c1m, ALU.mult)
            tt(er, er, em, ALU.add)
            tt(er, er, c1m, ALU.add)
            tt(ei, em, sn, ALU.mult)
            tt(ei, ei, sn, ALU.add)
            tt(u, cr_s, er, ALU.mult)
            tt(v, ci_s, ei, ALU.mult)
            tt(u, u, v, ALU.subtract)
            tt(v, cr_s, ei, ALU.mult)
            tt(s1_s, ci_s, er, ALU.mult)
            tt(v, v, s1_s, ALU.add)
            pool.wait_ge(s_dsm, 1)
            tt(s1_s, v, aim_s, ALU.mult)
            tt(s2_s, u, are, ALU.mult)
            tt(s1_s, s1_s, s2_s, ALU.subtract)
            tt(s1_s, s1_s, den, ALU.mult)
            tt(s2_s, u, aim_s, ALU.mult)
            tt(v, v, are, ALU.mult)
            tt(s2_s, s2_s, v, ALU.add)
            tt(s2_s, s2_s, den, ALU.mult)
            ts(s1_s, s1_s, cst[:, C_SGN:C_SGN + 1], 0.0, ALU.mult, ALU.add)

            def group(g):
                hs = bass.ds(g * HPG, HPG)

                def head(x):
                    return x[:, hs].unsqueeze(2).broadcast_to([P, HPG, TB])

                def ramp(at):
                    return cst[:, at:at + TB].unsqueeze(1).broadcast_to([P, HPG, TB])

                E2, EA, EB = ph
                tt(E2, head(th_s), ramp(C_TB), ALU.mult)
                ts(E2, E2, cst[:, C_PHA:C_PHA + 1], 0.0, ALU.add, ALU.add)
                fraction(E2, E2, mg[0])
                tt(EA, head(th_s), ramp(C_TA), ALU.mult)
                ts(EB, EA, cst[:, C_PHB:C_PHB + 1], 0.0, ALU.add, ALU.add)
                ts(EA, EA, cst[:, C_PHA:C_PHA + 1], 0.0, ALU.add, ALU.add)
                fraction(EB, EB, mg[0])
                fraction(EA, EA, mg[0])
                tt(mg[1], head(R_s), ramp(C_TA), ALU.mult)
                pool.tensor_tensor(mg[0], head(R_s), ramp(C_TB), ALU.mult).then_inc(s_ph, 1)
                for o in range(KT):
                    pool.wait_ge(s_hev, START + KT * g + o + 1)
                    pool.wait_ge(s_sq, START + 2 * (KT * g + o))
                    if o == 0:
                        pool.wait_ge(s_st, g)
                        pool.tensor_tensor(acc, h32[:, 0, :], h32[:, 0, :], ALU.mult).then_inc(s_sq, 2)
                        continue
                    pool.tensor_tensor(sq, h32[:, o % 2, :], h32[:, o % 2, :], ALU.mult).then_inc(s_sq, 1)
                    pool.wait_ge(s_sq, START + 2 * (KT * g + o) + 1)
                    pool.tensor_tensor(acc, acc, sq, ALU.add).then_inc(s_sq, 1)
                pool.wait_ge(s_phd, 5 * g + 5)
                tt(E2, E2, mg[0], ALU.mult)
                tt(EA, EA, mg[1], ALU.mult)
                tt(EB, EB, mg[1], ALU.mult)
                tt(EA, EA, head(s1_s), ALU.mult)
                tt(EB, EB, head(s2_s), ALU.mult)
                pool.tensor_tensor(EA, EA, EB, ALU.add).then_inc(s_L, 1)
                pool.wait_ge(s_k, g + 1)

            for g in range(NG):
                group(g)

            for g in range(NG):
                for o in range(1, KT, 2):
                    pool.wait_ge(s_uh, KT * g + o + 1)
                    pool.tensor_tensor(fsp[1][:, o, tok(g)], OUT[:, o, tok(g)], fsp[0][:, o, tok(g)], ALU.subtract)\
                        .then_inc(s_ulp, 1)


def kernel(**inputs):
    import concourse.bacc as _bacc
    from concourse.bass_utils import run_bass_kernel_spmd as _run

    v = {k: np.asarray(a) for k, a in inputs.items()}

    def turned(w):
        return w.reshape(-1, KT, P)[:, :, ::-1].reshape(-1, L)

    bands = np.zeros((L, C1R), np.float32)
    bands2 = np.zeros((C1R, INTER), np.float32)
    for i in range(3):
        bands[:, RB * i:RB * i + RANK] = turned(v["L1_ffn_c1_w"]).T
        bands2[RB * i:RB * i + RANK] = v["L1_ffn_c2_w"].T
    Cm = v["L1_cond_C"]
    arrays = {
        "xT": v["x"].transpose(2, 0, 1).reshape(L, TOK),
        "WT": v["L0_cond_W"].T,
        "WrT": v["L0_cond_Wr"].T,
        "AT": v["L0_cond_A"].reshape(NE * RK, L).T,
        "BT": v["L0_cond_B"].transpose(0, 2, 1).reshape(NE * RK, L),
        "WqT": v["L0_ffn_Wq"].T,
        "Wr": v["L0_ffn_Wr"],
        "Wr2T": v["L0_ffn_Wr"].T,
        "keysT": v["L0_ffn_aux_keys"].T,
        "valuesT": v["L0_ffn_aux_values"].T,
        "WvdT": v["L0_ffn_Wvd"].T,
        "WvuT": v["L0_ffn_Wvu"].T,
        "Wu1T": v["L0_ffn_Wu1"].T,
        "bu1": v["L0_ffn_bu1"].reshape(2, P).T,
        "Wu2": v["L0_ffn_Wu2"].reshape(2, P).T,
        "bu2": v["L0_ffn_bu2"].reshape(1),
        "gate_w1": v["L0_ffn_gate_w1"].reshape(1),
        "gate_bias": v["L0_ffn_gate_bias"].reshape(1),
        "log_rel": v["L0_ffn_log_rel"],
        "log_dt": v["L1_cond_log_dt"],
        "Cri": Cm.transpose(2, 1, 0),
        "lar": v["L1_cond_log_A_real"].T,
        "aim": v["L1_cond_A_imag"].T,
        "Dh": v["L1_cond_D"].reshape(1, H),
        "c1P": bands,
        "c2T": bands2,
        "w1L": turned(v["L1_ffn_w1"]).reshape(IT // 2, PAIR, KT, P).transpose(0, 3, 2, 1).reshape(IT // 2, P, KT * PAIR),
        "w2": v["L1_ffn_w2t"],
        "ids": v["itok_B_0_7"],
        "lens": v["itok_B_78_3631"],
        "consts": shape_constants(),
    }
    nc = _bacc.Bacc("TRN2", target_bir_lowering=False, num_devices=1)
    given, args = {}, []
    for name, a in arrays.items():
        a = np.ascontiguousarray(a)
        given[f"in_{name}"] = a
        args.append(nc.dram_tensor(f"in_{name}", a.shape, mybir.dt.from_np(a.dtype), kind="ExternalInput").ap())
    args.append(nc.dram_tensor("out_0", (L, TOK), F32, kind="ExternalOutput").ap())
    build(nc, *args)
    r = _run(nc, [given], core_ids=[0])
    return np.ascontiguousarray(r.results[0]["out_0"].reshape(L, B, H).transpose(1, 2, 0))
```

```python
from contextlib import ExitStack

import numpy as np

import concourse.bass as bass
from concourse import mybir

F32 = mybir.dt.float32
F16 = mybir.dt.float16
I32 = mybir.dt.int32
ALU = mybir.AluOpType
ACT = mybir.ActivationFunctionType
AX_X = mybir.AxisListType.X

P = 128
B, H, L = 32, 64, 1024
TOK = B * H
KT = L // P
GT = 512
NG = TOK // GT
TPG = GT // P
BPT = P // H
BPG = GT // H
HPG = H // NG
NE, RK = 8, 16
BOT, RD, NS = 64, 48, 256
UH = 256
SN = 64
TA, TB = 32, 32
RANK, INTER, BLK = 16, 3584, 64
IT = INTER // P
CI = 4
NC = IT // CI
RING = 6
BODY = 3
PAIR = 2 * P
STEP = 2
NT = TOK // P
SPC = NT // STEP
ST = STEP * P
OP = KT // 2
KROWS = L + P
RB = 32
C1R = 80

S_W = 64.0
S_R = 16.0
TWO_PI = 6.283185
LN2_HI, LN2_LO = 0.693359375, -2.12194440e-4
MAGIC = 12582912.0
BIG = 1.0e30

C_TB, C_TA, C_POS, C_EXP, C_PHA, C_PHB, C_SGN, C_ONE, C_E64, C_ID = 0, 32, 64, 72, 80, 81, 82, 83, 84, 85
C_N = C_ID + P
K_REL = C_N
K_SCAL = K_REL + NS
K_BU1, K_WU2 = K_SCAL + 3, K_SCAL + 5
K_MODE = K_WU2 + 2
K_N = K_MODE + 5 * H


def shape_constants():
    c = np.zeros((P, C_N), np.float32)
    c[:, C_TB:C_TB + TB] = np.arange(TB)[::-1]
    c[:, C_TA:C_TA + TA] = TB * np.arange(TA)[::-1]
    c[:, C_POS:C_POS + KT] = np.arange(KT)[None] * P + np.arange(P)[::-1, None]
    c[:, C_EXP:C_EXP + NE] = np.arange(NE)
    c[:SN, C_PHA] = 0.25
    c[SN:, C_PHB] = 0.25
    c[:SN, C_SGN] = 1.0
    c[SN:, C_SGN] = -1.0
    c[:, C_ONE] = 1.0
    c[64, C_E64] = 1.0
    c[:, C_ID:] = np.eye(P)
    return c


class Arena:

    def __init__(self, region, words):
        self.region, self.words, self.at = region, words, 0

    def take(self, shape, dt=F32, parts=P):
        n = int(np.prod(shape))
        words = n if dt != F16 else (n + 1) // 2
        words = (words + 7) // 8 * 8
        ap = self.region[0:parts, self.at:self.at + words]
        if dt != F32:
            ap = ap.bitcast(dt)
        ap = ap[:, 0:n]
        self.at += words
        assert self.at <= self.words, (self.at, self.words)
        if len(shape) == 2:
            ap = ap.rearrange("p (a b) -> p a b", a=shape[0])
        elif len(shape) == 3:
            ap = ap.rearrange("p (a b c) -> p a b c", a=shape[0], b=shape[1])
        return ap


def build(nc, xB, WT, WrT, AT, BT, WqT, Wr, Wr2T, keysT, valuesT, WvdT, WvuT, Wu1T, packed, Dh, c1P, c2T, w1L, w2, ids,
          lens, out):
    with ExitStack() as ctx:
        def sem(name):
            return ctx.enter_context(nc.semaphore(name))

        OUT = ctx.enter_context(nc.sbuf_tensor("OUT", [P, B, KT, H], F32))
        OUTF = OUT[:, :, :, :].rearrange("p b k h -> p (b k h)")
        OUTV = OUT[:, :, :, :].rearrange("p b k h -> p k b h")
        XF = ctx.enter_context(nc.sbuf_tensor("XF", [P, KT * TOK], F32))
        WORDS = 20440
        AR = ctx.enter_context(nc.sbuf_tensor("AR", [P, WORDS], F32))
        PS = ctx.enter_context(nc.psum_tensor("PS", [P, 8, 512], F32))
        PSH = PS[:, :, :].bitcast(F16)
        kp = nc.dram_tensor("taps", (2, H, KROWS), F16).ap()

        xr = Arena(XF, KT * TOK)
        Wsp = [xr.take([KT, L], F16) for _ in range(2)]
        xsp = [xr.take([KT, GT], F16) for _ in range(2)]
        hsp = [xr.take([KT, GT], F16) for _ in range(2)]
        assert xr.at == KT * TOK
        xr = Arena(XF, KT * TOK)
        fsp = [xr.take([KT, TOK], F16) for _ in range(2)]

        perm_i = AR[:, WORDS - B:WORDS].bitcast(I32)
        len_s = AR[:, WORDS - 2 * B:WORDS - B]

        a = Arena(AR, WORDS - 2 * B)
        cst = a.take([K_N])
        lrel = cst[:, K_REL:K_REL + NS]
        scal, bu1s, wu2s = cst[:, K_SCAL:K_SCAL + 3], cst[:, K_BU1:K_BU1 + 2], cst[:, K_WU2:K_WU2 + 2]
        stage = [a.take([L]) for _ in range(4)]
        e_g = stage[0].rearrange("p (t n) -> p t n", t=TPG)
        eT = stage[1].rearrange("p (n t) -> p n t", n=2)
        z_at = a.at - 2 * L
        z_all = AR[:, z_at:z_at + TOK]
        zsp = stage[0].bitcast(F16).rearrange("p (g t) -> p g t", g=NG)
        u1_at = a.at
        U1 = [a.take([KT, UH], F16) for _ in range(2)]
        Asp = [a.take([KT, P], F16) for _ in range(2)]
        Bsp = [a.take([L], F16) for _ in range(2)]
        Qsp = [a.take([KT, BOT + 1], F16) for _ in range(2)]
        Rsp = [a.take([KT, NE], F16) for _ in range(2)]
        h32 = a.take([2, GT])
        sq = a.take([GT])
        acc = a.take([GT])
        ones = sq[:, 0:P]
        gl = a.take([2, GT])
        Gx, gTs = gl[:, 0, :], gl[:, 1, :]
        hg32 = a.take([GT])
        kf = hg32[0:TA, :].rearrange("p (h b) -> p h b", h=HPG)
        hgsp = [a.take([GT], F16) for _ in range(2)]
        ksp = [a.take([HPG, TB], F16, TA) for _ in range(2)]
        qT = a.take([GT])
        MK = a.take([2 * NS])
        AV = a.take([2, 2 * BOT])
        SA = a.take([2 * NS])
        tm = a.take([NS])
        ph = [a.take([HPG, TB]) for _ in range(3)]
        mg = [a.take([HPG, TB]) for _ in range(2)]
        small = a.take([15, H])
        gts = a.take([7, TPG * NE])
        gs = a.take([6, TPG])
        st = a.take([3, NT])
        seall = a.take([NT])
        nm = a.take([2])
        v8 = a.take([8])
        gate = a.take([12, NT])
        b5 = gate[:, 0:NE, :].rearrange("p a b -> p (a b)").rearrange("p (t e) -> p t e", t=NT)
        zpad = gate[:, NE:12, :].rearrange("p a b -> p (a b)").bitcast(F16)
        ids_f = tm[:, NT:2 * NT]
        nkf = tm[:, 6 * NT:8 * NT].rearrange("p (a t) -> p a t", a=2)
        nk_i = tm[:, 8 * NT:9 * NT].bitcast(I32)
        row_i = tm[0:B, 160:160 + B + 2].bitcast(I32)
        row_f = sq[0:B, 0:B + 2]
        row_key, own_key = sq[0:B, 40:40 + B], sq[0:B, 72:73]
        longer, at_place = sq[0:B, 80:80 + B], sq[0:B, 112:112 + B]
        rank = sq[0:B, 73:74]
        spread = acc[0:B, 0:3 * P].rearrange("p (a c) -> p a c", a=3)
        Dall = a.take([H], F32, TA)
        c = Arena(AR, WORDS)
        c.at = u1_at
        wvu32 = c.take([L])
        wvu = [c.take([L], F16) for _ in range(2)]

        ident = cst[:, C_ID:C_ID + P]
        diag = [x.rearrange("p (t c) -> p t c", t=TPG) for x in (gl[:, 0, :], gl[:, 1, :], MK, SA)]
        modes = cst[:, K_MODE:K_N].rearrange("p (a h) -> p a h", a=5)
        logs, exps = modes[:, 0:2, :], small[:, 0:2, :]
        dt_s, are_s = exps[:, 0, :], exps[:, 1, :]
        aim_s, cr_s, ci_s = (modes[:, i, :] for i in range(2, 5))
        R_s, th_s, s1_s, s2_s = (small[:, i, :] for i in range(2, 6))
        t_ = [small[:, 6 + i, :] for i in range(9)]

        f = Arena(AR, WORDS - 2 * B)
        w1r = [f.take([RING // 2, KT, PAIR], F16) for _ in range(2)]
        w2_at = f.at
        w2r = [f.take([RING, L], F16) for _ in range(2)]
        m_at = f.at
        msp = [f.take([2, CI, ST], F16) for _ in range(2)]
        a1s = f.take([TOK], F16, C1R)
        c2s = f.take([INTER], F16, C1R)
        mk_at = f.at
        mtok = [f.take([2, CI * P], F16) for _ in range(2)]
        mk = f.take([2, CI * P], F16)
        fst = [f.take([512]) for _ in range(2)]
        m32 = f.take([CI * P])
        bm = f.take([BLK // 8])
        idF = f.take([P], F16)
        f2 = Arena(AR, WORDS)
        f2.at = w2_at
        toep = [f2.take([2, L], F16) for _ in range(4)]
        id32 = f2.take([P])
        posF = f2.take([KT])
        f2.at = w2_at + (RING + RING - 2) * L // 2
        c1s = [f2.take([KT, C1R], F16) for _ in range(2)]
        assert f2.at <= m_at
        f2.at = m_at
        y32 = f2.take([2, KT * 2 * B])
        f2.at = mk_at
        ymask = f2.take([KT, 2 * B])

        s_x = sem("x_loaded")
        s_key = sem("batch_places_made")
        s_sort = sem("batches_ordered")
        s_perm = sem("order_in_sbuf")
        s_stage = [sem(f"stage{i}_loaded") for i in range(4)]
        s_wt = [sem(f"W{i}_loaded") for i in range(KT)]
        s_shi = sem("stage_hi_made")
        s_slo = sem("stage_lo_made")
        s_small = sem("small_loaded")
        s_fold = sem("folded_operands_loaded")
        s_xh = sem("x_hi_made")
        s_xl = sem("x_lo_made")
        s_pre = sem("prep_product")
        s_prev = sem("prep_evacuated")
        s_lg = sem("logits_ready")
        s_ha = sem("lora_down_ready")
        s_base = sem("h0_ready")
        s_d = sem("expert_gap_ready")
        s_ex = sem("expert_exp_ready")
        s_gx = sem("gates_spread")
        s_gT = sem("gates_turned")
        s_gTs = sem("gates_turned_in_sbuf")
        s_hg = sem("gated_down_ready")
        s_hgh = sem("gated_hi_made")
        s_hgl = sem("gated_lo_made")
        s_hev = sem("h0_in_sbuf")
        s_hh = sem("h0_hi_made")
        s_hl = sem("h0_lo_made")
        s_oadd = sem("h0_added_to_x")
        s_sq = sem("h0_squares_summed")
        s_q = sem("query_ready")
        s_qT = sem("query_in_sbuf")
        s_u = sem("uncertainty_hidden_ready")
        s_gl = sem("gelu_done")
        s_sc = sem("scores_ready")
        s_scr = sem("scores_read")
        s_t = sem("attention_masked")
        s_e = sem("attention_exp_done")
        s_st = sem("token_sums_ready")
        s_str = sem("token_sums_read")
        s_rexp = sem("state_exp_small")
        s_dsm = sem("state_reciprocal")
        s_ph = sem("state_phases_ready")
        s_phd = sem("state_waves_done")
        s_L = sem("state_factors_ready")
        s_k = sem("taps_ready")
        s_kc = sem("taps_split")
        s_kst = sem("taps_stored")
        s_pz = sem("tap_zeros_made")
        s_dve = sem("vector_step")
        s_pool = sem("pool_step")
        s_one = sem("query_ones_set")
        s_wvu = sem("Wvu_loaded")
        s_var = sem("variance_ready")
        s_lv = sem("log_variance_ready")
        s_lvs = sem("log_variance_sums_ready")
        s_un = sem("uncertainty_ready")
        s_sg = sem("gate_sigmoid_ready")
        s_ulp = sem("x1_lo_made_by_gpsimd")
        s_idf = sem("identity_cast")
        s_bm = sem("block_max_ready")
        s_out = sem("out_stored")
        s_gsum = sem("log_var_summed")
        s_eT = sem("attention_turned")
        s_eTs = sem("attention_turned_in_sbuf")
        s_dg = sem("gates_on_diagonal")
        s_gb = sem("gates_spread_over_partitions")
        s_zg = sem("memory_gated")
        s_zh = sem("memory_hi_made")
        s_zl = sem("memory_lo_made")
        s_wh = sem("Wvu_hi_made")
        s_wl = sem("Wvu_lo_made")
        s_z = sem("memory_read")
        s_zc = sem("memory_reading_copied")
        s_aux = sem("memory_out_ready")
        s_x1 = sem("x1_ready")
        s_uh = sem("x1_hi_made")
        s_ul = sem("x1_lo_made")
        s_lenl = sem("lengths_loaded")
        s_ym = sem("length_mask_made")
        s_tp = [sem(f"toeplitz{i}_loaded") for i in range(4)]
        s_cv = sem("head_convolved")
        s_y = sem("y_masked")
        s_yh = sem("y_hi_made")
        s_yl = sem("y_lo_made")
        s_fst = [sem("ffn_stage0_loaded"), sem("ffn_stage1_loaded")]
        s_fhi = sem("ffn_weight_hi_made")
        s_flo = sem("ffn_weight_lo_made")
        s_a1 = sem("rank_product_ready")
        s_a1h = sem("rank_hi_made")
        s_a1l = sem("rank_lo_made")
        s_in = sem("inter_ready")
        s_mk = sem("argmax_mask_made")
        s_mT = sem("hidden_turned")
        s_mTs = sem("hidden_in_sbuf")
        s_nk = sem("tile_counts_made")
        s_g1 = sem("ffn_hidden_ready")
        s_m = sem("hidden_masked")
        s_mh = sem("hidden_hi_made")
        s_ml = sem("hidden_lo_made")
        s_o = sem("ffn_out_ready")
        s_oa = sem("ffn_out_added")

        START = 4
        from_start = [s_str, s_scr, s_hev, s_kc, s_gl, s_oadd, s_sq, s_x1, s_y, s_yh, s_yl, s_a1l, s_oa, s_o, s_e]

        pieces = [
            (Rsp[0], Rsp[1], WrT.rearrange("(k p) e -> p k e", p=P), [KT, NE], S_R),
            (Asp[0], Asp[1], AT.rearrange("(k p) e -> p k e", p=P), [KT, P], S_W),
        ]
        wt = WT.rearrange("(k p) o -> k p o", p=P)
        pieces += [(Wsp[0][:, k, :], Wsp[1][:, k, :], wt[k], [L], S_W) for k in range(KT)]
        pieces += [
            (Bsp[0], Bsp[1], BT, [L], S_W),
            (Qsp[0][:, :, 0:BOT], Qsp[1][:, :, 0:BOT], WqT.rearrange("(k p) e -> p k e", p=P), [KT, BOT], 1.0),
        ]
        u1v = Wu1T.rearrange("(k p) e -> p k e", p=P)
        pieces += [(U1[0][:, 4 * i:4 * i + 4, :], U1[1][:, 4 * i:4 * i + 4, :], u1v[:, 4 * i:4 * i + 4, :], [4, UH], 1.0)
                   for i in range(2)]
        NPC = len(pieces)
        N_A = 2
        X_AT = N_A + 4
        XP = KT // 2
        BANK0 = [2, 3, 5, 6, 7, 2, 3, 2]
        WIDE = 5
        X1_BANK = [4, 6, 7]
        DVE_LO = (3,)
        assert KT - 1 not in DVE_LO

        def h_bank(o, is_first):
            return BANK0[o] if is_first else 2 + o % 2

        RINGED = [n for n in range(NPC) if not N_A <= n < N_A + KT]
        STAGES = 4

        def stage_of(n):
            return RINGED.index(n) % STAGES

        def staged(n, shape):
            if N_A <= n < N_A + KT:
                return OUTF[:, KT * GT + (n - N_A) * L:KT * GT + (n - N_A + 1) * L]
            s = stage[stage_of(n)][:, 0:int(np.prod(shape))]
            return s.rearrange("p (a b) -> p a b", a=shape[0]) if len(shape) == 2 else s

        def arrived(eng, n):
            if N_A <= n < N_A + KT:
                eng.wait_ge(s_wt[n - N_A], 16)
            else:
                eng.wait_ge(s_stage[stage_of(n)], 16 * (RINGED.index(n) // STAGES + 1))

        def head_of(x, h, n):
            v = x.rearrange("p k (b h) -> p k h b", h=H)
            return v[:, :, bass.ds(h, n), :] if n > 1 else v[:, :, bass.ds(h, 1), :].rearrange("p k c b -> p k (c b)")

        def batches(g):
            return bass.ds(g * BPG, BPG)

        def by_batch(x):
            return x.rearrange("p (b h) -> p b h", h=H) if len(x.shape) == 2 else x.rearrange("p k (b h) -> p k b h", h=H)

        def tok(g):
            return bass.ds(g * GT, GT)

        small_loads = [(cst, packed), (Dall[TA - 1:TA, :], Dh)]
        small_loads += [(row_i[:, 0:B], lens.partition_broadcast(B)), (row_i[:, B:B + 1], lens.unsqueeze(1)),
                        (row_i[:, B + 1:B + 2], ids.unsqueeze(1))]
        vT, spare = [OUTF[:, (NG - 1) * KT * GT + i * KT * NS:(NG - 1) * KT * GT + (i + 1) * KT * NS]
                     .rearrange("p (k n) -> p k n", k=KT) for i in range(2)]
        fold_keys, fold_rk = spare[0:BOT, 0, :], spare[0:RD, 1, :]
        fold_wr, fold_wr2 = spare[0:RD, 2, 0:BOT], spare[0:BOT, 3, 0:RD]
        vdT = [spare[:, 4 + k // 4, BOT * (k % 4):BOT * (k % 4) + BOT] for k in range(KT)]
        NSM = len(small_loads)
        small_loads += [(fold_wr, Wr), (fold_wr2, Wr2T), (fold_keys, keysT),
                        (vT, valuesT.rearrange("(k p) n -> p k n", p=P))]
        small_loads += [(spare[:, 4 + i, :].rearrange("p (k e) -> p k e", k=4),
                         WvdT.rearrange("(k p) e -> p k e", p=P)[:, 4 * i:4 * i + 4, :]) for i in range(2)]
        NSF = len(small_loads)
        w1v = w1L.rearrange("t p c -> (t p) c")

        def w1_source(pair, q):
            return w1v[bass.ds(pair * P, P), q * 512:q * 512 + 512]

        def w2_source(it, half):
            return w2[bass.ds(it * P, P), half * 512:half * 512 + 512]

        N_C1, N_W1, N_C2, N_W2 = 2, 2 + 2 * CI, 2 + 2 * CI + 8, 2 + 2 * CI + 8 + 6
        CPC = INTER // 8
        W1_SLOTS = [(0, 1), (0, 2), (1, 2)]
        W1_EARLY = [1, 0, 0]

        def chunk_pieces(s, phase, last=False):
            def w1_pair(which):
                slot = W1_SLOTS[(phase + 1) % BODY][which]
                return [(1, w1_source((s + 1) * (CI // 2) + which, q), slot * KT * PAIR + q * 512) for q in range(4)]

            def w2_half(c, tile, half):
                slot = (CI * (phase + c) + tile) % RING
                return (2, w2_source((s + c) * CI + tile, half), slot * L + half * 512)

            own = [w2_half(0, 2, 1), w2_half(0, 3, 1)]
            if last:
                return own
            early = W1_EARLY[phase]
            return (own + w1_pair(early)
                    + [w2_half(1, t, h) for t in range(2) for h in range(2)]
                    + w1_pair(1 - early) + [w2_half(1, 2, 0), w2_half(1, 3, 0)])

        def first(n):
            return isinstance(n, int) and n == 0

        w2_first = [(0, 0), (0, 1), (1, 0), (1, 1), (2, 0), (3, 0)]
        PPC = 16

        AT_STEP = [((0, 1), (), (), ()), ((), (), (2,), (3,)), ((), (), (4,), (5,)), ((), (), (6,), (7,)),
                   ((), (), (8,), (9,)), ((), (), (), ()), ((), (10,), (11,), (12, 13)), ((), (), (), (14, 15))]

        def w1_flat(part):
            return w1r[part].rearrange("p a b c -> p (a b c)")

        def ring_slot(part, ring, at):
            flat = w1_flat(part) if ring == 1 else w2r[part].rearrange("p a b -> p (a b)")
            return flat[:, at:at + 512]

        POOL_DEN, POOL_HALF = 31, 34
        PREV = 5
        KST_FIRST, KST_GROUP = 32, 32 * HPG

        def tap_rows(i, g, hh):
            src = kp[i][bass.ds(g * HPG + hh, 1), 0:L]
            return bass.AP(tensor=src.tensor, offset=src.offset, ap=[[TB, TA], [1, TB]])

        block = ctx.enter_context(nc.Block())

        @block.sync
        def _(sp):
            def batches_at(place, count):
                return nc.values_load_multi_w_load_instructions(
                    perm_i[0:1, bass.ds(place, count)], engines=(mybir.EngineType.SP,), min_val=0, max_val=B - 1)[1]

            def load_x(g):
                for i, b in enumerate(batches_at(g * BPG, BPG)):
                    sp.dma_start(OUTF[:, bass.ds((g * BPG + i) * KT * H, KT * H)], xB[bass.ds(b * P, P), :]).then_inc(s_x, 16)

            for n, (hi, lo, src, shape, _) in enumerate(pieces):
                if n == X_AT:
                    sp.wait_ge(s_perm, 1)
                    load_x(0)
                    sp.wait_ge(s_nk, 1)
                    most_tiles = nc.values_load_multi_w_load_instructions(
                        nk_i[0:1, NT - 1:NT], engines=(mybir.EngineType.SP,), min_val=2, max_val=KT)[1][0]
                if n in RINGED and RINGED.index(n) >= STAGES:
                    before = RINGED[RINGED.index(n) - STAGES]
                    sp.wait_ge(s_shi, before + 1)
                    sp.wait_ge(s_slo, before + 1)
                sp.dma_start(staged(n, shape), src).then_inc(s_stage[stage_of(n)] if n in RINGED else s_wt[n - N_A], 16)
                if n == N_A - 1:
                    for dst, fold_src in small_loads[NSM:]:
                        sp.dma_start(dst, fold_src, allow_slow_non_contiguous=True).then_inc(s_fold, 16)
            sp.wait_ge(s_pz, 2)
            for i in range(2):
                sp.dma_start(kp[i][:, L:KROWS], zpad[0:H, :]).then_inc(s_kst, 16)
            sp.wait_ge(s_slo, N_A + KT)
            sp.wait_ge(s_pre, 3)
            sp.wait_ge(s_prev, PREV)
            with sp.Fori(0, NG - 1) as g:
                sp.wait_ge(s_xh, XP + g)
                load_x(g + 1)
                sp.wait_ge(s_kc, START + 2 * g + 2)
                for i in range(2):
                    for hh in range(HPG):
                        sp.dma_start(tap_rows(i, g, hh), ksp[i][:, hh, :]).then_inc(s_kst, 16)
            sp.wait_ge(s_u, 2 * NG)
            for i in range(2):
                sp.dma_start(wvu32[BOT * i:BOT * i + BOT, :], WvuT).then_inc(s_wvu, 16)
            sp.wait_ge(s_kc, START + 2 * NG)
            for i in range(2):
                for hh in range(HPG):
                    sp.dma_start(tap_rows(i, NG - 1, hh), ksp[i][:, hh, :]).then_inc(s_kst, 16)
            sp.wait_ge(s_aux, KT * NG)
            sp.dma_start(posF, packed[:, C_POS:C_POS + KT], allow_slow_non_contiguous=True).then_inc(s_lenl, 16)
            sp.dma_start(id32, packed[:, C_ID:C_ID + P], allow_slow_non_contiguous=True).then_inc(s_lenl, 16)
            sp.wait_ge(s_kst, 32 + 32 * HPG * NG)

            def toeplitz(h, i, skip):
                src = kp[0][bass.ds(h, 1), 0:L]
                src = bass.AP(tensor=src.tensor, offset=src.offset + skip * P, ap=[[1, P], [H * KROWS, 2], [1, L - skip * P]])
                sp.dma_start(toep[i][:, :, skip * P:L], src).then_inc(s_tp[i], 16)

            def piece(n, par, dst, src, first=False):
                if not first:
                    sp.wait_ge(s_fhi, n - 1)
                    sp.wait_ge(s_flo, n - 1)
                sp.dma_start(dst, src).then_inc(s_fst[par], 16)

            def during_convolution(skip):
                for i in range(4):
                    toeplitz(i, i, skip)
                c1v = c1P.rearrange("(k p) c -> p k c", p=P)
                for n in range(N_C1):
                    piece(n, n, fst[n][:, 0:4 * C1R].rearrange("p (k c) -> p k c", k=4), c1v[:, 4 * n:4 * n + 4, :], first=True)

                def heads(q, pieces_of):
                    for i in range(8):
                        if i in (0, 4):
                            pieces_of(q, i // 4)
                        sp.wait_ge(s_cv, 8 * q + i + 1)
                        toeplitz(8 * q + 4 + i, i % 4, skip)

                def w1_piece(q, par):
                    src = w1L[0:1, 0:P, 0:512]
                    at = (q // 2) * (P * KT * PAIR) + (2 * (q % 2) + par) * 512
                    src = bass.AP(tensor=src.tensor, offset=src.offset + at, ap=[[KT * PAIR, P], [1, 512]])
                    piece(N_C1 + 2 * q + par, par, fst[par], src)

                def c2_piece(q, par):
                    piece(N_W1 + 2 * (q - 4) + par, par, fst[par][0:C1R, 0:CPC],
                          c2T[:, bass.ds((2 * (q - 4) + par) * CPC, CPC)])

                with sp.Fori(0, 4) as q:
                    heads(q, w1_piece)
                with sp.Fori(4, 7) as q:
                    heads(q, c2_piece)
                c2_piece(7, 0)
                for i in range(4):
                    sp.wait_ge(s_cv, 56 + i + 1)
                    toeplitz(60 + i, i, skip)
                c2_piece(7, 1)

            with sp.If(most_tiles < KT):
                during_convolution(1)
            with sp.Else():
                during_convolution(0)
            for j, (tile, half) in enumerate(w2_first):
                piece(N_C2 + j, j % 2, fst[j % 2], w2_source(tile, half))

            def chunk(s, phase, last=False):
                for j, (_, src, _) in enumerate(chunk_pieces(s, phase, last)):
                    piece(N_W2 + PPC * s + j, j % 2, fst[j % 2], src)

            with sp.Fori(0, NC - BODY, BODY) as s:
                for j in range(BODY):
                    chunk(s + j, j)
            chunk(NC - 1, (NC - 1) % BODY, last=True)
            stores = 0
            for j in range(SPC):
                w = KT if j < SPC - 1 else 2
                places = batches_at(STEP * BPT * j, STEP * BPT)
                for o in range(0, KT, w):
                    sp.wait_ge(s_oa, START + OP * (SPC * (NC - 1) + j) + (o + w) // 2)
                    for i, b in enumerate(places):
                        at = (STEP * BPT * j + i) * KT * H
                        sp.dma_start(out[bass.ds(b * P, P), o * H:(o + w) * H], OUTF[:, at + o * H:at + (o + w) * H])\
                            .then_inc(s_out, 16)
                        stores += 1
            sp.wait_ge(s_out, 16 * stores)

        @block.tensor
        def _(pe):
            def mm3(dst, lhs, rhs, k, n, more=False):
                (lh, ll), (rh, rl) = lhs, rhs
                pe.matmul(dst, lh, rh, start=(k == 0), stop=False)
                pe.matmul(dst, lh, rl, start=False, stop=False)
                return pe.matmul(dst, ll, rh, start=False, stop=(k == n - 1 and not more))

            pe.wait_ge(s_key, 1)
            for i in range(3):
                mm = pe.matmul(PS[:, 7, B * i:B * i + B], spread[:, i, :], at_place, start=True, stop=True)
            mm.then_inc(s_sort, 1)

            tiles = []

            def fold():
                pe.wait_ge(s_fold, 16 * (NSF - NSM))
                pe.matmul(PS[0:RD, 4, 0:NS], fold_wr2, fold_keys, start=True, stop=True).then_inc(s_pre, 1)
                for n in range(2):
                    for k in range(KT):
                        mm = pe.matmul(PS[:, 4, NS + BOT * n:NS + BOT * n + BOT], vT[:, k, n * P:n * P + P], vdT[k],
                                       start=(k == 0), stop=(k == KT - 1))
                mm.then_inc(s_pre, 1)
                pe.wait_ge(s_prev, 4)
                pe.matmul(PS[0:BOT, 4, 0:NS], fold_wr, fold_rk, start=True, stop=True).then_inc(s_pre, 1)

            def read_memory(g, part):
                if part < 2:
                    pe.wait_ge(s_e, START + TPG * g + 2 * part + 2)
                    if part:
                        pe.wait_ge(s_eTs, 2 * g + 1)
                    for t in range(2 * part, 2 * part + 2):
                        for n in range(2):
                            at = ((t % 2) * 2 + n) * P
                            mm = pe.transpose(PS[:, 6, at:at + P], e_g[:, t, n * P:n * P + P], ident)
                    mm.then_inc(s_eT, 1)
                    return
                pe.wait_ge(s_eTs, 2 * g + 2)
                for n in range(2):
                    mm = pe.matmul(PS[:, 7, :], AV[:, n, :], eT[:, n, :], start=(n == 0), stop=(n == 1))
                mm.then_inc(s_z, 1)

            def group(g, is_first=False):
                def x_split(k):
                    if is_first and k % 2 == 0:
                        pe.wait_ge(s_xh, k // 2 + 1)
                        pe.wait_ge(s_xl, k // 2 + 1)

                def base(o, ks=range(KT)):
                    for k in ks:
                        mm3(PS[:, h_bank(o, is_first), :], [w[:, k, o * P:o * P + P] for w in Wsp],
                            [x[:, k, :] for x in xsp], k, KT, more=True)

                def lora(o):
                    dst = PS[:, h_bank(o, is_first), :]
                    (bh, bl), (gh, gl_) = [w[:, o * P:o * P + P] for w in Bsp], hgsp
                    pe.matmul(dst, bh, gh, start=False, stop=False)
                    pe.matmul(dst, bh, gl_, start=False, stop=False)
                    pe.matmul(dst, bl, gh, start=False, stop=True).then_inc(s_base, 1)

                def logits():
                    for t in range(TPG):
                        for k in range(KT):
                            mm = mm3(PS[:, 0, NE * t:NE * t + NE], [x[:, k, t * P:t * P + P] for x in xsp],
                                     [w[:, k, :] for w in Rsp], k, KT)
                    mm.then_inc(s_lg, 1)

                def down(ks=range(KT)):
                    for k in ks:
                        mm = mm3(PS[:, 1, :], [w[:, k, :] for w in Asp], [x[:, k, :] for x in xsp], k, KT)
                    if k == KT - 1:
                        mm.then_inc(s_ha, 1)

                def turn_gates():
                    pe.wait_ge(s_gx, g + 1)
                    for t in range(TPG):
                        mm = pe.transpose(PS[:, 4, t * P:t * P + P], Gx[:, t * P:t * P + P], ident)
                    mm.then_inc(s_gT, 1)

                if is_first:
                    fold()
                    pe.wait_ge(s_nk, 1)
                    tiles.extend(nc.values_load_multi_w_load_instructions(
                        nk_i[0:1, :], engines=(mybir.EngineType.PE,), min_val=2, max_val=KT)[1])
                    pe.wait_ge(s_shi, N_A)
                    pe.wait_ge(s_slo, N_A)
                    for k in range(KT):
                        x_split(k)
                        down([k])
                    logits()
                    for k in range(KT):
                        pe.wait_ge(s_shi, N_A + k + 1)
                        pe.wait_ge(s_slo, N_A + k + 1)
                        for o in range(WIDE):
                            base(o, [k])
                    pe.wait_ge(s_shi, NPC)
                    pe.wait_ge(s_slo, NPC)
                    pe.wait_ge(s_prev, PREV)
                    turn_gates()
                    pe.wait_ge(s_hgh, g + 1)
                    pe.wait_ge(s_hgl, g + 1)
                    for o in range(WIDE):
                        lora(o)
                    for o in range(WIDE, KT):
                        pe.wait_ge(s_hev, START + max(i for i in range(o) if BANK0[i] == BANK0[o]) + 1)
                        base(o)
                        lora(o)
                else:
                    pe.wait_ge(s_xh, XP + g)
                    pe.wait_ge(s_xl, XP + g)
                    logits()
                    pe.wait_ge(s_scr, START + TPG * g)
                    down()
                    for o in range(KT):
                        pe.wait_ge(s_hev, START + KT * g + o - 1)
                        base(o)
                        if o == 0:
                            turn_gates()
                            continue
                        if o == 1:
                            pe.wait_ge(s_hgh, g + 1)
                            pe.wait_ge(s_hgl, g + 1)
                            lora(0)
                        lora(o)
                        if o == 2:
                            pe.wait_ge(s_str, START + g)
                        if 2 <= o < 5:
                            read_memory(g - 1, o - 2)
                pe.wait_ge(s_one, 1)
                pe.wait_ge(s_kc, START + 2 * g)
                for k in range(KT):
                    pe.wait_ge(s_hh, KT * g + k + 1)
                    pe.wait_ge(s_hl, KT * g + k + 1)
                    mm = mm3(PS[0:BOT + 1, 5, :], [w[:, k, :] for w in Qsp], [x[:, k, :] for x in hsp], k, KT)
                mm.then_inc(s_q, 1)
                if not is_first:
                    pe.wait_ge(s_zc, g)

                def uncertain(n):
                    for k in range(KT):
                        mm = mm3(PS[:, 6 + n, :], [w[:, k, n * P:n * P + P] for w in U1], [x[:, k, :] for x in hsp], k, KT)
                    mm.then_inc(s_u, 1)

                def scores(t):
                    pe.wait_ge(s_scr, START + TPG * g + t - 1)
                    pe.matmul(PS[:, 1 + 3 * (t % 2), :], qT[0:BOT, t * P:t * P + P], MK[0:BOT, :],
                              start=True, stop=True).then_inc(s_sc, 1)

                uncertain(0)
                pe.wait_ge(s_qT, g + 1)
                scores(0)
                scores(1)
                uncertain(1)
                scores(2)
                scores(3)
                pe.wait_ge(s_L, g + 1)
                for h in range(HPG):
                    mm = pe.matmul(PS[0:TA, 5, h * TB:h * TB + TB], ph[1][:, h, :], ph[0][:, h, :], start=True, stop=True)
                mm.then_inc(s_k, 1)
                pe.wait_ge(s_sq, START + 2 * KT * g + 2 * KT)
                pe.wait_ge(s_gl, START + 2 * g + 2)
                for t in range(TPG):
                    c = slice(t * P, t * P + P)
                    pe.matmul(PS[:, 6, t:t + 1], qT[0:BOT + 1, c], cst[0:BOT + 1, C_E64:C_E64 + 1], start=True, stop=True)
                    pe.matmul(PS[:, 6, 4 + t:5 + t], acc[:, c], cst[:, C_ONE:C_ONE + 1], start=True, stop=True)
                    pe.matmul(PS[:, 6, 8 + t:9 + t], gl[:, 0, c], wu2s[:, 0:1], start=True, stop=False)
                    mm = pe.matmul(PS[:, 6, 8 + t:9 + t], gl[:, 1, c], wu2s[:, 1:2], start=False, stop=True)
                mm.then_inc(s_st, 1)

            group(0, is_first=True)
            with pe.Fori(1, NG - 1) as g:
                group(g)
            group(NG - 1)

            pe.wait_ge(s_str, START + NG)
            read_memory(NG - 1, 0)
            read_memory(NG - 1, 1)
            pe.wait_ge(s_lvs, 1)
            pe.matmul(PS[:, 3, 0:1], ones, gate[:, 3, 0:1], start=True, stop=True).then_inc(s_gsum, 1)
            read_memory(NG - 1, 2)
            for g in range(NG):
                pe.wait_ge(s_dg, g + 1)
                pe.matmul(PS[:, g, :], ones, diag[g].rearrange("p t c -> p (t c)"), start=True, stop=True).then_inc(s_gb, 1)
            pe.wait_ge(s_wh, 1)
            pe.wait_ge(s_wl, 1)

            for g in range(NG):
                pe.wait_ge(s_zh, g + 1)
                pe.wait_ge(s_zl, g + 1)
                for o in range(KT):
                    pe.wait_ge(s_x1, START + KT * g + o - 2)
                    dst = PS[:, X1_BANK[(KT * g + o) % 3], :]
                    pe.matmul(dst, wvu[0][:, o * P:o * P + P], zsp[:, g, :], start=True, stop=False)
                    pe.matmul(dst, wvu[1][0:BOT, o * P:o * P + P], zsp[0:BOT, g, :], start=False, stop=True).then_inc(s_aux, 1)

            pe.wait_ge(s_uh, KT * NG)
            pe.wait_ge(s_ul, len(DVE_LO) * NG)
            pe.wait_ge(s_ulp, (KT - len(DVE_LO)) * NG)

            def convolve(q, blocks):
                for i in range(8):
                    pair = i // 2
                    if i % 2 == 0:
                        pe.wait_ge(s_y, START + 4 * q + pair - 3)
                    pe.wait_ge(s_tp[i % 4], 16 * (2 * q + i // 4 + 1))
                    bank = PS[:, pair, :].rearrange("p (i c b) -> p i c b", i=KT, c=2)
                    for d in range(blocks):
                        dst = bank[:, d:blocks, i % 2, :]
                        th, tl = [toep[i % 4][:, part, (KT - 1 - d) * P:(KT - d) * P] for part in range(2)]
                        uh, ul = [head_of(u[:, 0:blocks - d, :], q * 8 + i, 1) for u in fsp]
                        pe.matmul(dst, th, uh, start=(d == 0), stop=False)
                        pe.matmul(dst, th, ul, start=False, stop=False)
                        mm = pe.matmul(dst, tl, uh, start=False, stop=(d == blocks - 1))
                    mm.then_inc(s_cv, 1)

            with pe.If(tiles[NT - 1] < KT):
                with pe.Fori(0, H // 8) as q:
                    convolve(q, KT - 1)
            with pe.Else():
                with pe.Fori(0, H // 8) as q:
                    convolve(q, KT)

            pe.wait_ge(s_fhi, N_C1)
            pe.wait_ge(s_flo, N_C1)
            pe.wait_ge(s_yh, START + H // 2)
            pe.wait_ge(s_yl, START + H // 2)
            def rank_product(g):
                pe.wait_ge(s_a1l, START + g - 1)
                for k in range(KT):
                    mm = mm3(PS[0:C1R, 6 + g % 2, :], [w[:, k, :] for w in c1s], [y[:, k, g * GT:g * GT + GT] for y in fsp], k, KT)
                mm.then_inc(s_a1, 1)

            rank_product(0)
            rank_product(1)

            def inter(n, s, j, t):
                if not first(n):
                    pe.wait_ge(s_mk, STEP * n + t - 1)
                T = STEP * j + t
                pe.matmul(PS[:, t, :], a1s[:, T * P:T * P + P], c2s[:, bass.ds(s * CI * P, CI * P)],
                          start=True, stop=True).then_inc(s_in, 1)

            def hidden(n, phase, j, t):
                if not first(n):
                    pe.wait_ge(s_m, STEP * n + t - 1)
                T, (a_, b_) = STEP * j + t, W1_SLOTS[phase]
                dst = PS[:, 2 + t, :]

                def operands(k):
                    if isinstance(k, int):
                        y = [x[:, k, T * P:T * P + P] for x in fsp]
                        return y, [w[:, a_:b_ + 1:b_ - a_, k, :] for w in w1r]
                    y = [x[:, bass.ds(k, 1), T * P:T * P + P].rearrange("p a b -> p (a b)") for x in fsp]
                    return y, [w[:, a_:b_ + 1:b_ - a_, bass.ds(k, 1), :].rearrange("p s a b -> p s (a b)") for w in w1r]

                (yh, yl), (wh, wl) = operands(0)
                pe.matmul(dst, yh, wh, start=True, stop=False)
                pe.matmul(dst, yh, wl, start=False, stop=False)
                with pe.Fori(1, tiles[T]) as k:
                    (kh, kl), (vh, vl) = operands(k)
                    pe.matmul(dst, kh, vh, start=False, stop=False)
                    pe.matmul(dst, kh, vl, start=False, stop=False)
                    pe.matmul(dst, kl, vh, start=False, stop=False)
                pe.matmul(dst, yl, wh, start=False, stop=True).then_inc(s_g1, 1)

            def turn(n, t):
                pe.wait_ge(s_mh, STEP * n + t + 1)
                pe.wait_ge(s_ml, STEP * n + t + 1)
                if not first(n):
                    pe.wait_ge(s_mTs, STEP * n + t - 1)
                for part in range(2):
                    for i in range(CI):
                        at = (part * CI + i) * P
                        mm = pe.transpose(PSH[:, 4 + t, at:at + P], mtok[t][:, part, i * P:i * P + P], idF)
                mm.then_inc(s_mT, 1)

            pe.wait_ge(s_idf, 1)
            pe.wait_ge(s_fhi, N_W1)
            pe.wait_ge(s_flo, N_W1)
            for t in range(STEP):
                hidden(0, 0, 0, t)
            pe.wait_ge(s_fhi, N_C2)
            pe.wait_ge(s_flo, N_C2)
            pe.wait_ge(s_a1h, 1)
            pe.wait_ge(s_a1l, START + 1)
            for t in range(STEP):
                inter(0, 0, 0, t)
            for t in range(STEP):
                rank_product(2 + t)
                turn(0, t)
            pe.wait_ge(s_a1h, NG)
            pe.wait_ge(s_a1l, START + NG)

            def chunk(s, phase, last=False):
                for j in range(SPC):
                    n = SPC * s + j
                    wrap = (j + 1) // SPC
                    nj, nphase = (j + 1) % SPC, (phase + wrap) % BODY
                    more = not (last and wrap)
                    if more:
                        for t in range(STEP):
                            inter(n + 1, s + wrap, nj, t)
                    pe.wait_ge(s_mTs, STEP * n + STEP)
                    for o in range(KT):
                        if j == 0 and o in (0, KT // 2):
                            pe.wait_ge(s_fhi, N_W2 + PPC * s + (2 if o else 0))
                            pe.wait_ge(s_flo, N_W2 + PPC * s + (2 if o else 0))
                        if o % 2 == 0:
                            pe.wait_ge(s_oa, START + OP * n + o // 2 - 1)
                        dst = PS[:, 6 + o // 2 % 2, :].rearrange("p (b k h) -> p k b h", k=2, h=H)[:, o % 2, :, :]
                        for k in range(CI):
                            r = (CI * phase + k) % RING
                            mm = mm3(dst, [w[:, r, o * P:o * P + P] for w in w2r], [msp[j % 2][:, part, k, :] for part in range(2)],
                                     k, CI)
                        if o % 2:
                            mm.then_inc(s_o, 1)
                        if more and o < STEP:
                            if wrap and o == 0:
                                pe.wait_ge(s_fhi, N_W2 + PPC * s + 14)
                                pe.wait_ge(s_flo, N_W2 + PPC * s + 14)
                            hidden(n + 1, nphase, nj, o)
                        if more and o in (4, 5):
                            turn(n + 1, o - 4)

            with pe.Fori(0, NC - BODY, BODY) as s:
                for j in range(BODY):
                    chunk(s + j, j)
            chunk(NC - 1, (NC - 1) % BODY, last=True)

        @block.scalar
        def _(act):
            act.wait_ge(s_pz, 2)
            for dst, src in small_loads[:NSM]:
                act.dma_start(dst, src, allow_slow_non_contiguous=True).then_inc(s_small, 16)

            def hi_piece(n):
                hi, _, _, shape, scale = pieces[n]
                arrived(act, n)
                act.activation(hi, staged(n, shape), ACT.Copy, scale=scale).then_inc(s_shi, 1)

            def folded():
                act.wait_ge(s_pre, 2)
                act.activation(fold_rk, PS[0:RD, 4, 0:NS], ACT.Copy).then_inc(s_prev, 1)
                act.activation(MK[0:BOT, NS:2 * NS], fold_keys, ACT.Copy, scale=BOT ** -0.5).then_inc(s_prev, 1)
                for i in range(2):
                    act.activation(AV[:, :, BOT * i:BOT * i + BOT], PS[:, 4, NS:NS + 2 * BOT].rearrange("p (n c) -> p n c", n=2),
                                   ACT.Copy).then_inc(s_prev, 1)
                act.wait_ge(s_pre, 3)
                act.activation(MK[0:BOT, 0:NS], PS[0:BOT, 4, 0:NS], ACT.Copy, scale=RD ** -0.5).then_inc(s_prev, 1)

            hi_piece(0)
            hi_piece(1)
            for n in range(N_A, NPC):
                if n == X_AT:
                    folded()
                    act.wait_ge(s_x, 16 * BPG)
                    for k in range(0, KT, 2):
                        act.activation(by_batch(xsp[0][:, k:k + 2, :]), OUTV[:, k:k + 2, batches(0), :], ACT.Copy).then_inc(s_xh, 1)
                hi_piece(n)
                if n == N_A + KT - 2:
                    act.wait_ge(s_pool, POOL_HALF)
                    act.activation(t_[1], t_[1], ACT.Sin, scale=TWO_PI).then_inc(s_rexp, 1)
                    act.activation(t_[2], t_[2], ACT.Sin, scale=TWO_PI / 2).then_inc(s_rexp, 1)

            def turned_memory(g, half):
                act.wait_ge(s_eT, 2 * g + half + 1)
                act.activation(eT[:, :, half * 2 * P:half * 2 * P + 2 * P].rearrange("p n (t c) -> p n t c", t=2),
                               PS[:, 6, :].rearrange("p (t n c) -> p n t c", t=2, n=2), ACT.Copy).then_inc(s_eTs, 1)

            def reading(g):
                act.wait_ge(s_z, g + 1)
                act.activation(z_all[:, bass.ds(g * GT, GT)], PS[:, 7, :], ACT.Copy).then_inc(s_zc, 1)

            def group(g, is_first=False, last=False):
                act.wait_ge(s_d, g + 1)
                act.activation(gs[:, 3, :], gs[:, 2, :], ACT.Exp).then_inc(s_ex, 1)
                act.wait_ge(s_gT, g + 1)
                act.activation(gTs, PS[:, 4, :], ACT.Copy).then_inc(s_gTs, 1)
                act.wait_ge(s_hg, g + 1)
                act.activation(hgsp[0], hg32, ACT.Copy).then_inc(s_hgh, 1)
                for o in range(KT):
                    act.wait_ge(s_base, KT * g + o + 1)
                    act.wait_ge(s_oadd, START + KT * g + o - 1)
                    act.wait_ge(s_sq, START + 2 * (KT * g + o - 1))
                    act.activation(h32[:, o % 2, :], PS[:, h_bank(o, is_first), :], ACT.Copy, scale=1.0 / S_W).then_inc(s_hev, 1)
                    act.wait_ge(s_hev, START + KT * g + o + 1)
                    act.activation(hsp[0][:, o, :], h32[:, o % 2, :], ACT.Copy).then_inc(s_hh, 1)
                    if not is_first and o in (2, 3):
                        turned_memory(g - 1, o - 2)
                    if not is_first and o == 5:
                        reading(g - 1)
                    if o == (KT - 1 if is_first else 4):
                        act.wait_ge(s_ph, g + 1)
                        for i in range(3):
                            act.activation(ph[i], ph[i], ACT.Sin, scale=TWO_PI).then_inc(s_phd, 1)
                        for i in range(2):
                            act.activation(mg[i], mg[i], ACT.Exp).then_inc(s_phd, 1)
                if not last:
                    act.wait_ge(s_x, 16 * BPG * (g + 2))
                    act.activation(by_batch(xsp[0]), OUTV[:, :, batches(g + 1), :], ACT.Copy).then_inc(s_xh, 1)
                act.wait_ge(s_q, g + 1)
                act.activation(qT[0:BOT + 1, :], PS[0:BOT + 1, 5, :], ACT.Copy).then_inc(s_qT, 1)
                for t in range(TPG):
                    if t < 2:
                        n = t
                        act.wait_ge(s_u, 2 * g + n + 1)
                        act.activation(gl[:, n, :], PS[:, 6 + n, :], ACT.Gelu_apprx_tanh, bias=bu1s[:, n:n + 1]).then_inc(s_gl, 1)
                    act.wait_ge(s_t, TPG * g + t + 1)
                    at = bass.ds(TPG * g + t, 1)
                    act.activation(e_g[:, t, :], tm, ACT.Exp, bias=nm[:, t % 2:t % 2 + 1], accum_out=seall[:, at]).then_inc(s_e, 1)

            group(0, is_first=True)
            with act.Fori(1, NG - 1) as g:
                group(g)
            group(NG - 1, last=True)

            act.wait_ge(s_var, 1)
            act.activation(gate[:, 2, :], gate[:, 1, :], ACT.Ln, bias=1.0).then_inc(s_lv, 1)
            turned_memory(NG - 1, 0)
            turned_memory(NG - 1, 1)
            act.activation(gate[:, 4, :], st[:, 2, :], ACT.Sigmoid, bias=scal[:, 0:1]).then_inc(s_lv, 1)
            act.wait_ge(s_un, 1)
            act.activation(gate[:, 7, :], gate[:, 6, :], ACT.Sigmoid, bias=scal[:, 2:3], scale=scal[:, 1:2]).then_inc(s_sg, 1)
            reading(NG - 1)
            act.wait_ge(s_wvu, 32)
            act.activation(wvu[0], wvu32, ACT.Copy, scale=S_W).then_inc(s_wh, 1)

            def high_memory(g):
                act.wait_ge(s_zg, g + 1)
                act.activation(zsp[:, bass.ds(g, 1), :].rearrange("p a t -> p (a t)"), z_all[:, bass.ds(g * GT, GT)],
                               ACT.Copy).then_inc(s_zh, 1)

            high_memory(0)
            for g in range(NG):
                for o in range(KT):
                    act.wait_ge(s_x1, START + KT * g + o + 1)
                    act.activation(by_batch(fsp[0][:, o, tok(g)]), OUTV[:, o, batches(g), :], ACT.Copy).then_inc(s_uh, 1)
                    if g + 1 < NG and o == 1:
                        high_memory(g + 1)

            act.wait_ge(s_lenl, 32)
            act.activation(idF, id32, ACT.Copy).then_inc(s_idf, 1)

            def piece(n, par, dst, src, scale):
                act.wait_ge(s_fst[par], 8 * (n - par) + 16)
                act.activation(dst, src, ACT.Copy, scale=scale).then_inc(s_fhi, 1)

            for n in range(N_C1):
                piece(n, n, c1s[0][:, 4 * n:4 * n + 4, :], fst[n][:, 0:4 * C1R].rearrange("p (k c) -> p k c", k=4), S_W)

            def w1_piece(q, par):
                piece(N_C1 + 2 * q + par, par, w1_flat(0)[:, bass.ds((2 * q + par) * 512, 512)], fst[par], S_W)

            def c2_piece(q, par):
                piece(N_W1 + 2 * (q - 4) + par, par, c2s[:, bass.ds((2 * (q - 4) + par) * CPC, CPC)],
                      fst[par][0:C1R, 0:CPC], S_R)

            def convolved(q, pieces_of):
                for pair in range(4):
                    act.wait_ge(s_y, START + 4 * q + pair + 1)
                    act.activation(head_of(fsp[0], q * 8 + pair * 2, 2), y32[:, pair % 2, :].rearrange("p (k c b) -> p k c b", k=KT, c=2),
                                   ACT.Copy).then_inc(s_yh, 1)
                    if pair % 2:
                        pieces_of(q, pair // 2)

            with act.Fori(0, 4) as q:
                convolved(q, w1_piece)
            with act.Fori(4, 8) as q:
                convolved(q, c2_piece)

            def first_w2(j):
                tile, half = w2_first[j]
                piece(N_C2 + j, j % 2, ring_slot(0, 2, tile * L + half * 512), fst[j % 2], S_W)

            def high_rank(g):
                act.wait_ge(s_a1, g + 1)
                act.activation(a1s[:, g * GT:g * GT + GT], PS[0:C1R, 6 + g % 2, :], ACT.Copy, scale=1.0 / S_W).then_inc(s_a1h, 1)

            def high(n, t):
                act.wait_ge(s_m, STEP * n + t + 1)
                if not first(n):
                    act.wait_ge(s_mT, STEP * n + t - 1)
                act.activation(mtok[t][:, 0, :], m32, ACT.Copy, scale=1.0 / S_W).then_inc(s_mh, 1)

            def turned(n, t, buf):
                act.wait_ge(s_mT, STEP * n + t + 1)
                if not first(n):
                    act.wait_ge(s_o, START + OP * (n - 1))
                act.activation(msp[buf][:, :, :, t * P:t * P + P],
                               PSH[:, 4 + t, :].rearrange("p (a i c) -> p a i c", a=2, i=CI), ACT.Copy).then_inc(s_mTs, 1)

            act.wait_ge(s_cv, H)
            first_w2(0)
            first_w2(1)
            high_rank(0)
            first_w2(2)
            high_rank(1)
            first_w2(3)
            high(0, 0)
            high(0, 1)
            high_rank(2)
            turned(0, 0, 0)
            first_w2(4)
            high_rank(3)
            turned(0, 1, 0)
            first_w2(5)

            def chunk(s, phase, last=False):
                what = chunk_pieces(s, phase, last)

                def pieces_of(js):
                    for j in js:
                        if j >= len(what):
                            continue
                        if j == 0:
                            act.wait_ge(s_o, START + OP * SPC * s)
                        elif j == 2:
                            act.wait_ge(s_g1, NT * s + 1)
                        elif j == 10:
                            act.wait_ge(s_g1, NT * s + NT)
                        elif j == 14:
                            act.wait_ge(s_o, START + OP * (SPC * s + SPC - 1) + OP // 2)
                        ring, _, at = what[j]
                        piece(N_W2 + PPC * s + j, j % 2, ring_slot(0, ring, at), fst[j % 2], S_W)

                for j in range(SPC):
                    n = SPC * s + j
                    start, behind_high, behind_first, behind_second = AT_STEP[j]
                    pieces_of(start)
                    if last and j == SPC - 1:
                        continue
                    high(n + 1, 0)
                    high(n + 1, 1)
                    pieces_of(behind_high)
                    turned(n + 1, 0, (j + 1) % 2)
                    pieces_of(behind_first)
                    turned(n + 1, 1, (j + 1) % 2)
                    pieces_of(behind_second)

            with act.Fori(0, NC - BODY, BODY) as s:
                for j in range(BODY):
                    chunk(s + j, j)
            chunk(NC - 1, (NC - 1) % BODY, last=True)

        @block.vector
        def _(dve):
            done = [0]

            def step(ins):
                ins.then_inc(s_dve, 1)
                done[0] += 1
                dve.wait_ge(s_dve, done[0])

            dve.memset(zpad, 0.0).then_inc(s_pz, 1)
            dve.memset(Dall, 0.0).then_inc(s_pz, 1)

            def lo_piece(n):
                hi, lo, _, shape, scale = pieces[n]
                dve.wait_ge(s_shi, n + 1)
                dve.scalar_tensor_tensor(out=lo, in0=staged(n, shape), scalar=scale, in1=hi, op0=ALU.mult,
                                         op1=ALU.subtract).then_inc(s_slo, 1)

            dve.memset(Qsp[0][:, :, BOT:BOT + 1], 1.0).then_inc(s_dve, 1)
            dve.memset(Qsp[1][:, :, BOT:BOT + 1], 0.0).then_inc(s_one, 1)
            done[0] = 1
            for n in range(N_A):
                lo_piece(n)
            dve.wait_ge(s_small, 16 * NSM)
            digit, own = cst[0:B, C_TB:C_TB + B], cst[0:B, C_POS:C_POS + 1]
            step(dve.tensor_copy(row_f, row_i))
            step(dve.tensor_scalar(row_f[:, 0:B + 1], row_f[:, 0:B + 1], 0.0, float(L), ALU.max, ALU.min))
            step(dve.scalar_tensor_tensor(out=row_key, in0=row_f[:, 0:B], scalar=float(B), in1=digit, op0=ALU.mult, op1=ALU.add))
            step(dve.scalar_tensor_tensor(out=own_key, in0=row_f[:, B:B + 1], scalar=float(B), in1=own, op0=ALU.mult, op1=ALU.add))
            step(dve.tensor_scalar(longer, row_key, float(P - B), own_key, ALU.add, ALU.is_gt))
            step(dve.tensor_reduce(rank, longer, AX_X, ALU.add))
            step(dve.tensor_scalar(at_place, digit, rank, None, ALU.is_equal))
            step(dve.tensor_scalar(spread[:, 0, :], own.broadcast_to([B, P]), -1.0, P - 1.0, ALU.mult, ALU.add))
            step(dve.tensor_copy(spread[:, 1, :], row_f[:, B:B + 1].broadcast_to([B, P])))
            dve.tensor_copy(spread[:, 2, :], row_f[:, B + 1:B + 2].broadcast_to([B, P])).then_inc(s_key, 1)
            dve.wait_ge(s_sort, 1)
            dve.tensor_copy(perm_i, PS[:, 7, 0:B]).then_inc(s_perm, 1)
            step(dve.tensor_copy(len_s, PS[:, 7, B:2 * B]))
            for i in range(BPT):
                step(dve.tensor_copy(ids_f[H * i:H * i + H, :],
                                     PS[H * i:H * i + H, 7, 2 * B:3 * B].rearrange("p (t c) -> p c t", c=BPT)[:, i, :]))
            step(dve.tensor_reduce(nkf[:, 0, :], len_s.rearrange("p (t c) -> p t c", c=BPT), AX_X, ALU.max))
            step(dve.tensor_scalar(nkf[:, 1, :], nkf[:, 0, :], 1.0 / P, (P - 1.0) / P - 0.5 + 0.5 / P, ALU.mult, ALU.add))
            step(dve.tensor_scalar(nkf[:, 1, :], nkf[:, 1, :], 2.0, float(KT), ALU.max, ALU.min))
            step(dve.tensor_scalar(nkf[:, 0, :], nkf[:, 1, :], MAGIC, -MAGIC, ALU.add, ALU.add))
            dve.tensor_copy(nk_i, nkf[:, 0, :]).then_inc(s_nk, 1)
            for n in range(N_A, X_AT):
                lo_piece(n)
            for k in range(0, KT, 2):
                dve.wait_ge(s_xh, k // 2 + 1)
                dve.tensor_tensor(by_batch(xsp[1][:, k:k + 2, :]), OUTV[:, k:k + 2, batches(0), :], by_batch(xsp[0][:, k:k + 2, :]),
                                  ALU.subtract)\
                   .then_inc(s_xl, 1)
            step(dve.tensor_tensor(b5, cst[:, C_EXP:C_EXP + NE].unsqueeze(1).broadcast_to([P, NT, NE]),
                                   ids_f.unsqueeze(2).broadcast_to([P, NT, NE]), ALU.is_equal))
            step(dve.tensor_scalar(b5, b5, 5.0, None, ALU.mult))
            for n in range(X_AT, N_A + KT):
                lo_piece(n)
            dve.wait_ge(s_pool, POOL_DEN)
            dve.reciprocal(t_[0], t_[0]).then_inc(s_dsm, 1)
            for n in range(N_A + KT, NPC):
                lo_piece(n)

            def t8(i):
                return gts[:, i, :].rearrange("p (t e) -> p t e", t=TPG)

            def wide(ap, n):
                return ap.unsqueeze(2).broadcast_to([P, TPG, n])

            def row(ap):
                return ap.unsqueeze(1).broadcast_to([P, TPG, NE])

            iota = cst[:, C_EXP:C_EXP + NE]

            def split_taps(g):
                dve.wait_ge(s_k, g + 1)
                dve.wait_ge(s_kst, KST_FIRST + g * KST_GROUP)
                step(dve.tensor_scalar(kf, PS[0:TA, 5, :].rearrange("p (h b) -> p h b", h=HPG), 2.0 * S_W, None, ALU.mult))
                step(dve.scalar_tensor_tensor(out=kf[:, :, TB - 1], in0=Dall[:, bass.ds(g * HPG, HPG)], scalar=S_W,
                                              in1=kf[:, :, TB - 1], op0=ALU.mult, op1=ALU.add))
                dve.tensor_copy(ksp[0], kf).then_inc(s_kc, 1)
                dve.wait_ge(s_kc, START + 2 * g + 1)
                dve.tensor_tensor(ksp[1], kf, ksp[0], ALU.subtract).then_inc(s_kc, 1)

            def token_sums(g):
                dve.wait_ge(s_st, g + 1)
                dve.tensor_copy(st[:, :, bass.ds(TPG * g, TPG)], PS[:, 6, 0:3 * TPG].rearrange("p (a t) -> p a t", a=3))\
                   .then_inc(s_str, 1)

            def variances():
                dve.wait_ge(s_str, START + NG)
                dve.wait_ge(s_sq, START + 2 * KT * NG)
                dve.wait_ge(s_kst, KST_FIRST)
                step(dve.memset(ones, 1.0))
                step(dve.tensor_scalar(gate[:, 0, :], st[:, 0, :], 1.0 / L, None, ALU.mult))
                step(dve.tensor_tensor(gate[:, 1, :], gate[:, 0, :], gate[:, 0, :], ALU.mult))
                dve.scalar_tensor_tensor(out=gate[:, 1, :], in0=st[:, 1, :], scalar=1.0 / L, in1=gate[:, 1, :], op0=ALU.mult,
                                         op1=ALU.subtract).then_inc(s_var, 1)

            def group(g, last=False):
                dve.wait_ge(s_lg, g + 1)
                Lg = t8(0)
                step(dve.scalar_tensor_tensor(out=Lg, in0=PS[:, 0, 0:TPG * NE].rearrange("p (t e) -> p t e", t=TPG),
                                              scalar=1.0 / S_R, in1=b5[:, TPG * g:TPG * g + TPG, :], op0=ALU.mult, op1=ALU.add))
                for i in range(2):
                    eq, cand, one = t8(1), t8(2), t8(3 + i)
                    top, first = gs[:, i, :], gs[:, 5, :]
                    step(dve.tensor_reduce(top, Lg, AX_X, ALU.max))
                    step(dve.tensor_tensor(eq, Lg, wide(top, NE), ALU.is_equal))
                    step(dve.scalar_tensor_tensor(out=cand, in0=eq, scalar=-100.0, in1=row(iota), op0=ALU.mult, op1=ALU.add))
                    step(dve.tensor_reduce(first, cand, AX_X, ALU.min))
                    step(dve.tensor_tensor(one, cand, wide(first, NE), ALU.is_equal))
                    if i == 0:
                        step(dve.scalar_tensor_tensor(out=t8(5), in0=one, scalar=-BIG, in1=Lg, op0=ALU.mult, op1=ALU.add))
                        Lg = t8(5)
                dve.tensor_tensor(gs[:, 2, :], gs[:, 1, :], gs[:, 0, :], ALU.subtract).then_inc(s_d, 1)
                dve.wait_ge(s_ex, g + 1)
                step(dve.tensor_scalar(gs[:, 4, :], gs[:, 3, :], 1.0, None, ALU.add))
                step(dve.reciprocal(gs[:, 0, :], gs[:, 4, :]))
                step(dve.tensor_tensor(gs[:, 1, :], gs[:, 0, :], gs[:, 3, :], ALU.mult))
                step(dve.tensor_tensor(t8(1), t8(3), wide(gs[:, 0, :], NE), ALU.mult))
                step(dve.tensor_tensor(t8(2), t8(4), wide(gs[:, 1, :], NE), ALU.mult))
                step(dve.tensor_tensor(gts[:, 6, :], gts[:, 1, :], gts[:, 2, :], ALU.add))
                dve.tensor_copy(Gx.rearrange("p (e r) -> p e r", r=RK),
                                gts[:, 6, :].unsqueeze(2).broadcast_to([P, TPG * NE, RK])).then_inc(s_gx, 1)
                dve.wait_ge(s_gTs, g + 1)
                dve.wait_ge(s_ha, g + 1)
                dve.scalar_tensor_tensor(out=hg32, in0=PS[:, 1, :], scalar=2.0 / S_W, in1=gTs, op0=ALU.mult,
                                         op1=ALU.mult).then_inc(s_hg, 1)
                dve.wait_ge(s_hgh, g + 1)
                dve.wait_ge(s_hg, g + 1)
                dve.tensor_tensor(hgsp[1], hg32, hgsp[0], ALU.subtract).then_inc(s_hgl, 1)
                for o in range(KT):
                    dve.wait_ge(s_hh, KT * g + o + 1)
                    dve.tensor_tensor(hsp[1][:, o, :], h32[:, o % 2, :], hsp[0][:, o, :], ALU.subtract).then_inc(s_hl, 1)
                    x = OUTV[:, o, batches(g), :]
                    dve.tensor_tensor(x, x, by_batch(h32[:, o % 2, :]), ALU.add).then_inc(s_oadd, 1)
                if not last:
                    dve.wait_ge(s_xh, XP + g + 1)
                    dve.tensor_tensor(by_batch(xsp[1]), OUTV[:, :, batches(g + 1), :], by_batch(xsp[0]), ALU.subtract).then_inc(s_xl, 1)
                for t in range(TPG):
                    dve.wait_ge(s_sc, TPG * g + t + 1)
                    dve.tensor_tensor(SA.rearrange("p (a n) -> p a n", a=2), PS[:, 1 + 3 * (t % 2), :].rearrange("p (a n) -> p a n", a=2),
                                      lrel.unsqueeze(1).broadcast_to([P, 2, NS]), ALU.add).then_inc(s_scr, 1)
                    dve.wait_ge(s_scr, START + TPG * g + t + 1)
                    step(dve.max(v8, SA[:, 0:NS]))
                    dve.wait_ge(s_e, START + TPG * g + t)
                    step(dve.match_replace(tm, v8, SA[:, 0:NS], -3.0e38))
                    step(dve.tensor_tensor(tm, tm, SA[:, 0:NS], ALU.is_equal))
                    step(dve.scalar_tensor_tensor(out=tm, in0=tm, scalar=-BIG, in1=SA[:, NS:2 * NS], op0=ALU.mult, op1=ALU.add))
                    dve.tensor_reduce(nm[:, t % 2:t % 2 + 1], tm, AX_X, ALU.max, negate=True).then_inc(s_t, 1)
                token_sums(g)
                if last:
                    variances()
                    dve.wait_ge(s_lv, 1)
                    dve.tensor_reduce(gate[:, 3, 0:1], gate[:, 2, :], AX_X, ALU.add).then_inc(s_lvs, 1)
                if not last:
                    split_taps(g)

            for g in range(NG):
                group(g, last=(g == NG - 1))

            dve.wait_ge(s_gsum, 1)
            dve.wait_ge(s_lv, 2)
            step(dve.tensor_scalar(gate[:, 3, 1:2], PS[:, 3, 0:1], 1.0 / TOK, 1e-6, ALU.mult, ALU.add))
            step(dve.reciprocal(gate[:, 3, 2:3], gate[:, 3, 1:2]))
            step(dve.tensor_scalar(gate[:, 5, :], gate[:, 2, :], gate[:, 3, 2:3], 0.5, ALU.mult, ALU.mult))
            step(dve.scalar_tensor_tensor(out=gate[:, 5, :], in0=gate[:, 4, :], scalar=2.5, in1=gate[:, 5, :], op0=ALU.mult, op1=ALU.add))
            step(dve.tensor_scalar(gate[:, 5, :], gate[:, 5, :], 0.0, 5.0, ALU.max, ALU.min))
            step(dve.tensor_scalar(gate[:, 6, :], gate[:, 5, :], -0.5, 1.0 / 1.5, ALU.add, ALU.mult))
            dve.tensor_scalar(gate[:, 6, :], gate[:, 6, :], 0.0, 1.0, ALU.max, ALU.min).then_inc(s_un, 1)
            dve.wait_ge(s_sg, 1)
            step(dve.tensor_scalar(gate[:, 8, :], gate[:, 7, :], 0.05, None, ALU.is_ge))
            step(dve.tensor_tensor(gate[:, 8, :], gate[:, 8, :], gate[:, 7, :], ALU.mult))
            dve.wait_ge(s_e, START + NG * TPG)
            step(dve.reciprocal(gate[:, 9, :], seall))
            step(dve.tensor_tensor(gate[:, 10, :], gate[:, 8, :], gate[:, 9, :], ALU.mult))
            for g in range(NG):
                dve.tensor_tensor(diag[g], ident.unsqueeze(1).broadcast_to([P, TPG, P]),
                                  gate[:, 10, TPG * g:TPG * g + TPG].unsqueeze(2).broadcast_to([P, TPG, P]), ALU.mult)\
                   .then_inc(s_dg, 1)
            dve.wait_ge(s_wh, 1)
            dve.scalar_tensor_tensor(out=wvu[1][0:BOT, :], in0=wvu32[0:BOT, :], scalar=S_W, in1=wvu[0][0:BOT, :], op0=ALU.mult,
                                     op1=ALU.subtract).then_inc(s_wl, 1)
            def gated_memory(g):
                dve.wait_ge(s_gb, g + 1)
                dve.wait_ge(s_zc, g + 1)
                z = z_all[:, g * GT:g * GT + GT]
                dve.tensor_tensor(z, z, PS[:, g, :], ALU.mult).then_inc(s_zg, 1)

            def low_memory(g):
                z = z_all[:, g * GT:g * GT + GT]
                dve.wait_ge(s_zh, g + 1)
                dve.wait_ge(s_zg, g + 1)
                dve.tensor_tensor(zsp[BOT:2 * BOT, g, :], z[BOT:2 * BOT, :], zsp[BOT:2 * BOT, g, :], ALU.subtract).then_inc(s_zl, 1)

            gated_memory(0)
            low_memory(0)
            for g in range(NG):
                for o in range(KT):
                    dve.wait_ge(s_aux, KT * g + o + 1)
                    x = OUTV[:, o, batches(g), :]
                    dve.scalar_tensor_tensor(out=x, in0=by_batch(PS[:, X1_BANK[(KT * g + o) % 3], :]), scalar=1.0 / S_W, in1=x,
                                             op0=ALU.mult, op1=ALU.add).then_inc(s_x1, 1)
                    if g + 1 < NG and o == 1:
                        gated_memory(g + 1)
                    if g + 1 < NG and o == 4:
                        low_memory(g + 1)
                    if g == 0 and o == 5:
                        split_taps(NG - 1)
                    if o in DVE_LO:
                        continue
                    if o - 1 in DVE_LO:
                        k = o - 1
                        dve.wait_ge(s_uh, KT * g + k + 1)
                        hi, lo = [by_batch(x[:, k, tok(g)]) for x in fsp]
                        dve.tensor_tensor(lo, OUTV[:, k, batches(g), :], hi, ALU.subtract)\
                           .then_inc(s_ul, 1)

            dve.wait_ge(s_lenl, 32)
            dve.wait_ge(s_aux, KT * NG)
            for k in range(KT):
                for c in range(2):
                    ins = dve.tensor_scalar(ymask[:, k, c * B:c * B + B], len_s, posF[:, k:k + 1], 1.0 / S_W, ALU.is_gt, ALU.mult)
            ins.then_inc(s_ym, 1)
            dve.wait_ge(s_ym, 1)

            def piece(n, lo, src, hi, scale):
                dve.wait_ge(s_fhi, n + 1)
                dve.scalar_tensor_tensor(out=lo, in0=src, scalar=scale, in1=hi, op0=ALU.mult, op1=ALU.subtract).then_inc(s_flo, 1)

            for n in range(N_C1):
                c = [x[:, 4 * n:4 * n + 4, :] for x in c1s]
                piece(n, c[1], fst[n][:, 0:4 * C1R].rearrange("p (k c) -> p k c", k=4), c[0], S_W)

            def w1_piece(q, par):
                c = [w1_flat(part)[:, bass.ds((2 * q + par) * 512, 512)] for part in range(2)]
                piece(N_C1 + 2 * q + par, c[1], fst[par], c[0], S_W)

            def c2_piece(q, par):
                c = c2s[RB:RB + RANK, bass.ds((2 * (q - 4) + par) * CPC, CPC)]
                piece(N_W1 + 2 * (q - 4) + par, c, fst[par][RB:RB + RANK, 0:CPC], c, S_R)

            def convolved(q, pieces_of):
                def mask(pair):
                    dve.wait_ge(s_cv, 8 * q + 2 * pair + 2)
                    dve.wait_ge(s_yh, START + 4 * q + pair - 1)
                    dve.wait_ge(s_yl, START + 4 * q + pair - 1)
                    dve.tensor_tensor(y32[:, pair % 2, :], PS[:, pair, :], ymask.rearrange("p k c -> p (k c)"), ALU.mult)\
                       .then_inc(s_y, 1)

                def low(pair):
                    dve.wait_ge(s_yh, START + 4 * q + pair + 1)
                    c = [head_of(x, q * 8 + pair * 2, 2) for x in fsp]
                    dve.tensor_tensor(c[1], y32[:, pair % 2, :].rearrange("p (k c b) -> p k c b", k=KT, c=2), c[0], ALU.subtract)\
                       .then_inc(s_yl, 1)
                    if pair % 2:
                        pieces_of(q, pair // 2)

                mask(0)
                mask(1)
                low(0)
                mask(2)
                low(1)
                mask(3)
                low(2)
                low(3)

            with dve.Fori(0, 4) as q:
                convolved(q, w1_piece)
            with dve.Fori(4, 8) as q:
                convolved(q, c2_piece)

            def first_w2(j):
                tile, half = w2_first[j]
                hi, lo = [ring_slot(part, 2, tile * L + half * 512) for part in range(2)]
                piece(N_C2 + j, lo, fst[j % 2], hi, S_W)

            def low_rank(g):
                dve.wait_ge(s_a1h, g + 1)
                c = a1s[2 * RB:2 * RB + RANK, g * GT:g * GT + GT]
                dve.scalar_tensor_tensor(out=c, in0=PS[2 * RB:2 * RB + RANK, 6 + g % 2, :], scalar=1.0 / S_W, in1=c,
                                         op0=ALU.mult, op1=ALU.subtract).then_inc(s_a1l, 1)

            def mask(n, t):
                sc = PS[:, t, :].rearrange("p (k i) -> p k i", i=BLK)
                dve.wait_ge(s_in, STEP * n + t + 1)
                if not first(n) or t:
                    dve.wait_ge(s_mk, STEP * n + t)
                dve.tensor_reduce(bm, sc, AX_X, ALU.max).then_inc(s_bm, 1)
                dve.wait_ge(s_bm, STEP * n + t + 1)
                if not first(n):
                    dve.wait_ge(s_m, STEP * n + t - 1)
                dve.tensor_tensor(mk[:, t, :].rearrange("p (k i) -> p k i", i=BLK), sc,
                                  bm.unsqueeze(2).broadcast_to([P, CI * P // BLK, BLK]), ALU.is_equal).then_inc(s_mk, 1)

            def masked(n, t):
                dve.wait_ge(s_mk, STEP * n + t + 1)
                dve.wait_ge(s_g1, STEP * n + t + 1)
                if not first(n) or t:
                    dve.wait_ge(s_ml, STEP * n + t)
                dve.scalar_tensor_tensor(out=m32, in0=PS[:, 2 + t, :], scalar=0.0, in1=mk[:, t, :], op0=ALU.max,
                                         op1=ALU.mult).then_inc(s_m, 1)

            def low(n, t):
                dve.wait_ge(s_mh, STEP * n + t + 1)
                dve.scalar_tensor_tensor(out=mtok[t][:, 1, :], in0=m32, scalar=1.0 / S_W, in1=mtok[t][:, 0, :], op0=ALU.mult,
                                         op1=ALU.subtract).then_inc(s_ml, 1)

            first_w2(0)
            first_w2(1)
            low_rank(0)
            first_w2(2)
            low_rank(1)
            first_w2(3)
            mask(0, 0)
            mask(0, 1)
            masked(0, 0)
            low(0, 0)
            masked(0, 1)
            low(0, 1)
            low_rank(2)
            first_w2(4)
            low_rank(3)
            first_w2(5)

            def chunk(s, phase, last=False):
                what = chunk_pieces(s, phase, last)

                def pieces_of(js):
                    for j in js:
                        if j < len(what):
                            ring, _, at = what[j]
                            hi, lo = [ring_slot(part, ring, at) for part in range(2)]
                            piece(N_W2 + PPC * s + j, lo, fst[j % 2], hi, S_W)

                for j in range(SPC):
                    n = SPC * s + j
                    start, behind_high, behind_first, behind_second = AT_STEP[j]
                    more = not (last and j == SPC - 1)

                    def add(a):
                        dve.wait_ge(s_o, START + OP * n + a + 1)
                        c = OUT[:, j * STEP * BPT:(j + 1) * STEP * BPT, 2 * a:2 * a + 2, :].rearrange("p b k h -> p b (k h)")
                        dve.scalar_tensor_tensor(out=c, in0=PS[:, 6 + a % 2, :].rearrange("p (b c) -> p b c", c=2 * H),
                                                 scalar=1.0 / S_W, in1=c, op0=ALU.mult, op1=ALU.add).then_inc(s_oa, 1)

                    if more:
                        mask(n + 1, 0)
                    pieces_of(start)
                    if more:
                        mask(n + 1, 1)
                        masked(n + 1, 0)
                    add(0)
                    if more:
                        low(n + 1, 0)
                        masked(n + 1, 1)
                        low(n + 1, 1)
                    add(1)
                    pieces_of(behind_high)
                    pieces_of(behind_first)
                    add(2)
                    pieces_of(behind_second)
                    add(3)

            with dve.Fori(0, NC - BODY, BODY) as s:
                for j in range(BODY):
                    chunk(s + j, j)
            chunk(NC - 1, (NC - 1) % BODY, last=True)

        @block.gpsimd
        def _(pool):
            done = [0]

            def step(ins):
                ins.then_inc(s_pool, 1)
                done[0] += 1
                pool.wait_ge(s_pool, done[0])

            def tt(out_, a_, b_, op):
                step(pool.tensor_tensor(out_, a_, b_, op))

            def ts(out_, a_, x, y, o0, o1):
                step(pool.tensor_scalar(out_, a_, x, y, o0, o1))

            def fraction(out_, a_, tmp):
                ts(tmp, a_, MAGIC, -MAGIC, ALU.add, ALU.add)
                tt(out_, a_, tmp, ALU.subtract)

            for one in from_start:
                pool.sem_inc(one, START)

            pool.wait_ge(s_small, 16 * NSM)
            k2, r2, p2, e2 = (small[:, 6 + 2 * i:8 + 2 * i, :] for i in range(4))
            ts(logs, logs, -87.0, 88.0, ALU.max, ALU.min)
            ts(k2, logs, float(np.log2(np.e)), MAGIC, ALU.mult, ALU.add)
            ts(k2, k2, -MAGIC, 0.0, ALU.add, ALU.add)
            ts(r2, k2, -LN2_HI, 0.0, ALU.mult, ALU.add)
            tt(r2, logs, r2, ALU.add)
            ts(p2, k2, -LN2_LO, 0.0, ALU.mult, ALU.add)
            tt(r2, r2, p2, ALU.add)
            ts(p2, r2, 1.0 / 8, 1.0, ALU.mult, ALU.add)
            for i in range(7, 0, -1):
                tt(p2, p2, r2, ALU.mult)
                ts(p2, p2, 1.0 / i, 1.0, ALU.mult, ALU.add)
            ts(e2.bitcast(I32), k2, 127.0, float(2 ** 23), ALU.add, ALU.mult)
            tt(exps, p2, e2, ALU.mult)
            are, den, sn, sh, em = are_s, t_[0], t_[1], t_[2], t_[3]
            tt(R_s, are, dt_s, ALU.mult)
            ts(R_s, R_s, -1.0, 0.0, ALU.mult, ALU.add)
            tt(th_s, aim_s, dt_s, ALU.mult)
            ts(th_s, th_s, 1.0 / (2.0 * np.pi), 0.0, ALU.mult, ALU.add)
            tt(t_[4], are, are, ALU.mult)
            tt(t_[5], aim_s, aim_s, ALU.mult)
            tt(den, t_[4], t_[5], ALU.add)
            assert done[0] == POOL_DEN
            fraction(sn, th_s, t_[4])
            ts(sh, sn, 1.0, 0.0, ALU.mult, ALU.add)
            assert done[0] == POOL_HALF
            ts(em, R_s, 1.0 / 9, 1.0, ALU.mult, ALU.add)
            for i in range(8, 1, -1):
                tt(em, em, R_s, ALU.mult)
                ts(em, em, 1.0 / i, 1.0, ALU.mult, ALU.add)
            tt(em, em, R_s, ALU.mult)
            pool.wait_ge(s_rexp, 2)
            c1m, er, ei, u, v = t_[4], t_[5], t_[6], t_[7], t_[8]
            tt(c1m, sh, sh, ALU.mult)
            ts(c1m, c1m, -2.0, 0.0, ALU.mult, ALU.add)
            tt(er, em, c1m, ALU.mult)
            tt(er, er, em, ALU.add)
            tt(er, er, c1m, ALU.add)
            tt(ei, em, sn, ALU.mult)
            tt(ei, ei, sn, ALU.add)
            tt(u, cr_s, er, ALU.mult)
            tt(v, ci_s, ei, ALU.mult)
            tt(u, u, v, ALU.subtract)
            tt(v, cr_s, ei, ALU.mult)
            tt(s1_s, ci_s, er, ALU.mult)
            tt(v, v, s1_s, ALU.add)
            pool.wait_ge(s_dsm, 1)
            tt(s1_s, v, aim_s, ALU.mult)
            tt(s2_s, u, are, ALU.mult)
            tt(s1_s, s1_s, s2_s, ALU.subtract)
            tt(s1_s, s1_s, den, ALU.mult)
            tt(s2_s, u, aim_s, ALU.mult)
            tt(v, v, are, ALU.mult)
            tt(s2_s, s2_s, v, ALU.add)
            tt(s2_s, s2_s, den, ALU.mult)
            ts(s1_s, s1_s, cst[:, C_SGN:C_SGN + 1], 0.0, ALU.mult, ALU.add)

            def group(g):
                hs = bass.ds(g * HPG, HPG)

                def head(x):
                    return x[:, hs].unsqueeze(2).broadcast_to([P, HPG, TB])

                def ramp(at):
                    return cst[:, at:at + TB].unsqueeze(1).broadcast_to([P, HPG, TB])

                E2, EA, EB = ph
                tt(E2, head(th_s), ramp(C_TB), ALU.mult)
                ts(E2, E2, cst[:, C_PHA:C_PHA + 1], 0.0, ALU.add, ALU.add)
                fraction(E2, E2, mg[0])
                tt(EA, head(th_s), ramp(C_TA), ALU.mult)
                ts(EB, EA, cst[:, C_PHB:C_PHB + 1], 0.0, ALU.add, ALU.add)
                ts(EA, EA, cst[:, C_PHA:C_PHA + 1], 0.0, ALU.add, ALU.add)
                fraction(EB, EB, mg[0])
                fraction(EA, EA, mg[0])
                tt(mg[1], head(R_s), ramp(C_TA), ALU.mult)
                pool.tensor_tensor(mg[0], head(R_s), ramp(C_TB), ALU.mult).then_inc(s_ph, 1)
                for o in range(KT):
                    pool.wait_ge(s_hev, START + KT * g + o + 1)
                    pool.wait_ge(s_sq, START + 2 * (KT * g + o))
                    if o == 0:
                        pool.wait_ge(s_st, g)
                        pool.tensor_tensor(acc, h32[:, 0, :], h32[:, 0, :], ALU.mult).then_inc(s_sq, 2)
                        continue
                    pool.tensor_tensor(sq, h32[:, o % 2, :], h32[:, o % 2, :], ALU.mult).then_inc(s_sq, 1)
                    pool.wait_ge(s_sq, START + 2 * (KT * g + o) + 1)
                    pool.tensor_tensor(acc, acc, sq, ALU.add).then_inc(s_sq, 1)
                pool.wait_ge(s_phd, 5 * g + 5)
                tt(E2, E2, mg[0], ALU.mult)
                tt(EA, EA, mg[1], ALU.mult)
                tt(EB, EB, mg[1], ALU.mult)
                tt(EA, EA, head(s1_s), ALU.mult)
                tt(EB, EB, head(s2_s), ALU.mult)
                pool.tensor_tensor(EA, EA, EB, ALU.add).then_inc(s_L, 1)
                pool.wait_ge(s_k, g + 1)

            for g in range(NG):
                group(g)

            for g in range(NG):
                for o in (x for x in range(KT) if x not in DVE_LO):
                    pool.wait_ge(s_uh, KT * g + o + 1)
                    hi, lo = [by_batch(x[:, o, tok(g)]) for x in fsp]
                    pool.tensor_tensor(lo, OUTV[:, o, batches(g), :], hi, ALU.subtract)\
                        .then_inc(s_ulp, 1)


def kernel(**inputs):
    import concourse.bacc as _bacc
    from concourse.bass_utils import run_bass_kernel_spmd as _run

    v = {k: np.asarray(a) for k, a in inputs.items()}

    def turned(w):
        return w.reshape(-1, KT, P)[:, :, ::-1].reshape(-1, L)

    bands = np.zeros((L, C1R), np.float32)
    bands2 = np.zeros((C1R, INTER), np.float32)
    for i in range(3):
        bands[:, RB * i:RB * i + RANK] = turned(v["L1_ffn_c1_w"]).T
        bands2[RB * i:RB * i + RANK] = v["L1_ffn_c2_w"].T
    Cm = v["L1_cond_C"]

    def rows(x):
        return np.broadcast_to(np.asarray(x).reshape(1, -1), (P, np.asarray(x).size))

    modes = [v["L1_cond_log_A_real"].T, v["L1_cond_A_imag"].T, Cm[:, :, 0].T, Cm[:, :, 1].T]
    packed = np.concatenate(
        [shape_constants(), rows(v["L0_ffn_log_rel"]), rows(v["L0_ffn_bu2"]), rows(v["L0_ffn_gate_w1"]),
         rows(v["L0_ffn_gate_bias"]), v["L0_ffn_bu1"].reshape(2, P).T, v["L0_ffn_Wu2"].reshape(2, P).T,
         rows(v["L1_cond_log_dt"])] + [np.concatenate([m, m], axis=0) for m in modes], axis=1)
    assert packed.shape == (P, K_N)
    arrays = {
        "xB": v["x"].transpose(0, 2, 1).reshape(B, KT, P, H).transpose(0, 2, 1, 3).reshape(B * P, KT * H),
        "WT": v["L0_cond_W"].T,
        "WrT": v["L0_cond_Wr"].T,
        "AT": v["L0_cond_A"].reshape(NE * RK, L).T,
        "BT": v["L0_cond_B"].transpose(0, 2, 1).reshape(NE * RK, L),
        "WqT": v["L0_ffn_Wq"].T,
        "Wr": v["L0_ffn_Wr"],
        "Wr2T": v["L0_ffn_Wr"].T,
        "keysT": v["L0_ffn_aux_keys"].T,
        "valuesT": v["L0_ffn_aux_values"].T,
        "WvdT": v["L0_ffn_Wvd"].T,
        "WvuT": v["L0_ffn_Wvu"].T,
        "Wu1T": v["L0_ffn_Wu1"].T,
        "packed": packed,
        "Dh": v["L1_cond_D"].reshape(1, H),
        "c1P": bands,
        "c2T": bands2,
        "w1L": turned(v["L1_ffn_w1"]).reshape(IT // 2, PAIR, KT, P).transpose(0, 3, 2, 1).reshape(IT // 2, P, KT * PAIR),
        "w2": v["L1_ffn_w2t"],
        "ids": v["itok_B_0_7"],
        "lens": v["itok_B_78_3631"],
    }
    nc = _bacc.Bacc("TRN2", target_bir_lowering=False, num_devices=1)
    given, args = {}, []
    for name, a in arrays.items():
        a = np.ascontiguousarray(a)
        given[f"in_{name}"] = a
        args.append(nc.dram_tensor(f"in_{name}", a.shape, mybir.dt.from_np(a.dtype), kind="ExternalInput").ap())
    args.append(nc.dram_tensor("out_0", (B * P, KT * H), F32, kind="ExternalOutput").ap())
    build(nc, *args)
    r = _run(nc, [given], core_ids=[0])
    return np.ascontiguousarray(r.results[0]["out_0"].reshape(B, P, KT, H).transpose(0, 3, 2, 1).reshape(B, H, L))
```
